# Optimizing a Trainium2 kernel written in Bass

```python
import numpy as np
import jax
import jax.numpy as jnp

def _softmax(x, axis=-1):
    return jax.nn.softmax(x, axis=axis)

def _gelu(x):
    return jax.nn.gelu(x, approximate=True)

def _silu(x):
    return jax.nn.silu(x)

def _sigmoid(x):
    return jax.nn.sigmoid(x)

def _layernorm(x, axis=-1, eps=1e-05):
    m = jnp.mean(x, axis=axis, keepdims=True)
    v = jnp.var(x, axis=axis, keepdims=True)
    return (x - m) / jnp.sqrt(v + eps)

def _scatter_add(tgt, idx, src, axis=0):
    return tgt.at[idx].add(src)

def _segment_sum(src, seg, n):
    return jax.ops.segment_sum(src, seg, n)
kernel_name = 'mk_gnn_preln_d4_gnn_r8_08e29d'

def setup_inputs(seed: int=0):
    np.random.seed(seed)
    _w = jnp.asarray

    def _rec_inputs():
        import jax
        import jax.numpy as jnp
        _gk = jax.random.key(seed)
        x = -0.0009044 + 1 * jax.random.normal(jax.random.fold_in(_gk, 1), (12500, 16), jnp.float32)
        _s = jax.random.randint(jax.random.fold_in(_gk, 2), (200000,), 0, 12500, jnp.int32)
        _d = jax.random.randint(jax.random.fold_in(_gk, 3), (200000,), 0, 12500, jnp.int32)
        _loop = jnp.arange(12500, dtype=jnp.int32)
        src = jnp.concatenate([_s, _d, _loop])
        dst = jnp.concatenate([_d, _s, _loop])
        _o = jnp.argsort(dst, stable=True)
        src = src[_o]
        dst = dst[_o]
        edge_attr_16 = -0.00010739 + 0.99994 * jax.random.normal(jax.random.fold_in(_gk, 12), (412500, 16), jnp.float32)
        edge_type_8 = jax.random.randint(jax.random.fold_in(_gk, 14), (412500,), 0, 8, jnp.int32)
        edge_type_90 = jax.random.randint(jax.random.fold_in(_gk, 15), (412500,), 0, 90, jnp.int32)
        return (x, src, dst, edge_attr_16, edge_type_8, edge_type_90)
    x, src, dst, edge_attr_16, edge_type_8, edge_type_90 = _rec_inputs()

    def _L0_gnn_setup():
        import jax, jax.numpy as jnp
        import numpy as np
        N = 12500
        E = 100000
        F_IN = 16
        H1, C1 = (3, 32)
        H2, C2 = (1, 32)
        NC = 16
        SLOPE = 0.2

        def _gat_layer(x, src, dst, W, a_s, a_d, b, heads, outc):
            h = (x @ W).reshape(N, heads, outc)
            alpha_s = (h * a_s).sum(-1)
            alpha_d = (h * a_d).sum(-1)
            e = jax.nn.leaky_relu(alpha_s[src] + alpha_d[dst], SLOPE)
            m = jax.ops.segment_max(e, dst, num_segments=N)
            p = jnp.exp(e - m[dst])
            z = jax.ops.segment_sum(p, dst, num_segments=N)
            alpha = p / (z[dst] + 1e-16)
            out = jax.ops.segment_sum(h[src] * alpha[:, :, None], dst, num_segments=N)
            return out.reshape(N, heads * outc) + b
        key = jax.random.key(seed)
        ks = jax.random.split(key, 12)
        s = 0.1
        return {'x': jax.random.normal(ks[0], (N, F_IN), jnp.float32), 'edge_index': jax.random.randint(ks[1], (2, E), 0, N, dtype=jnp.int32), 'W1': jax.random.normal(ks[2], (F_IN, H1 * C1), jnp.float32) * s, 'a_src1': jax.random.normal(ks[3], (H1, C1), jnp.float32) * s, 'a_dst1': jax.random.normal(ks[4], (H1, C1), jnp.float32) * s, 'b1': jnp.zeros((H1 * C1,), jnp.float32), 'W2': jax.random.normal(ks[5], (H1 * C1, H2 * C2), jnp.float32) * s, 'a_src2': jax.random.normal(ks[6], (H2, C2), jnp.float32) * s, 'a_dst2': jax.random.normal(ks[7], (H2, C2), jnp.float32) * s, 'b2': jnp.zeros((H2 * C2,), jnp.float32), 'Wf': jax.random.normal(ks[8], (C2, NC), jnp.float32) * s, 'bf': jnp.zeros((NC,), jnp.float32)}
    _L0_gnn_all = _L0_gnn_setup()
    _L0_gnn_in = {k: v for k, v in _L0_gnn_all.items() if k in ('W1', 'a_src1', 'a_dst1', 'b1', 'W2', 'a_src2', 'a_dst2', 'b2', 'Wf', 'bf')}
    del _L0_gnn_all

    def _L1_gnn_setup():
        import jax, jax.numpy as jnp
        import numpy as np
        NUM_ENTITIES = 12500
        NUM_RELATIONS = 8
        NUM_CLASSES = 16
        HIDDEN = 16
        NUM_EDGES = 400000

        def rgcn_conv(x, src, dst, edge_type, W, root, bias):
            num_nodes = x.shape[0]
            x_src = x[src]
            msg = jnp.zeros((src.shape[0], W.shape[2]), x.dtype)
            for r in range(NUM_RELATIONS):
                msg = msg + jnp.where((edge_type == r)[:, None], x_src @ W[r], jnp.zeros((), x.dtype))
            cnt = jnp.zeros((num_nodes, NUM_RELATIONS), x.dtype).at[dst, edge_type].add(1.0)
            norm = 1.0 / jnp.maximum(cnt[dst, edge_type], 1.0)
            agg = jax.ops.segment_sum(msg * norm[:, None], dst, num_segments=num_nodes)
            return agg + x @ root + bias
        key = jax.random.key(seed)
        ks = jax.random.split(key, 9)
        s = 1.0 / np.sqrt(HIDDEN)
        edge_index = jax.random.randint(ks[0], (2, NUM_EDGES), 0, NUM_ENTITIES, dtype=jnp.int32)
        edge_type = jax.random.randint(ks[1], (NUM_EDGES,), 0, NUM_RELATIONS, dtype=jnp.int32)
        return {'embed': jax.random.normal(ks[2], (NUM_ENTITIES, HIDDEN), jnp.float32), 'W1': jax.random.normal(ks[3], (NUM_RELATIONS, HIDDEN, HIDDEN), jnp.float32) * s, 'root1': jax.random.normal(ks[4], (HIDDEN, HIDDEN), jnp.float32) * s, 'b1': jnp.zeros((HIDDEN,), jnp.float32), 'W2': jax.random.normal(ks[5], (NUM_RELATIONS, HIDDEN, NUM_CLASSES), jnp.float32) * s, 'root2': jax.random.normal(ks[6], (HIDDEN, NUM_CLASSES), jnp.float32) * s, 'b2': jnp.zeros((NUM_CLASSES,), jnp.float32), 'edge_index': edge_index, 'edge_type': edge_type}
    _L1_gnn_all = _L1_gnn_setup()
    _L1_gnn_in = {k: v for k, v in _L1_gnn_all.items() if k in ('W1', 'root1', 'b1', 'W2', 'root2', 'b2')}
    del _L1_gnn_all

    def _L2_gnn_setup():
        import jax, jax.numpy as jnp
        import numpy as np
        STALK_DIM = 16
        N_NODES = 6250
        N_EDGES = 50000
        HIDDEN = 64
        key = jax.random.key(seed)
        k1, k2, k3, k4 = jax.random.split(key, 4)
        d = STALK_DIM
        x = jax.random.normal(k1, (N_NODES, d), dtype=jnp.float32)
        edge_index = jax.random.randint(k2, (2, N_EDGES), 0, N_NODES, dtype=jnp.int64)
        W1 = jax.random.normal(k3, (HIDDEN, 2 * d), dtype=jnp.float32) * (1.0 / np.sqrt(2 * d))
        b1 = jnp.zeros((HIDDEN,), dtype=jnp.float32)
        W2 = jax.random.normal(k4, (d, HIDDEN), dtype=jnp.float32) * (1.0 / np.sqrt(HIDDEN))
        b2 = jnp.zeros((d,), dtype=jnp.float32)
        return {'x': x, 'edge_index': edge_index, 'W1': W1, 'b1': b1, 'W2': W2, 'b2': b2}
    _L2_gnn_all = _L2_gnn_setup()
    _L2_gnn_in = {k: v for k, v in _L2_gnn_all.items() if k in ('W1', 'b1', 'W2', 'b2')}
    del _L2_gnn_all

    def _L3_gnn_setup():
        import jax, jax.numpy as jnp
        import numpy as np
        N, E, IN, OUT, R, B = (6250, 100000, 16, 16, 90, 30)
        key = jax.random.key(seed)
        ks = jax.random.split(key, 9)
        h = jax.random.normal(ks[0], (N, IN), dtype=jnp.float32)
        he = jax.random.normal(ks[1], (E, IN), dtype=jnp.float32)
        Ws = jax.random.normal(ks[2], (OUT, IN), dtype=jnp.float32) * 0.1
        Wa = jax.random.normal(ks[3], (1, 3 * OUT), dtype=jnp.float32) * 0.1
        weight = jax.random.normal(ks[4], (B, IN, OUT), dtype=jnp.float32) * 0.1
        w_comp = jax.random.normal(ks[5], (R, B), dtype=jnp.float32) * 0.1
        src = jax.random.randint(ks[6], (E,), 0, N)
        dst = jax.random.randint(ks[7], (E,), 0, N)
        rel_type = jax.random.randint(ks[8], (E,), 0, R)
        return {'h': h, 'he': he, 'Ws': Ws, 'Wa': Wa, 'weight': weight, 'w_comp': w_comp, 'src': src, 'dst': dst, 'rel_type': rel_type}
    _L3_gnn_all = _L3_gnn_setup()
    _L3_gnn_in = {k: v for k, v in _L3_gnn_all.items() if k in ('Ws', 'Wa', 'weight', 'w_comp')}
    del _L3_gnn_all
    return {'x': x, 'src': src, 'dst': dst, 'edge_attr_16': edge_attr_16, 'edge_type_8': edge_type_8, 'edge_type_90': edge_type_90, 'L0_gnn_W1': _L0_gnn_in['W1'], 'L0_gnn_a_src1': _L0_gnn_in['a_src1'], 'L0_gnn_a_dst1': _L0_gnn_in['a_dst1'], 'L0_gnn_b1': _L0_gnn_in['b1'], 'L0_gnn_W2': _L0_gnn_in['W2'], 'L0_gnn_a_src2': _L0_gnn_in['a_src2'], 'L0_gnn_a_dst2': _L0_gnn_in['a_dst2'], 'L0_gnn_b2': _L0_gnn_in['b2'], 'L0_gnn_Wf': _L0_gnn_in['Wf'], 'L0_gnn_bf': _L0_gnn_in['bf'], 'L1_gnn_W1': _L1_gnn_in['W1'], 'L1_gnn_root1': _L1_gnn_in['root1'], 'L1_gnn_b1': _L1_gnn_in['b1'], 'L1_gnn_W2': _L1_gnn_in['W2'], 'L1_gnn_root2': _L1_gnn_in['root2'], 'L1_gnn_b2': _L1_gnn_in['b2'], 'L2_gnn_W1': _L2_gnn_in['W1'], 'L2_gnn_b1': _L2_gnn_in['b1'], 'L2_gnn_W2': _L2_gnn_in['W2'], 'L2_gnn_b2': _L2_gnn_in['b2'], 'L3_gnn_Ws': _L3_gnn_in['Ws'], 'L3_gnn_Wa': _L3_gnn_in['Wa'], 'L3_gnn_weight': _L3_gnn_in['weight'], 'L3_gnn_w_comp': _L3_gnn_in['w_comp']}

def reference(x, src, dst, edge_attr_16, edge_type_8, edge_type_90, L0_gnn_W1, L0_gnn_a_src1, L0_gnn_a_dst1, L0_gnn_b1, L0_gnn_W2, L0_gnn_a_src2, L0_gnn_a_dst2, L0_gnn_b2, L0_gnn_Wf, L0_gnn_bf, L1_gnn_W1, L1_gnn_root1, L1_gnn_b1, L1_gnn_W2, L1_gnn_root2, L1_gnn_b2, L2_gnn_W1, L2_gnn_b1, L2_gnn_W2, L2_gnn_b2, L3_gnn_Ws, L3_gnn_Wa, L3_gnn_weight, L3_gnn_w_comp):
    import jax
    import jax.numpy as jnp

    def _L0_gnn_ref(x, edge_index, W1, a_src1, a_dst1, b1, W2, a_src2, a_dst2, b2, Wf, bf):
        import jax, jax.numpy as jnp
        import numpy as np
        N = 12500
        E = 100000
        F_IN = 16
        H1, C1 = (3, 32)
        H2, C2 = (1, 32)
        NC = 16
        SLOPE = 0.2

        def _gat_layer(x, src, dst, W, a_s, a_d, b, heads, outc):
            h = (x @ W).reshape(N, heads, outc)
            alpha_s = (h * a_s).sum(-1)
            alpha_d = (h * a_d).sum(-1)
            e = jax.nn.leaky_relu(alpha_s[src] + alpha_d[dst], SLOPE)
            m = jax.ops.segment_max(e, dst, num_segments=N)
            p = jnp.exp(e - m[dst])
            z = jax.ops.segment_sum(p, dst, num_segments=N)
            alpha = p / (z[dst] + 1e-16)
            out = jax.ops.segment_sum(h[src] * alpha[:, :, None], dst, num_segments=N)
            return out.reshape(N, heads * outc) + b
        loops = jnp.arange(N, dtype=edge_index.dtype)
        src = jnp.concatenate([edge_index[0], loops])
        dst = jnp.concatenate([edge_index[1], loops])
        h = jax.nn.selu(_gat_layer(x, src, dst, W1, a_src1, a_dst1, b1, H1, C1))
        h = jax.nn.selu(_gat_layer(h, src, dst, W2, a_src2, a_dst2, b2, H2, C2))
        return h @ Wf + bf

    def _L1_gnn_ref(embed, W1, root1, b1, W2, root2, b2, edge_index, edge_type):
        import jax, jax.numpy as jnp
        import numpy as np
        NUM_ENTITIES = 12500
        NUM_RELATIONS = 8
        NUM_CLASSES = 16
        HIDDEN = 16
        NUM_EDGES = 400000

        def rgcn_conv(x, src, dst, edge_type, W, root, bias):
            num_nodes = x.shape[0]
            x_src = x[src]
            msg = jnp.zeros((src.shape[0], W.shape[2]), x.dtype)
            for r in range(NUM_RELATIONS):
                msg = msg + jnp.where((edge_type == r)[:, None], x_src @ W[r], jnp.zeros((), x.dtype))
            cnt = jnp.zeros((num_nodes, NUM_RELATIONS), x.dtype).at[dst, edge_type].add(1.0)
            norm = 1.0 / jnp.maximum(cnt[dst, edge_type], 1.0)
            agg = jax.ops.segment_sum(msg * norm[:, None], dst, num_segments=num_nodes)
            return agg + x @ root + bias
        src, dst = (edge_index[0], edge_index[1])
        h = rgcn_conv(embed, src, dst, edge_type, W1, root1, b1)
        h = jax.nn.relu(h)
        h = rgcn_conv(h, src, dst, edge_type, W2, root2, b2)
        return jax.nn.log_softmax(h, axis=1)

    def _L2_gnn_ref(x, edge_index, W1, b1, W2, b2):
        import jax, jax.numpy as jnp
        import numpy as np
        STALK_DIM = 16
        N_NODES = 6250
        N_EDGES = 50000
        HIDDEN = 64
        d = x.shape[1]
        n = x.shape[0]
        src, dst = (edge_index[0], edge_index[1])
        xs, xd = (x[src], x[dst])

        def reflection(a, b):
            h = jax.nn.relu(jnp.concatenate([a, b], axis=1) @ W1.T + b1)
            return h @ W2.T + b2

        def householder(v):
            vn = v / jnp.maximum(jnp.linalg.norm(v, axis=1, keepdims=True), 1e-12)
            return jnp.eye(d, dtype=v.dtype)[None] - 2.0 * vn[:, :, None] * vn[:, None, :]
        F_s = householder(reflection(xs, xd))
        F_d = householder(reflection(xd, xs))
        L_sd = -jnp.einsum('eki,ekj->eij', F_s, F_d)
        ones_e = jnp.ones(src.shape[0], dtype=x.dtype)
        deg = jnp.zeros(n, dtype=x.dtype).at[src].add(ones_e).at[dst].add(ones_e)
        deg_inv_sqrt = 1.0 / jnp.sqrt(jnp.maximum(deg, 1e-05))
        coef = deg_inv_sqrt[src] * deg_inv_sqrt[dst]
        msg_s = coef[:, None] * jnp.einsum('eij,ej->ei', L_sd, xd)
        msg_d = coef[:, None] * jnp.einsum('eji,ej->ei', L_sd, xs)
        out = x - jnp.zeros_like(x).at[src].add(msg_s) - jnp.zeros_like(x).at[dst].add(msg_d)
        return jax.nn.relu(out)

    def _L3_gnn_ref(h, he, Ws, Wa, weight, w_comp, src, dst, rel_type):
        import jax, jax.numpy as jnp
        import numpy as np
        N, E, IN, OUT, R, B = (6250, 100000, 16, 16, 90, 30)
        n_nodes, in_dim = h.shape
        num_bases, _, out_dim = weight.shape
        num_rels = w_comp.shape[0]
        V = weight.reshape(in_dim, num_bases, out_dim)
        W_rel = jnp.matmul(w_comp, V).reshape(num_rels, in_dim, out_dim)
        h_src = h[src]
        z_src = h_src @ Ws.T
        z_dst = h[dst] @ Ws.T
        z_e = he @ Ws.T
        e = jnp.concatenate([z_src, z_e, z_dst], axis=1) @ Wa.T
        msg = jnp.einsum('ei,eio->eo', h_src, W_rel[rel_type]) * e
        h_out = jax.ops.segment_sum(msg, dst, num_segments=n_nodes)
        return h_out
    edge_index = jnp.stack([src, dst])
    h = jnp.maximum(_layernorm(x, axis=-1), 0.0)
    x = x + _L0_gnn_ref(h, edge_index, L0_gnn_W1, L0_gnn_a_src1, L0_gnn_a_dst1, L0_gnn_b1, L0_gnn_W2, L0_gnn_a_src2, L0_gnn_a_dst2, L0_gnn_b2, L0_gnn_Wf, L0_gnn_bf)
    h = jnp.maximum(_layernorm(x, axis=-1), 0.0)
    x = x + _L1_gnn_ref(h, L1_gnn_W1, L1_gnn_root1, L1_gnn_b1, L1_gnn_W2, L1_gnn_root2, L1_gnn_b2, edge_index, edge_type_8)
    h = jnp.maximum(_layernorm(x, axis=-1), 0.0)
    x = x + _L2_gnn_ref(h, edge_index, L2_gnn_W1, L2_gnn_b1, L2_gnn_W2, L2_gnn_b2)
    h = jnp.maximum(_layernorm(x, axis=-1), 0.0)
    x = x + _L3_gnn_ref(h, edge_attr_16, L3_gnn_Ws, L3_gnn_Wa, L3_gnn_weight, L3_gnn_w_comp, src, dst, edge_type_90)
    return x

_drawn_inputs = setup_inputs


def setup_inputs(seed=0):
    import zlib

    import numpy as np

    out = dict(_drawn_inputs(seed))
    spreads = {'L0_gnn_b1': (0.0, 0.1),
     'L0_gnn_b2': (0.0, 0.1),
     'L0_gnn_bf': (0.0, 0.1),
     'L1_gnn_b1': (0.0, 0.1),
     'L1_gnn_b2': (0.0, 0.441),
     'L2_gnn_b1': (0.0, 2.0),
     'L2_gnn_b2': (0.0, 2.0)}
    factors = {'L0_gnn_a_src1': 26.55,
     'L0_gnn_a_dst1': 143.011,
     'L0_gnn_a_src2': 200.0,
     'L0_gnn_a_dst2': 200.0,
     'L2_gnn_W2': 36.708,
     'L2_gnn_W1': 4.292}
    for name, (base, spread) in spreads.items():
        noise = np.random.default_rng([zlib.crc32(name.encode()), seed]).standard_normal(out[name].shape)
        drawn = base * np.exp(spread * noise) if base else spread * noise
        out[name] = jnp.asarray(drawn.astype(out[name].dtype))
    for name, factor in factors.items():
        out[name] = (out[name] * factor).astype(out[name].dtype)
    return out
```

```python
from contextlib import ExitStack

import numpy as np

import concourse.bass as bass
from concourse import mybir

F32 = mybir.dt.float32
BF16 = mybir.dt.bfloat16
I32 = mybir.dt.int32
ALU = mybir.AluOpType
ACT = mybir.ActivationFunctionType
AX = mybir.AxisListType

P = 128
N, FD = 12500, 16
E = 412500
NT = -(-N // P)
NP = NT * P
J = 52
EP = 2 * J * -(-E // (P * 2 * J))
NCH = EP // J
EROWS = P * EP
XROWS = EROWS + NP
NSUM = 4
GT = 7
NG = NT // GT
R8, R90, NB = 8, 90, 30
BIG = 1.0e38
SLOPE = 0.2
SELU_SCALE, SELU_ALPHA = 1.0507009873554805, 1.6732632423543772
CSPLIT = 8
CROW = EP // CSPLIT


class Stage:

    def __init__(self, nc, name):
        self.nc, self.name, self.stack, self.sems = nc, name, ExitStack(), []

    def __enter__(self):
        return self

    def sb(self, name, shape, dt=F32):
        return self.stack.enter_context(self.nc.sbuf_tensor(f"{self.name}_{name}", shape, dt))

    def ps(self, name, shape):
        return self.stack.enter_context(self.nc.psum_tensor(f"{self.name}_{name}", shape, F32))

    def sem(self, name):
        s = self.nc.alloc_semaphore(f"{self.name}_{name}")
        self.sems.append(s)
        return s

    def __exit__(self, *a):
        self.stack.close()
        if a[0] is None:
            self.nc.clear_and_free_semaphores(self.sems)
            self.nc.all_engine_barrier()


class Order:

    def __init__(self, eng, sem, base=0):
        self.eng, self.sem, self.base, self.n = eng, sem, base, 0

    def step(self, ins):
        self.n += 1
        ins.then_inc(self.sem, 1)

    def link(self, ins):
        self.step(ins)
        self.eng.wait_ge(self.sem, self.base + self.n)


def by_edge(table):
    return table[0:EROWS].rearrange("(p j) w -> p j w", p=P)


def by_node(table):
    return table.rearrange("(t p) w -> p t w", p=P)


def chunk(view, i, k):
    return view[:, bass.ds((i * 2 + k) * J, J)]


def rows(ap):
    return bass.IndirectOffsetOnAxis(ap=ap, axis=0)



def set_up(nc, a, g):
    with Stage(nc, "setup") as s:
        src_i, dst_i, t8_i, t90_i = (s.sb(n, [P, EP], I32) for n in ("src", "dst", "t8", "t90"))
        idx8, idx90 = s.sb("idx8", [P, EP], I32), s.sb("idx90", [P, EP], I32)
        src_f, dst_f, t8_f, keep = (s.sb(n, [P, EP]) for n in ("srcf", "dstf", "t8f", "keep"))
        zero = s.sb("zero", [P, XROWS // P])
        iota_n, iota_j, iota_p = s.sb("ion", [P, NT], I32), s.sb("ioj", [P, P], I32), s.sb("iop", [P, 1], I32)
        loaded = [s.sem(f"loaded{n}") for n in range(5)]
        stored, iotas, zeroed, zero_ready, ready, dve_o, pool_o = (
            s.sem(n) for n in ("stored", "iotas", "zeroed", "zero_ready", "ready", "dve", "pool"))
        n_zero = len(g.to_zero)
        with nc.Block() as block:
            @block.sync
            def _(sp):
                for n, (dst, src) in enumerate(((dst_i, a.dst), (src_i, a.src), (t8_i, a.type8), (t90_i, a.type90))):
                    sp.dma_start(dst[:, :], src).then_inc(loaded[n], 16)
                sp.dma_start(g.x[:, :, :], by_node(a.x)).then_inc(loaded[4], 16)
                sp.wait_ge(zero_ready, 1)
                for table in g.to_zero:
                    n_rows, w = table.shape
                    flat = table.rearrange("(p m) w -> p (m w)", p=P)
                    m = n_rows // P
                    sp.dma_start(flat.rearrange("p (w m) -> p w m", w=w),
                                 zero[:, 0:m].unsqueeze(1).to_broadcast([P, w, m])).then_inc(zeroed, 16)
                sp.wait_ge(zeroed, 16 * n_zero)
                sp.wait_ge(loaded[4], 16)

            @block.gpsimd
            def _(pool):
                pool.iota(iota_n[:, :], pattern=[[P, NT]], base=0, channel_multiplier=1).then_inc(iotas, 1)
                pool.iota(iota_j[:, :], pattern=[[1, P]], base=0, channel_multiplier=0).then_inc(iotas, 1)
                pool.iota(iota_p[:, :], pattern=[[0, 1]], base=0, channel_multiplier=EP).then_inc(iotas, 1)
                pool.iota(g.first_row[:, :], pattern=[[0, 1]], base=0, channel_multiplier=EP).then_inc(iotas, 1)
                pool.iota(g.lane_i[:, :], pattern=[[0, 1]], base=0, channel_multiplier=1).then_inc(iotas, 1)
                pool.memset(g.ident[:, :], 0.0).then_inc(pool_o, 1)
                pool.wait_ge(pool_o, 1)
                pool.affine_select(out=g.ident[:, :], in_=g.ident[:, :], compare_op=ALU.not_equal, fill=1.0, base=0,
                                   pattern=[[-1, P]], channel_multiplier=1).then_inc(pool_o, 1)
                pool.memset(g.strict[:, :], 1.0).then_inc(pool_o, 1)
                pool.wait_ge(pool_o, 3)
                pool.affine_select(out=g.strict[:, :], in_=g.strict[:, :], compare_op=ALU.is_gt, fill=0.0, base=0,
                                   pattern=[[-1, P]], channel_multiplier=1).then_inc(pool_o, 1)

            @block.vector
            def _(dve):
                o = Order(dve, dve_o)
                dve.memset(zero[:, :], 0.0).then_inc(zero_ready, 1)
                dve.memset(keep[:, 0:1], 0.0)
                dve.wait_ge(iotas, 5)
                dve.tensor_copy(g.node_f[:, :], iota_n[:, :])
                dve.tensor_copy(g.count_f[:, :], iota_j[:, :])
                dve.tensor_copy(g.lane_f[:, :], g.lane_i[:, :])
                o.step(dve.tensor_copy(g.first_f[:, :], iota_p[:, :]))
                dve.wait_ge(loaded[0], 16)
                o.link(dve.tensor_copy(dst_f[:, :], dst_i[:, :]))
                dve.tensor_tensor(keep[:, 1:EP], dst_f[:, 1:EP], dst_f[:, 0:EP - 1], ALU.is_equal)
                dve.wait_ge(loaded[1], 16)
                o.step(dve.tensor_copy(src_f[:, :], src_i[:, :]))
                dve.tensor_scalar(g.src_lo[:, :], src_i[:, :], P - 1, None, ALU.bitwise_and)
                o.step(dve.tensor_scalar(g.src_hi[:, :], src_i[:, :], 7, None, ALU.logical_shift_right))
                dve.wait_ge(loaded[2], 16)
                dve.tensor_copy(t8_f[:, :], t8_i[:, :])
                dve.scalar_tensor_tensor(idx8[:, :], src_i[:, :], float(R8), t8_i[:, :], ALU.mult, ALU.add)
                dve.wait_ge(loaded[3], 16)
                dve.scalar_tensor_tensor(idx90[:, :], src_i[:, :], float(R90), t90_i[:, :], ALU.mult,
                                         ALU.add).then_inc(ready, 1)

            @block.scalar
            def _(act):
                act.wait_ge(ready, 1)
                pairs = ((g.keep_d, keep), (g.dst_d, dst_f), (g.src_fd, src_f), (g.type8_d, t8_f), (g.idx8_d, idx8),
                         (g.idx90_d, idx90))
                for dram, tile in pairs:
                    act.dma_start(dram, tile[:, :]).then_inc(stored, 16)
                act.wait_ge(stored, 16 * len(pairs))


def source_degrees(nc, g):
    with Stage(nc, "degrees") as s:
        lo_hot = [s.sb(f"lo{k}", [P, J, P], BF16) for k in range(2)]
        hi_hot = [s.sb(f"hi{k}", [P, J, NT], BF16) for k in range(2)]
        lo_f = [s.sb(f"lof{k}", [P, J]) for k in range(2)]
        hi_f = [s.sb(f"hif{k}", [P, J]) for k in range(2)]
        none = s.sb("none", [P, P], BF16)
        hist = s.ps("hist", [P, 512])
        none_ready, counted, dve_o = s.sem("none_ready"), s.sem("counted"), s.sem("dve")
        hot = [s.sem(f"hot{k}") for k in range(2)]
        used = [s.sem(f"used{k}") for k in range(2)]
        with nc.Block() as block:
            @block.vector
            def _(dve):
                dve.memset(none[:, :], 0.0).then_inc(none_ready, 1)
                with dve.Fori(0, NCH // 2) as i:
                    o = Order(dve, dve_o, i * 2)
                    for k in range(2):
                        dve.wait_ge(used[k], i)
                        dve.tensor_copy(lo_f[k][:, :], chunk(g.src_lo, i, k))
                        o.link(dve.tensor_copy(hi_f[k][:, :], chunk(g.src_hi, i, k)))
                        dve.tensor_tensor(lo_hot[k][:, :, :], g.count_f[:, :].unsqueeze(1).to_broadcast([P, J, P]),
                                          lo_f[k][:, :].unsqueeze(2).to_broadcast([P, J, P]), ALU.is_equal)
                        dve.tensor_tensor(hi_hot[k][:, :, :],
                                          g.count_f[:, 0:NT].unsqueeze(1).to_broadcast([P, J, NT]),
                                          hi_f[k][:, :].unsqueeze(2).to_broadcast([P, J, NT]),
                                          ALU.is_equal).then_inc(hot[k], 1)
                dve.wait_ge(counted, 1)
                dve.tensor_copy(g.deg[:, :], hist[:, 0:NT])

            @block.tensor
            def _(pe):
                pe.wait_ge(none_ready, 1)
                pe.matmul(hist[:, 0:NT], none[:, :], none[:, 0:NT], start=True, stop=False)
                with pe.Fori(0, NCH // 2) as i:
                    for k in range(2):
                        pe.wait_ge(hot[k], i + 1)
                        for j in range(J):
                            last = pe.matmul(hist[:, 0:NT], lo_hot[k][:, j, :], hi_hot[k][:, j, :], start=False,
                                             stop=False)
                        last.then_inc(used[k], 1)
                pe.matmul(hist[:, 0:NT], none[:, :], none[:, 0:NT], start=False, stop=True).then_inc(counted, 1)


def gather_by_node(nc, g, name, table, index, width, consume, per_turn):
    with Stage(nc, name) as s:
        got_rows = [s.sb(f"rows{k}", [P, GT, width]) for k in range(2)]
        row_g = [s.sb(f"index{k}", [P, GT], I32) for k in range(2)]
        dve_o = s.sem("dve")
        staged = [s.sem(f"staged{k}") for k in range(2)]
        got = [s.sem(f"got{k}") for k in range(2)]
        with nc.Block() as block:
            @block.gpsimd
            def _(pool):
                with pool.Fori(0, NG // 2) as i:
                    for k in range(2):
                        pool.wait_ge(staged[k], i + 1)
                        pool.sem_inc(g.gate, 1)
                        for c in range(GT):
                            pool.indirect_dma_start(got_rows[k][:, c, :], None, table, rows(row_g[k][:, c:c + 1]))\
                                .then_inc(got[k], 16)

            @block.vector
            def _(dve):
                with dve.Fori(0, NG // 2) as i:
                    o = Order(dve, dve_o, i * per_turn)
                    for k in range(2):
                        dve.tensor_copy(row_g[k][:, :], index[:, bass.ds((i * 2 + k) * GT, GT)])\
                            .then_inc(staged[k], 1)
                    for k in range(2):
                        dve.wait_ge(got[k], i * (16 * GT) + 16 * GT)
                        consume(dve, o, i * 2 + k, got_rows[k])
                    assert o.n == per_turn, (name, o.n)


def gather_to(nc, g, name, table, index, width, into):
    def copy(dve, o, group, rows_):
        o.link(dve.tensor_copy(into[:, bass.ds(group * GT, GT), 0:width], rows_[:, :, :]))
    gather_by_node(nc, g, name, table, index, width, copy, 2)


def node_ranges(nc, g):
    n_rows = P * CSPLIT
    dst_rows = g.dst_d.rearrange("p (k c) -> (p k) c", k=CSPLIT)
    with Stage(nc, "ranges") as r:
        cnt, row_f, row_i = r.sb("cnt", [P, NT]), r.sb("rowf", [P, NT]), r.sb("rowi", [P, NT], I32)
        node_g, cnt_g, seen = r.sb("node", [P, GT]), r.sb("cntg", [P, GT]), r.sb("seen", [P, n_rows])

        with Stage(nc, "heads") as s:
            heads = s.sb("heads", [P, n_rows])
            in_, dve_o = s.sem("in"), s.sem("dve")
            with nc.Block() as block:
                @block.sync
                def _(sp):
                    with nc.allow_non_contiguous_dma(reason="one word of each row, once"):
                        sp.dma_start(heads[:, :], dst_rows[:, 0:1].rearrange("r c -> c r").to_broadcast([P, n_rows]))\
                          .then_inc(in_, 16)

                @block.vector
                def _(dve):
                    dve.wait_ge(in_, 16)
                    with dve.Fori(0, NG) as i:
                        o = Order(dve, dve_o, i * (GT + 2))
                        o.link(dve.tensor_copy(node_g[:, :], g.node_f[:, bass.ds(i * GT, GT)]))
                        for c in range(GT):
                            o.link(dve.tensor_scalar(seen[:, :], heads[:, :], node_g[:, c:c + 1], None, ALU.is_le,
                                                     ALU.add, accum_out=cnt_g[:, c:c + 1]))
                        o.link(dve.tensor_copy(cnt[:, bass.ds(i * GT, GT)], cnt_g[:, :]))
                    o = Order(dve, dve_o, NG * (GT + 2))
                    o.link(dve.tensor_scalar(row_f[:, :], cnt[:, :], -1.0, 0.0, ALU.add, ALU.max))
                    dve.tensor_copy(row_i[:, :], row_f[:, :])

        def count(dve, o, group, rows_):
            o.link(dve.tensor_copy(node_g[:, :], g.node_f[:, bass.ds(group * GT, GT)]))
            for c in range(GT):
                o.link(dve.tensor_scalar(seen[:, 0:CROW], rows_[:, c, :], node_g[:, c:c + 1], None, ALU.is_le,
                                         ALU.add, accum_out=cnt_g[:, c:c + 1]))
            o.link(dve.tensor_copy(cnt[:, bass.ds(group * GT, GT)], cnt_g[:, :]))
        gather_by_node(nc, g, "count", dst_rows, row_i, CROW, count, 2 * (GT + 2))

        with Stage(nc, "limits") as s:
            total, before, t = s.sb("total", [P, NT]), s.sb("before", [P, NT]), s.sb("t", [P, NT])
            zero = s.sb("zero", [1, 1])
            d_first, d_prev, d_row = s.sb("dfirst", [P, 1]), s.sb("dprev", [P, 1]), s.sb("drow", [1, P + 1])
            after_first, t_first, fix, ins_ = (s.sb("af", [P, 1], I32), s.sb("tf", [P, 1]), s.sb("fix", [P, 1]),
                                               s.sb("ins", [P, 1]))
            dump_f, dump_n, t1 = s.sb("dump", [P, 1]), s.sb("dumpn", [P, NT]), s.sb("t1", [P, 1])
            dve_o, cleared, ends_in, totalled, stored, before_in, asked, first_total = (
                s.sem(n) for n in ("dve", "cleared", "ends_in", "totalled", "stored", "before_in", "asked",
                                   "first_total"))
            with nc.Block() as block:
                @block.sync
                def _(sp):
                    with nc.allow_non_contiguous_dma(reason="one word per partition or node, once"):
                        sp.wait_ge(cleared, 1)
                        sp.dma_start(d_first[:, :], g.dst_d[:, 0:1]).then_inc(ends_in, 16)
                        sp.dma_start(d_prev[1:P, :], g.dst_d[0:P - 1, EP - 1:EP]).then_inc(ends_in, 16)
                        sp.dma_start(d_row[:, 1:P + 1], g.dst_d[:, EP - 1:EP].rearrange("p o -> o p"))\
                          .then_inc(ends_in, 16)
                        sp.wait_ge(totalled, 1)
                        sp.dma_start(g.total_d[1:NP + 1].rearrange("(t p) o -> p (t o)", p=P), total[:, :])\
                          .then_inc(stored, 16)
                        sp.dma_start(g.total_d[0:1], zero[:, :]).then_inc(stored, 16)
                        sp.wait_ge(stored, 32)
                        sp.dma_start(before[:, :], g.total_d[0:NP].rearrange("(t p) o -> p (t o)", p=P))\
                          .then_inc(before_in, 16)

                @block.gpsimd
                def _(pool):
                    pool.wait_ge(asked, 1)
                    pool.wait_ge(stored, 32)
                    pool.sem_inc(g.gate, 1)
                    pool.indirect_dma_start(t_first[:, :], None, g.total_d, rows(after_first[:, :]))\
                        .then_inc(first_total, 16)

                @block.vector
                def _(dve):
                    o = Order(dve, dve_o)
                    dve.memset(zero[:, :], 0.0)
                    dve.memset(d_row[:, 0:1], -1.0)
                    dve.memset(d_prev[:, :], -1.0).then_inc(cleared, 1)
                    o.link(dve.scalar_tensor_tensor(total[:, :], row_f[:, :], float(CROW), cnt[:, :], ALU.mult,
                                                    ALU.add))
                    dve.tensor_copy(t[:, :], total[:, :]).then_inc(totalled, 1)
                    dve.wait_ge(ends_in, 48)
                    o.link(dve.tensor_scalar(t1[:, :], d_first[:, :], 1.0, None, ALU.add))
                    dve.tensor_copy(after_first[:, :], t1[:, :]).then_inc(asked, 1)
                    dve.tensor_copy(g.dst_first[:, :], d_first[:, :])
                    dve.tensor_tensor(g.joined[:, :], d_row[:, 1:P + 1], d_row[:, 0:P], ALU.is_equal)
                    o.link(dve.tensor_scalar(t[:, :], total[:, :], -1.0, 0.0, ALU.add, ALU.max))
                    dve.tensor_copy(g.last_row[:, :], t[:, :])
                    dve.wait_ge(before_in, 16)
                    o.link(dve.tensor_tensor(g.has[:, :], total[:, :], before[:, :], ALU.is_gt))
                    o.link(dve.tensor_tensor(g.deg[:, :], g.deg[:, :], total[:, :], ALU.add))
                    o.link(dve.tensor_tensor(g.deg[:, :], g.deg[:, :], before[:, :], ALU.subtract))
                    o.link(dve.tensor_scalar(dump_f[:, :], g.lane_f[:, :], float(EROWS), None, ALU.add))
                    o.link(dve.tensor_scalar(dump_n[:, :], g.node_f[:, :], float(EROWS), None, ALU.add))
                    o.link(dve.tensor_tensor(before[:, :], before[:, :], dump_n[:, :], ALU.subtract))
                    o.link(dve.tensor_tensor(before[:, :], before[:, :], g.has[:, :], ALU.mult))
                    o.link(dve.tensor_tensor(before[:, :], before[:, :], dump_n[:, :], ALU.add))
                    dve.tensor_copy(g.start_row[:, :], before[:, :])
                    dve.wait_ge(first_total, 16)
                    o.link(dve.tensor_tensor(fix[:, :], d_first[:, :], d_prev[:, :], ALU.is_equal))
                    o.link(dve.tensor_scalar(t1[:, :], g.first_f[:, :], float(EP), None, ALU.add))
                    o.link(dve.tensor_tensor(ins_[:, :], t_first[:, :], t1[:, :], ALU.is_le))
                    o.link(dve.tensor_tensor(fix[:, :], fix[:, :], ins_[:, :], ALU.mult))
                    for base, row in ((g.first_f, g.mend_from), (dump_f, g.mend_to)):
                        o.link(dve.scalar_tensor_tensor(t1[:, :], t_first[:, :], -1.0, base[:, :], ALU.add,
                                                        ALU.subtract))
                        o.link(dve.tensor_tensor(t1[:, :], t1[:, :], fix[:, :], ALU.mult))
                        o.link(dve.tensor_tensor(t1[:, :], t1[:, :], base[:, :], ALU.add))
                        o.link(dve.tensor_copy(row[:, :], t1[:, :]))



def project(nc, g, name, x, width, weights, cols, table=None, keep=None):
    most = -(-cols // -(-cols // 512))
    parts = [(c, min(most, cols - c)) for c in range(0, cols, most)]
    width_t = table.shape[1] if table is not None else 0
    with Stage(nc, name) as s:
        rows_in = [s.sb(f"x{k}", [P, width]) for k in range(2)]
        turned = [s.sb(f"xt{k}", [width, P]) for k in range(2)]
        rows_out = [s.sb(f"y{k}", [P, cols]) for k in range(2)]
        xt_ps = [s.ps(f"xtp{k}", [P, 512]) for k in range(2)]
        y_ps = [[s.ps(f"yp{k}{n}", [P, 512]) for n in range(len(parts))] for k in range(2)]
        staged, turned_ps, turned_sb, product, copied, stored = (
            [s.sem(f"{n}{k}") for k in range(2)] for n in ("staged", "tps", "tsb", "product", "copied", "stored"))
        view = by_node(table) if table is not None else None
        with nc.Block() as block:
            @block.vector
            def _(dve):
                with dve.Fori(0, NT // 2) as i:
                    for k in range(2):
                        t = i * 2 + k
                        dve.wait_ge(turned_ps[k], i)
                        dve.tensor_copy(rows_in[k][:, :], x[:, bass.ds(t, 1), 0:width].rearrange("p o w -> p (o w)"))\
                            .then_inc(staged[k], 1)
                    for k in range(2):
                        t = i * 2 + k
                        dve.wait_ge(product[k], i + 1)
                        dve.wait_ge(stored[k], i * 16)
                        for n, (c, w) in enumerate(parts):
                            last = dve.tensor_copy(rows_out[k][:, c:c + w], y_ps[k][n][:, 0:w])
                        if keep is not None:
                            into, c0 = keep
                            kw = into.shape[2]
                            c = max(n for n, (c, _) in enumerate(parts) if c <= c0)
                            off = c0 - parts[c][0]
                            last = dve.tensor_copy(into[:, bass.ds(t, 1), :].rearrange("p o w -> p (o w)"),
                                                   y_ps[k][c][:, off:off + kw])
                        last.then_inc(copied[k], 1)

            @block.tensor
            def _(pe):
                with pe.Fori(0, NT // 2) as i:
                    for k in range(2):
                        pe.wait_ge(staged[k], i + 1)
                        pe.wait_ge(turned_sb[k], i)
                        pe.transpose(xt_ps[k][0:width, 0:P], rows_in[k][:, :], g.ident[:, :]).then_inc(turned_ps[k], 1)
                        pe.wait_ge(turned_sb[k], i + 1)
                        pe.wait_ge(copied[k], i)
                        for n, (c, w) in enumerate(parts):
                            last = pe.matmul(y_ps[k][n][:, 0:w], turned[k][:, :], weights[0:width, c:c + w],
                                             start=True, stop=True)
                        last.then_inc(product[k], 1)

            @block.scalar
            def _(act):
                with act.Fori(0, NT // 2) as i:
                    for k in range(2):
                        act.wait_ge(turned_ps[k], i + 1)
                        act.wait_ge(product[k], i)
                        act.copy(turned[k][:, :], xt_ps[k][0:width, 0:P]).then_inc(turned_sb[k], 1)

            @block.sync
            def _(sp):
                with sp.Fori(0, NT // 2) as i:
                    for k in range(2):
                        sp.wait_ge(copied[k], i + 1)
                        if view is None:
                            sp.sem_inc(stored[k], 16)
                        else:
                            sp.dma_start(view[:, bass.ds(i * 2 + k, 1), :].rearrange("p o w -> p (o w)"),
                                         rows_out[k][:, 0:width_t]).then_inc(stored[k], 16)
                for k in range(2):
                    sp.wait_ge(stored[k], 16 * (NT // 2))


def spread(nc, g, name, values, node_table, expand, width):
    w_t = node_table.shape[1]
    with Stage(nc, name) as s:
        vals = [s.sb(f"v{k}", [P, GT, width]) for k in range(2)]
        row_g = [s.sb(f"row{k}", [P, GT], I32) for k in range(2)]
        first = s.sb("first", [P, w_t])
        first_v = s.sb("firstv", [P, width])
        got, ready, put = s.sem("got"), s.sem("ready"), s.sem("put")
        staged = [s.sem(f"staged{k}") for k in range(2)]
        out = [s.sem(f"out{k}") for k in range(2)]
        with nc.Block() as block:
            @block.vector
            def _(dve):
                with dve.Fori(0, NG // 2) as i:
                    for k in range(2):
                        dve.wait_ge(out[k], i * (16 * GT))
                        grp = bass.ds((i * 2 + k) * GT, GT)
                        dve.tensor_copy(row_g[k][:, :], g.start_row[:, grp])
                        dve.tensor_copy(vals[k][:, :, :], values[:, grp, :]).then_inc(staged[k], 1)
                dve.wait_ge(got, 16)
                dve.tensor_copy(first_v[:, :], first[:, w_t - width:w_t]).then_inc(ready, 1)

            @block.gpsimd
            def _(pool):
                pool.indirect_dma_start(first[:, :], None, node_table, rows(g.dst_first[:, :])).then_inc(got, 16)
                with pool.Fori(0, NG // 2) as i:
                    for k in range(2):
                        pool.wait_ge(staged[k], i + 1)
                        pool.sem_inc(g.gate, 1)
                        for c in range(GT):
                            pool.indirect_dma_start(expand, rows(row_g[k][:, c:c + 1]), vals[k][:, c, :], None)\
                                .then_inc(out[k], 16)
                for k in range(2):
                    pool.wait_ge(out[k], 16 * GT * (NG // 2))
                pool.wait_ge(ready, 1)
                pool.indirect_dma_start(expand, rows(g.first_row[:, :]), first_v[:, :], None).then_inc(put, 16)
                pool.wait_ge(put, 16)




def scan_sum(dve, out, keep, values, before):
    return dve.tensor_tensor_scan(out, keep, values, before, ALU.mult, ALU.add)


def scan_max(dve, out, penalty, values, before):
    return dve.tensor_tensor_scan(out, penalty, values, before, ALU.add, ALU.max)


class EdgeBuffers:

    def __init__(self, s, g, table_w, index_d, extras, sums_w):
        self.index_d, self.extras = index_d, extras
        self.rows = [s.sb(f"rows{k}", [P, J, table_w]) for k in range(2)] if table_w else None
        self.index = [s.sb(f"index{k}", [P, J], I32) for k in range(2)] if table_w else None
        self.extra = [[s.sb(f"extra{n}{k}", [P, J, e.shape[2]]) for n, e in enumerate(extras)] for k in range(2)]
        self.keep = [e[0][:, :, :].rearrange("p j o -> p (j o)") for e in self.extra]
        self.sums = [s.sb(f"sums{k}", [P, J, sums_w]) for k in range(2)]
        self.index_in, self.extra_in, self.gathered, self.used, self.done, self.stored = (
            [s.sem(f"{n}{k}") for k in range(2)] for n in ("index_in", "extra_in", "gathered", "used", "done",
                                                           "stored"))

    def load(self, sp):
        with sp.Fori(0, NCH // 2) as i:
            for k in range(2):
                if self.index:
                    sp.wait_ge(self.gathered[k], i * (16 * J))
                    sp.dma_start(self.index[k][:, :], chunk(self.index_d, i, k)).then_inc(self.index_in[k], 16)
                sp.wait_ge(self.done[k], i)
                for n, e in enumerate(self.extras):
                    sp.dma_start(self.extra[k][n][:, :, :], chunk(e, i, k)).then_inc(self.extra_in[k], 16)

    def gather_chunk(self, pool, g, table, turn, k):
        pool.wait_ge(self.done[k], turn)
        pool.wait_ge(self.index_in[k], turn * 16 + 16)
        pool.sem_inc(g.gate, 1)
        for j in range(J):
            pool.indirect_dma_start(self.rows[k][:, j, :], None, table, rows(self.index[k][:, j:j + 1]))\
                .then_inc(self.gathered[k], 16)

    def gather(self, pool, g, table):
        with pool.Fori(0, NCH // 2) as i:
            for k in range(2):
                self.gather_chunk(pool, g, table, i, k)

    def store_chunk(self, act, acc, i, k):
        act.wait_ge(self.done[k], i + 1)
        act.dma_start(chunk(acc, i, k), self.sums[k][:, :, :]).then_inc(self.stored[k], 16)

    def all_stored(self, act):
        for k in range(2):
            act.wait_ge(self.stored[k], 16 * (NCH // 2))

    def wait_rows(self, dve, i, k):
        dve.wait_ge(self.gathered[k], i * (16 * J) + 16 * J)

    def wait_extra(self, dve, i, k):
        dve.wait_ge(self.extra_in[k], (i + 1) * (16 * len(self.extras)))


def attention_pass(nc, g, name, heads, width, table, expand, sums_d):
    hw = heads * width
    with Stage(nc, name) as s:
        b = EdgeBuffers(s, g, hw + 2 * heads, g.src_id, [by_edge(g.keep_t), by_edge(expand)], hw + 2 * heads)
        dst_part = [s.sb(f"dst{k}", [P, J, heads]) for k in range(2)]
        top = [s.sb(f"top{k}", [P, J + 1, heads]) for k in range(2)]
        e_, penalty = s.sb("e", [P, J, heads]), s.sb("penalty", [P, J])
        drop, factor = s.sb("drop", [P, 2, J, heads]), s.sb("factor", [P, 2, J, heads])
        dve_o = s.sem("dve")
        dropped, raised = [s.sem(f"dropped{k}") for k in range(2)], [s.sem(f"raised{k}") for k in range(2)]
        acc = by_edge(sums_d)
        with nc.Block() as block:
            @block.sync
            def _(sp):
                b.load(sp)

            @block.gpsimd
            def _(pool):
                b.gather(pool, g, table)

            @block.vector
            def _(dve):
                o = Order(dve, dve_o)
                dve.memset(dst_part[1][:, J - 1, :], 0.0)
                dve.memset(top[1][:, J, :], 0.0)
                o.link(dve.memset(b.sums[1][:, J - 1, :], 0.0))
                with dve.Fori(0, NCH // 2) as i:
                    o = Order(dve, dve_o, i * 14 + 1)
                    for k in range(2):
                        keep, rows_, sums = b.keep[k], b.rows[k], b.sums[k]
                        before = b.sums[1 - k]
                        b.wait_extra(dve, i, k)
                        for h in range(heads):
                            scan_sum(dve, dst_part[k][:, :, h], keep, b.extra[k][1][:, :, h],
                                     dst_part[1 - k][:, J - 1, h:h + 1])
                        dve.tensor_scalar(penalty[:, :], keep, -1.0, BIG, ALU.add, ALU.mult)
                        o.link(dve.tensor_copy(top[k][:, 0, :], top[1 - k][:, J, :]))
                        b.wait_rows(dve, i, k)
                        o.link(dve.tensor_tensor(e_[:, :, :], rows_[:, :, hw:hw + heads], dst_part[k][:, :, :],
                                                 ALU.add))
                        o.link(dve.scalar_tensor_tensor(e_[:, :, :], e_[:, :, :], SLOPE, e_[:, :, :], ALU.mult,
                                                        ALU.max))
                        for h in range(heads):
                            last = scan_max(dve, top[k][:, 1:J + 1, h], penalty[:, :], e_[:, :, h],
                                            top[k][:, 0, h:h + 1])
                        o.link(last)
                        dve.tensor_tensor(drop[:, 1, :, :], e_[:, :, :], top[k][:, 1:J + 1, :], ALU.subtract)
                        o.link(dve.tensor_tensor(drop[:, 0, :, :], top[k][:, 0:J, :], top[k][:, 1:J + 1, :],
                                                 ALU.subtract))
                        dve.tensor_scalar(drop[:, 0, :, :], drop[:, 0, :, :], 0.0, None, ALU.min)\
                            .then_inc(dropped[k], 1)
                        dve.wait_ge(raised[k], i + 1)
                        o.link(dve.tensor_tensor(factor[:, 0, :, :], factor[:, 0, :, :],
                                                 keep.unsqueeze(2).to_broadcast([P, J, heads]), ALU.mult))
                        shaped = rows_[:, :, 0:hw].rearrange("p j (h c) -> p j h c", h=heads)
                        o.link(dve.tensor_tensor(shaped, shaped, factor[:, 1, :, :].unsqueeze(3)
                                                 .to_broadcast([P, J, heads, width]), ALU.mult))
                        dve.wait_ge(b.stored[k], i * 16)
                        dve.tensor_copy(sums[:, :, hw + heads:], top[k][:, 1:J + 1, :])
                        for h in range(heads):
                            decay = factor[:, 0, :, h]
                            c = hw + h
                            scan_sum(dve, sums[:, :, c], decay, factor[:, 1, :, h], before[:, J - 1, c:c + 1])
                            for c in range(h * width, (h + 1) * width):
                                last = scan_sum(dve, sums[:, :, c], decay, rows_[:, :, c], before[:, J - 1, c:c + 1])
                        last.then_inc(b.done[k], 1)
                        dve.wait_ge(b.done[k], i + 1)
                    assert o.n == 14, o.n

            @block.scalar
            def _(act):
                with act.Fori(0, NCH // 2) as i:
                    for k in range(2):
                        act.wait_ge(dropped[k], i + 1)
                        act.activation(factor[:, :, :, :], drop[:, :, :, :], ACT.Exp).then_inc(raised[k], 1)
                        b.store_chunk(act, acc, i, k)
                b.all_stored(act)


def carry_over(nc, g, name, sums_d, width, heads=0):
    acc = by_edge(sums_d)
    hw = width - 2 * heads
    per = hw // heads if heads else 0
    with Stage(nc, name) as s:
        line = s.sb("line", [1, P, width])
        own, from_before = s.sb("own", [P, width]), s.sb("before", [P, width])
        top = s.sb("top", [1, P + 1, max(heads, 1)])
        penalty, drop, factor = (s.sb("penalty", [1, P]), s.sb("drop", [1, 2, P, max(heads, 1)]),
                                 s.sb("factor", [1, 2, P, max(heads, 1)]))
        top2, drop2, factor2 = (s.sb("top2", [P, max(heads, 1)]), s.sb("drop2", [P, 2, max(heads, 1)]),
                                s.sb("factor2", [P, 2, max(heads, 1)]))
        line_in, dve_o, scanned, line_out, before_in, cleared, own_in, mended, put, dropped, raised = (
            s.sem(n) for n in ("line_in", "dve", "scanned", "line_out", "before_in", "cleared", "own_in", "mended",
                               "put", "dropped", "raised"))
        carry = g.carry_d[:, 0:width]
        joined = g.joined[:, :]
        with nc.Block() as block:
            @block.sync
            def _(sp):
                sp.dma_start(line[:, :, :], acc[:, EP - 1:EP, :].rearrange("p o w -> o p w")).then_inc(line_in, 16)
                sp.wait_ge(scanned, 1)
                sp.dma_start(carry[1:P, :].unsqueeze(0), line[:, 0:P - 1, :]).then_inc(line_out, 16)
                sp.wait_ge(line_out, 16)
                sp.wait_ge(cleared, 1)
                sp.dma_start(from_before[1:P, :], carry[1:P, :]).then_inc(before_in, 16)

            @block.gpsimd
            def _(pool):
                pool.indirect_dma_start(own[:, :], None, sums_d, rows(g.mend_from[:, :])).then_inc(own_in, 16)
                pool.wait_ge(mended, 1)
                pool.indirect_dma_start(sums_d, rows(g.mend_to[:, :]), own[:, :], None).then_inc(put, 16)
                pool.wait_ge(put, 16)

            @block.vector
            def _(dve):
                o = Order(dve, dve_o)
                dve.memset(from_before[:, :], 0.0).then_inc(cleared, 1)
                dve.wait_ge(line_in, 16)
                if not heads:
                    for c in range(width):
                        last = scan_sum(dve, line[:, :, c], joined, line[:, :, c], 0.0)
                    last.then_inc(scanned, 1)
                    dve.wait_ge(own_in, 16)
                    dve.wait_ge(before_in, 16)
                    dve.tensor_tensor(own[:, :], own[:, :], from_before[:, :], ALU.add).then_inc(mended, 1)
                    return
                dve.tensor_scalar(penalty[:, :], joined, -1.0, BIG, ALU.add, ALU.mult)
                o.link(dve.memset(top[:, 0, :], 0.0))
                for h in range(heads):
                    last = scan_max(dve, top[:, 1:P + 1, h], penalty[:, :], line[:, :, hw + heads + h], 0.0)
                o.link(last)
                dve.tensor_tensor(drop[:, 1, :, :], line[:, :, hw + heads:], top[:, 1:P + 1, :], ALU.subtract)
                o.link(dve.tensor_tensor(drop[:, 0, :, :], top[:, 0:P, :], top[:, 1:P + 1, :], ALU.subtract))
                dve.tensor_scalar(drop[:, 0, :, :], drop[:, 0, :, :], 0.0, None, ALU.min).then_inc(dropped, 1)
                dve.wait_ge(raised, 1)
                dve.tensor_tensor(factor[:, 0, :, :], factor[:, 0, :, :],
                                  joined.unsqueeze(2).to_broadcast([1, P, heads]), ALU.mult)
                shaped = line[:, :, 0:hw].rearrange("o p (h c) -> o p h c", h=heads)
                dve.tensor_tensor(shaped, shaped, factor[:, 1, :, :].unsqueeze(3).to_broadcast([1, P, heads, per]),
                                  ALU.mult)
                dve.tensor_copy(line[:, :, hw + heads:], top[:, 1:P + 1, :])
                o.link(dve.tensor_tensor(line[:, :, hw:hw + heads], line[:, :, hw:hw + heads], factor[:, 1, :, :],
                                         ALU.mult))
                for h in range(heads):
                    for c in [hw + h, *range(h * per, (h + 1) * per)]:
                        last = scan_sum(dve, line[:, :, c], factor[:, 0, :, h], line[:, :, c], 0.0)
                last.then_inc(scanned, 1)
                dve.wait_ge(own_in, 16)
                dve.wait_ge(before_in, 16)
                o.link(dve.tensor_tensor(top2[:, :], own[:, hw + heads:], from_before[:, hw + heads:], ALU.max))
                dve.tensor_tensor(drop2[:, 0, :], own[:, hw + heads:], top2[:, :], ALU.subtract)
                dve.tensor_tensor(drop2[:, 1, :], from_before[:, hw + heads:], top2[:, :], ALU.subtract)\
                    .then_inc(dropped, 1)
                dve.wait_ge(raised, 2)
                for n, t in enumerate((own, from_before)):
                    shaped = t[:, 0:hw].rearrange("p (h c) -> p h c", h=heads)
                    dve.tensor_tensor(shaped, shaped, factor2[:, n, :].unsqueeze(2).to_broadcast([P, heads, per]),
                                      ALU.mult)
                    last = dve.tensor_tensor(t[:, hw:hw + heads], t[:, hw:hw + heads], factor2[:, n, :], ALU.mult)
                o.link(last)
                dve.tensor_copy(own[:, hw + heads:], top2[:, :])
                dve.tensor_tensor(own[:, 0:hw + heads], own[:, 0:hw + heads], from_before[:, 0:hw + heads], ALU.add)\
                    .then_inc(mended, 1)

            @block.scalar
            def _(act):
                if heads:
                    act.wait_ge(dropped, 1)
                    act.activation(factor[:, :, :, :], drop[:, :, :, :], ACT.Exp).then_inc(raised, 1)
                    act.wait_ge(dropped, 2)
                    act.activation(factor2[:, :, :], drop2[:, :, :], ACT.Exp).then_inc(raised, 1)



def load_constants(nc, name, pairs):
    with Stage(nc, name) as s:
        in_ = s.sem("in")
        with nc.Block() as block:
            @block.sync
            def _(sp):
                with nc.allow_non_contiguous_dma(reason="small weights, once"):
                    for dst, src in pairs:
                        sp.dma_start(dst, src).then_inc(in_, 16)
                    sp.wait_ge(in_, 16 * len(pairs))


def layer_norm(nc, g, name):
    with Stage(nc, name) as s:
        sq, total, mean, var, std = s.sb("sq", [P, NT, FD]), *(s.sb(n, [P, NT]) for n in ("tot", "mean", "var", "std"))
        dve_o, var_ready, root = s.sem("dve"), s.sem("var_ready"), s.sem("root")
        x, h = g.x[:, :, :], g.h[:, :, :]
        wide = [P, NT, FD]
        with nc.Block() as block:
            @block.vector
            def _(dve):
                o = Order(dve, dve_o)
                o.link(dve.tensor_reduce(total[:, :], x, AX.X, ALU.add))
                o.link(dve.tensor_scalar(mean[:, :], total[:, :], 1.0 / FD, None, ALU.mult))
                o.link(dve.tensor_tensor(h, x, mean[:, :].unsqueeze(2).to_broadcast(wide), ALU.subtract))
                o.link(dve.tensor_tensor(sq[:, :, :], h, h, ALU.mult))
                o.link(dve.tensor_reduce(total[:, :], sq[:, :, :], AX.X, ALU.add))
                dve.tensor_scalar(var[:, :], total[:, :], 1.0 / FD, 1e-5, ALU.mult, ALU.add).then_inc(var_ready, 1)
                dve.wait_ge(root, 1)
                o.link(dve.reciprocal(mean[:, :], std[:, :]))
                o.link(dve.tensor_tensor(h, h, mean[:, :].unsqueeze(2).to_broadcast(wide), ALU.mult))
                dve.tensor_scalar(h, h, 0.0, None, ALU.max)

            @block.scalar
            def _(act):
                act.wait_ge(var_ready, 1)
                act.activation(std[:, :], var[:, :], ACT.Sqrt).then_inc(root, 1)


def attention_weights(nc, g, name, w, a_src, a_dst, into, rows_w, heads, width):
    hw = heads * width
    with Stage(nc, name) as s:
        both, prod = s.sb("both", [rows_w, 2, hw]), s.sb("prod", [rows_w, 2, hw])
        in_, dve_o = s.sem("in"), s.sem("dve")
        with nc.Block() as block:
            @block.sync
            def _(sp):
                sp.dma_start(into[0:rows_w, 0:hw], w).then_inc(in_, 16)
                for n, v in enumerate((a_src, a_dst)):
                    sp.dma_start(both[:, n, :], v.rearrange("h c -> (h c)").partition_broadcast(rows_w))\
                        .then_inc(in_, 16)

            @block.vector
            def _(dve):
                o = Order(dve, dve_o)
                dve.wait_ge(in_, 48)
                o.link(dve.tensor_tensor(prod[:, :, :], both[:, :, :],
                                         into[0:rows_w, 0:hw].unsqueeze(1).to_broadcast([rows_w, 2, hw]), ALU.mult))
                dve.tensor_reduce(into[0:rows_w, hw:hw + 2 * heads],
                                  prod[:, :, :].rearrange("p n (h c) -> p (n h) c", h=heads), AX.X, ALU.add)


def finish_attention(nc, g, name, sums, table, bias, heads, width):
    hw = heads * width
    part_w = [P, NT, heads]
    with Stage(nc, name) as s:
        own, e_, top, drop, factor, inv = (s.sb("own", [P, NT, hw + 2 * heads]), s.sb("e", part_w), s.sb("top", part_w),
                                           s.sb("drop", [P, 2, NT, heads]), s.sb("factor", [P, 2, NT, heads]),
                                           s.sb("inv", part_w))
        own_in, dve_o, dropped, weighed, cut, raised = (
            s.sem(n) for n in ("own_in", "dve", "dropped", "weighed", "cut", "raised"))
        v, low = sums[:, :, 0:hw], own[:, :, 0:hw]

        def per_head(dve, t, scale):
            for h in range(heads):
                part = t[:, :, h * width:(h + 1) * width]
                last = dve.tensor_tensor(part, part, scale[:, :, h].unsqueeze(2).to_broadcast([P, NT, width]),
                                         ALU.mult)
            return last

        with nc.Block() as block:
            @block.sync
            def _(sp):
                sp.dma_start(own[:, :, :], by_node(table)).then_inc(own_in, 16)

            @block.vector
            def _(dve):
                o = Order(dve, dve_o)
                o.link(dve.tensor_scalar(inv[:, :, 0], g.has[:, :], -1.0, BIG, ALU.add, ALU.mult))
                m = sums[:, :, hw + heads:]
                o.link(dve.tensor_tensor(m, m, inv[:, :, 0].unsqueeze(2).to_broadcast(part_w), ALU.add))
                dve.wait_ge(own_in, 16)
                o.link(dve.tensor_tensor(e_[:, :, :], own[:, :, hw:hw + heads], own[:, :, hw + heads:], ALU.add))
                o.link(dve.scalar_tensor_tensor(e_[:, :, :], e_[:, :, :], SLOPE, e_[:, :, :], ALU.mult, ALU.max))
                o.link(dve.tensor_tensor(top[:, :, :], e_[:, :, :], m, ALU.max))
                dve.tensor_tensor(drop[:, 0, :, :], m, top[:, :, :], ALU.subtract)
                dve.tensor_tensor(drop[:, 1, :, :], e_[:, :, :], top[:, :, :], ALU.subtract).then_inc(dropped, 1)
                dve.wait_ge(weighed, 1)
                z = sums[:, :, hw:hw + heads]
                per_head(dve, v, factor[:, 0, :, :])
                per_head(dve, low, factor[:, 1, :, :])
                o.link(dve.tensor_tensor(z, z, factor[:, 0, :, :], ALU.mult))
                o.link(dve.tensor_tensor(z, z, factor[:, 1, :, :], ALU.add))
                o.link(dve.tensor_scalar(inv[:, :, :], z, 1e-16, None, ALU.add))
                o.step(dve.reciprocal(inv[:, :, :], inv[:, :, :]))
                o.link(dve.tensor_tensor(v, v, low, ALU.add))
                o.link(per_head(dve, v, inv))
                o.link(dve.tensor_tensor(v, v, bias.unsqueeze(1).to_broadcast([P, NT, hw]), ALU.add))
                dve.tensor_scalar(low, v, 0.0, None, ALU.min).then_inc(cut, 1)
                dve.wait_ge(raised, 1)
                sa = SELU_SCALE * SELU_ALPHA
                dve.tensor_scalar(v, v, 0.0, SELU_SCALE, ALU.max, ALU.mult)
                o.link(dve.tensor_scalar(low, low, sa, -sa, ALU.mult, ALU.add))
                dve.tensor_tensor(v, v, low, ALU.add)

            @block.scalar
            def _(act):
                act.wait_ge(dropped, 1)
                act.activation(factor[:, :, :, :], drop[:, :, :, :], ACT.Exp).then_inc(weighed, 1)
                act.wait_ge(cut, 1)
                act.activation(low, low, ACT.Exp).then_inc(raised, 1)


def relation_pass(nc, g, name, table, index_d, sums_d, expand=None):
    first = expand is not None
    extras = [by_edge(g.keep_t)] + ([by_edge(g.type8_t), by_edge(expand)] if first else [by_edge(g.norm_t)])
    with Stage(nc, name) as s:
        b = EdgeBuffers(s, g, FD, index_d, extras, FD)
        inv = [s.sb(f"inv{k}", [P, J, R8]) for k in range(2)]
        hot = s.sb("hot", [P, J, R8])
        norm = [s.sb(f"norm{k}", [P, J]) for k in range(2)]
        dve_o = s.sem("dve")
        norm_ready, norm_stored = [s.sem(f"norm_ready{k}") for k in range(2)], [s.sem(f"norm_out{k}") for k in range(2)]
        acc = by_edge(sums_d)
        norm_d = g.norm_t.rearrange("(p j) o -> p (j o)", p=P)
        with nc.Block() as block:
            @block.sync
            def _(sp):
                b.load(sp)

            @block.gpsimd
            def _(pool):
                b.gather(pool, g, table)

            @block.vector
            def _(dve):
                o = Order(dve, dve_o)
                dve.memset(inv[1][:, J - 1, :], 0.0)
                o.link(dve.memset(b.sums[1][:, J - 1, :], 0.0))
                per = 8 if first else 2
                with dve.Fori(0, NCH // 2) as i:
                    o = Order(dve, dve_o, i * per + 1)
                    for k in range(2):
                        rows_, sums = b.rows[k], b.sums[k]
                        b.wait_extra(dve, i, k)
                        if first:
                            kind = b.extra[k][1][:, :, :].rearrange("p j o -> p (j o)")
                            for r in range(R8):
                                last = scan_sum(dve, inv[k][:, :, r], b.keep[k], b.extra[k][2][:, :, r],
                                                inv[1 - k][:, J - 1, r:r + 1])
                            o.step(last)
                            o.link(dve.tensor_tensor(hot[:, :, :],
                                                     g.count_f[:, 0:R8].unsqueeze(1).to_broadcast([P, J, R8]),
                                                     kind.unsqueeze(2).to_broadcast([P, J, R8]), ALU.is_equal))
                            o.link(dve.tensor_tensor(hot[:, :, :], hot[:, :, :], inv[k][:, :, :], ALU.mult))
                            dve.wait_ge(norm_stored[k], i * 16)
                            dve.tensor_reduce(norm[k][:, :], hot[:, :, :], AX.X, ALU.add).then_inc(norm_ready[k], 1)
                            dve.wait_ge(norm_ready[k], i + 1)
                            scale = norm[k][:, :]
                        else:
                            scale = b.extra[k][1][:, :, :].rearrange("p j o -> p (j o)")
                        b.wait_rows(dve, i, k)
                        o.link(dve.tensor_tensor(rows_[:, :, :], rows_[:, :, :],
                                                 scale.unsqueeze(2).to_broadcast([P, J, FD]), ALU.mult))
                        dve.wait_ge(b.stored[k], i * 16)
                        for c in range(FD):
                            last = scan_sum(dve, sums[:, :, c], b.keep[k], rows_[:, :, c],
                                            b.sums[1 - k][:, J - 1, c:c + 1])
                        last.then_inc(b.done[k], 1)
                        dve.wait_ge(b.done[k], i + 1)
                    assert o.n == per, o.n

            @block.scalar
            def _(act):
                with act.Fori(0, NCH // 2) as i:
                    for k in range(2):
                        if first:
                            act.wait_ge(norm_ready[k], i + 1)
                            act.dma_start(chunk(norm_d, i, k), norm[k][:, :]).then_inc(norm_stored[k], 16)
                        b.store_chunk(act, acc, i, k)
                b.all_stored(act)
                if first:
                    for k in range(2):
                        act.wait_ge(norm_stored[k], 16 * (NCH // 2))


def count_pass(nc, g, name, sums_d):
    with Stage(nc, name) as s:
        b = EdgeBuffers(s, g, 0, None, [by_edge(g.keep_t), by_edge(g.type8_t)], R8)
        hot = s.sb("hot", [P, J, R8])
        dve_o = s.sem("dve")
        acc = by_edge(sums_d)
        with nc.Block() as block:
            @block.sync
            def _(sp):
                b.load(sp)

            @block.vector
            def _(dve):
                o = Order(dve, dve_o)
                o.link(dve.memset(b.sums[1][:, J - 1, :], 0.0))
                with dve.Fori(0, NCH // 2) as i:
                    o = Order(dve, dve_o, i * 2 + 1)
                    for k in range(2):
                        b.wait_extra(dve, i, k)
                        kind = b.extra[k][1][:, :, :].rearrange("p j o -> p (j o)")
                        o.link(dve.tensor_tensor(hot[:, :, :],
                                                 g.count_f[:, 0:R8].unsqueeze(1).to_broadcast([P, J, R8]),
                                                 kind.unsqueeze(2).to_broadcast([P, J, R8]), ALU.is_equal))
                        dve.wait_ge(b.stored[k], i * 16)
                        for r in range(R8):
                            last = scan_sum(dve, b.sums[k][:, :, r], b.keep[k], hot[:, :, r],
                                            b.sums[1 - k][:, J - 1, r:r + 1])
                        last.then_inc(b.done[k], 1)
                        dve.wait_ge(b.done[k], i + 1)

            @block.scalar
            def _(act):
                with act.Fori(0, NCH // 2) as i:
                    for k in range(2):
                        b.store_chunk(act, acc, i, k)
                b.all_stored(act)


def reciprocal_counts(nc, g, name, counts, node_table):
    with Stage(nc, name) as s:
        dve_o, ready, out_ = s.sem("dve"), s.sem("ready"), s.sem("out")
        with nc.Block() as block:
            @block.vector
            def _(dve):
                o = Order(dve, dve_o)
                c = counts[:, :, :]
                o.link(dve.tensor_tensor(c, c, g.has[:, :].unsqueeze(2).to_broadcast([P, NT, R8]), ALU.mult))
                o.link(dve.tensor_scalar(c, c, 1.0, None, ALU.max))
                dve.reciprocal(c, c).then_inc(ready, 1)

            @block.sync
            def _(sp):
                sp.wait_ge(ready, 1)
                sp.dma_start(by_node(node_table), counts[:, :, :]).then_inc(out_, 16)
                sp.wait_ge(out_, 16)


def finish_relation(nc, g, name, agg, root_part, bias, into, last):
    wide = [P, NT, FD]
    with Stage(nc, name) as s:
        exps, top, total, log = s.sb("exps", wide), *(s.sb(n, [P, NT]) for n in ("top", "total", "log"))
        dve_o, shifted, raised, summed, logged = (s.sem(n) for n in ("dve", "shifted", "raised", "summed", "logged"))
        with nc.Block() as block:
            @block.vector
            def _(dve):
                o = Order(dve, dve_o)
                v = agg[:, :, :]
                o.link(dve.tensor_tensor(v, v, g.has[:, :].unsqueeze(2).to_broadcast(wide), ALU.mult))
                o.link(dve.tensor_tensor(v, v, root_part[:, :, :], ALU.add))
                o.link(dve.tensor_tensor(v, v, bias.unsqueeze(1).to_broadcast(wide), ALU.add))
                if not last:
                    dve.tensor_scalar(into[:, :, :], v, 0.0, None, ALU.max)
                    return
                o.link(dve.tensor_reduce(top[:, :], v, AX.X, ALU.max))
                dve.tensor_tensor(v, v, top[:, :].unsqueeze(2).to_broadcast(wide), ALU.subtract).then_inc(shifted, 1)
                dve.wait_ge(raised, 1)
                dve.tensor_reduce(total[:, :], exps[:, :, :], AX.X, ALU.add).then_inc(summed, 1)
                dve.wait_ge(logged, 1)
                o.link(dve.tensor_tensor(v, v, log[:, :].unsqueeze(2).to_broadcast(wide), ALU.subtract))
                dve.tensor_tensor(g.x[:, :, :], g.x[:, :, :], v, ALU.add)

            @block.scalar
            def _(act):
                if last:
                    act.wait_ge(shifted, 1)
                    act.activation(exps[:, :, :], agg[:, :, :], ACT.Exp).then_inc(raised, 1)
                    act.wait_ge(summed, 1)
                    act.activation(log[:, :], total[:, :], ACT.Ln).then_inc(logged, 1)


def sheaf_pass(nc, g, name, w1, w2, b1, b2, table, expand, sums_d):
    QC = 4
    NQ = J // QC
    HALF = J // 2
    F2 = 2 * FD
    HID = P // 2
    with Stage(nc, name) as s:
        b = EdgeBuffers(s, g, FD + 1, g.src_id, [by_edge(g.keep_t), by_edge(expand), by_edge(g.src_t)], FD)
        src_of = [e[2][:, :, :].rearrange("p j o -> p (j o)") for e in b.extra]
        filled = [s.sb(f"filled{k}", [P, J, FD + 1]) for k in range(2)]
        ends = s.sb("ends", [P, J, F2])
        v = s.sb("v", [P, J, F2])
        prod, once, twice = s.sb("prod", [P, J, F2]), s.sb("once", [P, J, F2]), s.sb("twice", [P, J, F2])
        dots, inv2 = s.sb("dots", [P, J, 2]), s.sb("inv2", [P, J, 2])
        same = s.sb("same", [P, J, P])
        earlier = s.sb("earlier", [P, QC, P])
        rank, place = s.sb("rank", [P, J]), s.sb("place", [P, J])
        spare_f = s.sb("spare", [P, 1])
        to_row = [s.sb(f"torow{k}", [P, J], I32) for k in range(2)]
        to_add = [s.sb(f"toadd{k}", [P, J, FD]) for k in range(2)]
        ends_t = s.sb("endst", [F2, QC * P])
        hidden = [s.sb(f"hidden{k}", [P, QC * P]) for k in range(2)]
        across = [s.ps(f"across{k}", [P, QC * P]) for k in range(2)]
        ends_ps, hidden_ps, v_ps = s.ps("endsp", [F2, QC * P]), s.ps("hiddenp", [P, QC * P]), s.ps("vp", [P, QC * F2])
        added_ps = [s.ps(f"added{n}", [P, HALF * FD]) for n in range(2)]
        (dve_o, ends_ready, across_ready, across_used, ends_turned, ends_copied, hid_ready, hid_done, v_ready, v_used,
         same_ready, msg_ready, added) = (
            s.sem(n) for n in ("dve", "ends_ready", "across_ready", "across_used", "ends_turned", "ends_copied",
                               "hid_ready", "hid_done", "v_ready", "v_used", "same_ready", "msg_ready", "added"))
        to_add_ready = [s.sem(f"to_add_ready{k}") for k in range(2)]
        summed = [[s.sem(f"summed{k}{r}") for r in range(NSUM)] for k in range(2)]
        acc = by_edge(sums_d)
        per_table = J // NSUM
        with nc.Block() as block:
            @block.sync
            def _(sp):
                b.load(sp)

            @block.gpsimd
            def _(pool):
                def scatter_chunk(i, k):
                    pool.wait_ge(to_add_ready[k], i + 1)
                    pool.sem_inc(g.gate, 1)
                    for j in range(J):
                        r = j % NSUM
                        pool.wait_ge(summed[k][r], i * (16 * per_table) + 16 * (j // NSUM))
                        pool.sem_inc(g.gate, 1)
                        pool.indirect_dma_start(g.by_src[k][r], rows(to_row[k][:, j:j + 1]), to_add[k][:, j, :], None,
                                                compute_op=ALU.add).then_inc(summed[k][r], 16)
                for k in range(2):
                    b.gather_chunk(pool, g, table, 0, k)
                with pool.Fori(0, NCH // 2 - 1) as i:
                    for k in range(2):
                        scatter_chunk(i, k)
                        b.gather_chunk(pool, g, table, i + 1, k)
                for k in range(2):
                    scatter_chunk(NCH // 2 - 1, k)
                for k in range(2):
                    for r in range(NSUM):
                        pool.wait_ge(summed[k][r], 16 * per_table * (NCH // 2))

            @block.vector
            def _(dve):
                o = Order(dve, dve_o)
                dve.memset(filled[1][:, J - 1, :], 0.0)
                dve.tensor_scalar(spare_f[:, :], g.lane_f[:, :], float(NP), None, ALU.add)
                o.link(dve.memset(b.sums[1][:, J - 1, :], 0.0))
                per = 2 * (NQ + 16)
                with dve.Fori(0, NCH // 2) as i:
                    o = Order(dve, dve_o, i * per + 1)
                    for k in range(2):
                        q0 = i * (2 * NQ) + k * NQ
                        c0 = i * 2 + k
                        rows_, sums = b.rows[k], b.sums[k]
                        b.wait_extra(dve, i, k)
                        for c in range(FD + 1):
                            last = scan_sum(dve, filled[k][:, :, c], b.keep[k], b.extra[k][1][:, :, c],
                                            filled[1 - k][:, J - 1, c:c + 1])
                        o.link(last)
                        b.wait_rows(dve, i, k)
                        dve.tensor_copy(ends[:, :, 0:FD], rows_[:, :, 0:FD])
                        dve.tensor_copy(ends[:, :, FD:F2], filled[k][:, :, 0:FD]).then_inc(ends_ready, 1)

                        def take_v(q):
                            dve.wait_ge(v_ready, q0 + q + 1)
                            dve.tensor_tensor(v[:, q * QC:(q + 1) * QC, :],
                                              v_ps[:, :].rearrange("p (c w) -> p c w", c=QC),
                                              b2.unsqueeze(1).to_broadcast([P, QC, F2]), ALU.add).then_inc(v_used, 1)
                        for q in range(NQ):
                            js = slice(q * QC, (q + 1) * QC)
                            dve.wait_ge(across_ready, q0 + q + 1)
                            o.link(dve.tensor_tensor(same[:, js, :],
                                                     across[q % 2][:, :].rearrange("p (c w) -> p c w", c=QC),
                                                     src_of[k][:, js].unsqueeze(2).to_broadcast([P, QC, P]),
                                                     ALU.is_equal))
                            dve.tensor_tensor(earlier[:, :, :], same[:, js, :],
                                              g.strict[:, :].unsqueeze(1).to_broadcast([P, QC, P]), ALU.mult)\
                                .then_inc(across_used, 1)
                            dve.wait_ge(across_used, q0 + q + 1)
                            dve.tensor_reduce(rank[:, js], earlier[:, :, :], AX.X, ALU.add).then_inc(same_ready, 1)
                            if q >= 1:
                                take_v(q - 1)
                            dve.wait_ge(same_ready, q0 + q + 1)
                        take_v(NQ - 1)
                        dve.wait_ge(v_used, q0 + NQ)
                        o.link(dve.tensor_scalar(rank[:, :], rank[:, :], 0.0, None, ALU.is_equal))
                        o.link(dve.tensor_scalar(place[:, :], src_of[k], spare_f[:, :], None, ALU.subtract))
                        o.link(dve.tensor_tensor(place[:, :], place[:, :], rank[:, :], ALU.mult))
                        for r in range(NSUM):
                            dve.wait_ge(summed[k][r], i * (16 * per_table))
                        dve.tensor_scalar(to_row[k][:, :], place[:, :], spare_f[:, :], None, ALU.add)
                        pairs = [P, J, 2]

                        def halves(t):
                            return t[:, :, :].rearrange("p j (n c) -> p j n c", n=2)

                        def wide(t):
                            return t[:, :, :].unsqueeze(3).to_broadcast([P, J, 2, FD])
                        o.link(dve.tensor_tensor(prod[:, :, :], v[:, :, :], v[:, :, :], ALU.mult))
                        o.link(dve.tensor_reduce(inv2[:, :, :], halves(prod), AX.X, ALU.add))
                        o.link(dve.tensor_scalar(inv2[:, :, :], inv2[:, :, :], 0.5, 0.5e-24, ALU.mult, ALU.max))
                        dve.reciprocal(inv2[:, :, :], inv2[:, :, :])
                        o.link(dve.tensor_tensor(prod[:, :, :], v[:, :, :], ends[:, :, :], ALU.mult))
                        o.link(dve.tensor_reduce(dots[:, :, :], halves(prod), AX.X, ALU.add))
                        o.link(dve.tensor_tensor(dots[:, :, :], dots[:, :, :], inv2[:, :, :], ALU.mult))
                        o.link(dve.tensor_tensor(halves(prod), halves(v), wide(dots), ALU.mult))
                        o.link(dve.tensor_tensor(once[:, :, :], ends[:, :, :], prod[:, :, :], ALU.subtract))
                        dve.tensor_tensor(prod[:, :, 0:FD], v[:, :, 0:FD], once[:, :, FD:F2], ALU.mult)
                        o.link(dve.tensor_tensor(prod[:, :, FD:F2], v[:, :, FD:F2], once[:, :, 0:FD], ALU.mult))
                        o.link(dve.tensor_reduce(dots[:, :, :], halves(prod), AX.X, ALU.add))
                        o.link(dve.tensor_tensor(dots[:, :, :], dots[:, :, :], inv2[:, :, :], ALU.mult))
                        o.link(dve.tensor_tensor(halves(prod), halves(v), wide(dots), ALU.mult))
                        dve.tensor_tensor(twice[:, :, 0:FD], once[:, :, FD:F2], prod[:, :, 0:FD], ALU.subtract)\
                            .then_inc(msg_ready, 1)
                        dve.tensor_tensor(twice[:, :, FD:F2], once[:, :, 0:FD], prod[:, :, FD:F2], ALU.subtract)\
                            .then_inc(msg_ready, 1)
                        dve.wait_ge(msg_ready, c0 * 4 + 2)
                        dve.tensor_tensor(twice[:, :, FD:F2], twice[:, :, FD:F2],
                                          rows_[:, :, FD:].to_broadcast([P, J, FD]), ALU.mult).then_inc(msg_ready, 1)
                        dve.tensor_tensor(twice[:, :, 0:FD], twice[:, :, 0:FD],
                                          filled[k][:, :, FD:].to_broadcast([P, J, FD]), ALU.mult)\
                            .then_inc(msg_ready, 1)
                        dve.wait_ge(msg_ready, c0 * 4 + 4)
                        dve.wait_ge(b.stored[k], i * 16)
                        for c in range(FD):
                            last = scan_sum(dve, sums[:, :, c], b.keep[k], twice[:, :, FD + c],
                                            b.sums[1 - k][:, J - 1, c:c + 1])
                        last.then_inc(b.done[k], 1)
                        dve.wait_ge(added, c0 + 1)
                        for n in range(2):
                            last = dve.tensor_copy(to_add[k][:, n * HALF:(n + 1) * HALF, :],
                                                   added_ps[n][:, :].rearrange("p (c w) -> p c w", w=FD))
                        last.then_inc(to_add_ready[k], 1)
                        dve.wait_ge(to_add_ready[k], i + 1)
                    assert o.n == per, o.n

            @block.tensor
            def _(pe):
                with pe.Fori(0, NCH // 2) as i:
                    for k in range(2):
                        q0 = i * (2 * NQ) + k * NQ
                        c0 = i * 2 + k
                        pe.wait_ge(ends_ready, c0 + 1)

                        def hide(q):
                            pe.wait_ge(ends_copied, q0 + q + 1)
                            if q == 0:
                                pe.wait_ge(hid_done, q0)
                            else:
                                pe.wait_ge(hid_done, q0 + q)
                            pe.matmul(hidden_ps[:, :], w1, ends_t[:, :], start=True, stop=True).then_inc(hid_ready, 1)

                        def unhide(q):
                            pe.wait_ge(hid_done, q0 + q + 1)
                            pe.wait_ge(v_used, q0 + q)
                            for c in range(QC):
                                last = pe.matmul(v_ps[:, c * F2:(c + 1) * F2],
                                                 hidden[(q + k * NQ) % 2][:, c * P:(c + 1) * P], w2,
                                                 start=True, stop=True)
                            last.then_inc(v_ready, 1)
                        for q in range(NQ):
                            if q >= 2:
                                pe.wait_ge(across_used, q0 + q - 1)
                            for c in range(QC):
                                j = q * QC + c
                                last = pe.matmul(across[q % 2][:, c * P:(c + 1) * P],
                                                 src_of[k][:, j:j + 1].to_broadcast([P, P]), g.ident[:, :],
                                                 start=True, stop=True)
                            last.then_inc(across_ready, 1)
                            pe.wait_ge(ends_copied, q0 + q)
                            for c in range(QC):
                                last = pe.transpose(ends_ps[:, c * P:(c + 1) * P], ends[:, q * QC + c, :],
                                                    g.ident[:, :])
                            last.then_inc(ends_turned, 1)
                            hide(q)
                            if q >= 1:
                                unhide(q - 1)
                        unhide(NQ - 1)
                        pe.wait_ge(msg_ready, c0 * 4 + 4)
                        pe.wait_ge(same_ready, q0 + NQ)
                        for j in range(J):
                            last = pe.matmul(added_ps[j // HALF][:, (j % HALF) * FD:(j % HALF + 1) * FD],
                                             same[:, j, :], twice[:, j, 0:FD], start=True, stop=True)
                        last.then_inc(added, 1)

            @block.scalar
            def _(act):
                with act.Fori(0, NCH // 2) as i:
                    for k in range(2):
                        q0 = i * (2 * NQ) + k * NQ
                        for q in range(NQ):
                            act.wait_ge(ends_turned, q0 + q + 1)
                            act.wait_ge(hid_ready, q0 + q)
                            act.copy(ends_t[:, :], ends_ps[:, :]).then_inc(ends_copied, 1)
                            act.wait_ge(hid_ready, q0 + q + 1)
                            if q >= 2:
                                act.wait_ge(v_ready, q0 + q - 1)
                            elif k == 0:
                                act.wait_ge(v_ready, q0)
                            else:
                                act.wait_ge(v_ready, q0 + q - 1)
                            act.activation(hidden[(q + k * NQ) % 2][:, :], hidden_ps[:, :], ACT.Relu, bias=b1)\
                                .then_inc(hid_done, 1)
                        b.store_chunk(act, acc, i, k)
                b.all_stored(act)


def sheaf_table(nc, g, name, table, values):
    with Stage(nc, name) as s:
        t1 = s.sb("t1", [P, NT])
        dve_o, capped, root, ready, out_ = (s.sem(n) for n in ("dve", "capped", "root", "ready", "out"))
        with nc.Block() as block:
            @block.vector
            def _(dve):
                dve.tensor_scalar(t1[:, :], g.deg[:, :], 1e-5, None, ALU.max).then_inc(capped, 1)
                dve.tensor_copy(values[:, :, 0:FD], g.h[:, :, :])
                dve.wait_ge(root, 1)
                dve.reciprocal(values[:, :, FD], t1[:, :]).then_inc(ready, 1)

            @block.scalar
            def _(act):
                act.wait_ge(capped, 1)
                act.activation(t1[:, :], t1[:, :], ACT.Sqrt).then_inc(root, 1)

            @block.sync
            def _(sp):
                sp.wait_ge(ready, 1)
                sp.dma_start(by_node(table), values[:, :, :]).then_inc(out_, 16)
                sp.wait_ge(out_, 16)


def finish_sheaf(nc, g, name, agg, values):
    wide = [P, NT, FD]
    tables = [t for ts in g.by_src for t in ts]
    with Stage(nc, name) as s:
        parts = [s.sb(f"part{n}", wide) for n in range(len(tables))]
        in_ = [s.sem(f"in{n}") for n in range(len(tables))]
        dve_o = s.sem("dve")
        with nc.Block() as block:
            @block.sync
            def _(sp):
                for n, t in enumerate(tables):
                    sp.dma_start(parts[n][:, :, :], by_node(t[0:NP])).then_inc(in_[n], 16)

            @block.vector
            def _(dve):
                o = Order(dve, dve_o)
                v = agg[:, :, :]
                o.link(dve.tensor_tensor(v, v, g.has[:, :].unsqueeze(2).to_broadcast(wide), ALU.mult))
                for n in range(len(tables)):
                    dve.wait_ge(in_[n], 16)
                    o.link(dve.tensor_tensor(v, v, parts[n][:, :, :], ALU.add))
                o.link(dve.tensor_tensor(v, v, values[:, :, FD:].to_broadcast(wide), ALU.mult))
                o.link(dve.tensor_tensor(v, v, g.h[:, :, :], ALU.add))
                o.link(dve.tensor_scalar(v, v, 0.0, None, ALU.max))
                dve.tensor_tensor(g.x[:, :, :], g.x[:, :, :], v, ALU.add)


def sheaf_weights(nc, g, name, a, w1, w2, b1, b2):
    hid = P // 2
    with Stage(nc, name) as s:
        in_, cleared = s.sem("in"), s.sem("cleared")
        with nc.Block() as block:
            @block.vector
            def _(dve):
                dve.memset(w2[:, :], 0.0).then_inc(cleared, 1)

            @block.sync
            def _(sp):
                w1t, w2t = a.L2_gnn_W1.rearrange("h i -> i h"), a.L2_gnn_W2.rearrange("o h -> h o")
                b1c = a.L2_gnn_b1.unsqueeze(1)
                sp.wait_ge(cleared, 1)
                with nc.allow_non_contiguous_dma(reason="small weights, once"):
                    pairs = [(w1[:, 0:hid], w1t), (w1[0:FD, hid:], w1t[FD:, :]), (w1[FD:, hid:], w1t[0:FD, :]),
                             (w2[0:hid, 0:FD], w2t), (w2[hid:, FD:], w2t), (b1[0:hid, :], b1c), (b1[hid:, :], b1c),
                             (b2[:, 0:FD], a.L2_gnn_b2.partition_broadcast(P)),
                             (b2[:, FD:], a.L2_gnn_b2.partition_broadcast(P))]
                    for dst, src in pairs:
                        sp.dma_start(dst, src).then_inc(in_, 16)
                    sp.wait_ge(in_, 16 * len(pairs))


def relation_weights(nc, g, name, a, w, attr_w):
    M = R90 * (FD + 1)
    with Stage(nc, name) as s:
        comp_t, bases = s.sb("compt", [NB, R90]), s.sb("bases", [NB, FD, FD])
        mixed, ws, wa = s.sb("mixed", [R90, FD, FD]), s.sb("ws", [FD, FD]), s.sb("wa", [FD, 3])
        wa_wide, parts = s.sb("wawide", [FD, P]), s.sb("parts", [FD, 2])
        mixed_ps, parts_ps, attr_ps = s.ps("mixedp", [R90, FD * FD]), s.ps("partsp", [FD, 2]), s.ps("attrp", [P, FD])
        in_, mixed_ready, mixed_sb, out_, back, wide_ready, small, cp = (
            s.sem(n) for n in ("in", "mixed_ready", "mixed_sb", "out", "back", "wide_ready", "small", "cp"))
        w_view = w[:, 0:M].rearrange("i (r c) -> i r c", r=R90)
        flat = g.mixed_d
        with nc.Block() as block:
            @block.sync
            def _(sp):
                with nc.allow_non_contiguous_dma(reason="small weights, once"):
                    v = a.L3_gnn_weight.rearrange("b i o -> (b i) o").rearrange("(i b) o -> b i o", b=NB)
                    pairs = [(comp_t[:, :], a.L3_gnn_w_comp.rearrange("r b -> b r")), (bases[:, :, :], v),
                             (ws[:, :], a.L3_gnn_Ws), (wa[:, :], a.L3_gnn_Wa.rearrange("u (n o) -> o (u n)", n=3))]
                    for dst, src in pairs:
                        sp.dma_start(dst, src).then_inc(in_, 16)
                sp.wait_ge(mixed_sb, 1)
                sp.dma_start(flat.rearrange("(i r) o -> r i o", r=R90), mixed[:, :, :]).then_inc(out_, 16)
                sp.wait_ge(out_, 16)
                sp.dma_start(w_view[:, :, 0:FD], flat.rearrange("(r i) o -> i r o", i=FD)).then_inc(back, 16)
                sp.wait_ge(back, 16)

            @block.tensor
            def _(pe):
                pe.wait_ge(in_, 64)
                pe.matmul(mixed_ps[:, :], comp_t[:, :], bases[:, :, :].rearrange("b i o -> b (i o)"), start=True,
                          stop=True).then_inc(mixed_ready, 1)
                pe.matmul(parts_ps[:, 0:1], ws[:, :], wa[:, 0:1], start=True, stop=True)
                pe.matmul(parts_ps[:, 1:2], ws[:, :], wa[:, 2:3], start=True, stop=True)
                pe.wait_ge(wide_ready, 1)
                pe.matmul(attr_ps[:, :], wa_wide[:, :], ws[:, :], start=True, stop=True).then_inc(small, 1)

            @block.vector
            def _(dve):
                dve.wait_ge(in_, 64)
                dve.tensor_copy(wa_wide[:, :], wa[:, 1:2].to_broadcast([FD, P])).then_inc(wide_ready, 1)
                dve.wait_ge(mixed_ready, 1)
                dve.tensor_copy(mixed[:, :, :].rearrange("r i o -> r (i o)"), mixed_ps[:, :]).then_inc(mixed_sb, 1)
                dve.wait_ge(small, 1)
                dve.tensor_copy(attr_w, attr_ps[:, :])
                dve.tensor_copy(parts[:, :], parts_ps[:, :]).then_inc(cp, 1)
                dve.wait_ge(cp, 1)
                dve.tensor_copy(w[:, M:M + 1], parts[:, 1:2])
                dve.tensor_copy(w_view[:, :, FD], parts[:, 0:1].to_broadcast([FD, R90]))


def store_nodes(nc, name, table, values):
    with Stage(nc, name) as s:
        out_ = s.sem("out")
        with nc.Block() as block:
            @block.sync
            def _(sp):
                with nc.allow_non_contiguous_dma(reason="one word per node, once"):
                    sp.dma_start(by_node(table), values[:, :, :]).then_inc(out_, 16)
                    sp.wait_ge(out_, 16)


def typed_attention_pass(nc, g, name, table, expand, attr, attr_w, sums_d):
    with Stage(nc, name) as s:
        b = EdgeBuffers(s, g, FD + 1, g.idx90_d, [by_edge(g.keep_t), by_edge(expand), attr], FD)
        dst_part = [s.sb(f"dst{k}", [P, J]) for k in range(2)]
        weight = s.sb("weight", [P, J])
        dve_o = s.sem("dve")
        acc = by_edge(sums_d)
        with nc.Block() as block:
            @block.sync
            def _(sp):
                b.load(sp)

            @block.gpsimd
            def _(pool):
                b.gather(pool, g, table)

            @block.vector
            def _(dve):
                o = Order(dve, dve_o)
                dve.memset(dst_part[1][:, :], 0.0)
                o.link(dve.memset(b.sums[1][:, J - 1, :], 0.0))
                per = 10
                with dve.Fori(0, NCH // 2) as i:
                    o = Order(dve, dve_o, i * per + 1)
                    for k in range(2):
                        rows_, at = b.rows[k], b.extra[k][2]
                        b.wait_extra(dve, i, k)
                        o.step(scan_sum(dve, dst_part[k][:, :], b.keep[k], b.extra[k][1][:, :, 0],
                                        dst_part[1 - k][:, J - 1:J]))
                        o.link(dve.tensor_tensor(at[:, :, :], at[:, :, :],
                                                 attr_w.unsqueeze(1).to_broadcast([P, J, FD]), ALU.mult))
                        o.link(dve.tensor_reduce(weight[:, :], at[:, :, :], AX.X, ALU.add))
                        o.link(dve.tensor_tensor(weight[:, :], weight[:, :], dst_part[k][:, :], ALU.add))
                        b.wait_rows(dve, i, k)
                        part = rows_[:, :, FD:].rearrange("p j o -> p (j o)")
                        o.link(dve.tensor_tensor(weight[:, :], weight[:, :], part, ALU.add))
                        dve.tensor_tensor(rows_[:, :, 0:FD], rows_[:, :, 0:FD],
                                          weight[:, :].unsqueeze(2).to_broadcast([P, J, FD]), ALU.mult)\
                            .then_inc(b.used[k], 1)
                        dve.wait_ge(b.used[k], i + 1)
                        dve.wait_ge(b.stored[k], i * 16)
                        for c in range(FD):
                            last = scan_sum(dve, b.sums[k][:, :, c], b.keep[k], rows_[:, :, c],
                                            b.sums[1 - k][:, J - 1, c:c + 1])
                        last.then_inc(b.done[k], 1)
                        dve.wait_ge(b.done[k], i + 1)
                    assert o.n == per, o.n

            @block.scalar
            def _(act):
                with act.Fori(0, NCH // 2) as i:
                    for k in range(2):
                        b.store_chunk(act, acc, i, k)
                b.all_stored(act)


def finish_all(nc, g, name, agg, out):
    with Stage(nc, name) as s:
        dve_o, ready, out_ = s.sem("dve"), s.sem("ready"), s.sem("out")
        with nc.Block() as block:
            @block.vector
            def _(dve):
                v = agg[:, :, :]
                Order(dve, dve_o).link(dve.tensor_tensor(v, v, g.has[:, :].unsqueeze(2).to_broadcast([P, NT, FD]),
                                                         ALU.mult))
                dve.tensor_tensor(v, v, g.x[:, :, :], ALU.add).then_inc(ready, 1)

            @block.sync
            def _(sp):
                sp.wait_ge(ready, 1)
                sp.dma_start(by_node(out), agg[:, :, :]).then_inc(out_, 16)
                sp.wait_ge(out_, 16)


class Arrays:
    pass


def build(nc, a, out):
    g = Arrays()
    dram = lambda name, shape, dt=F32: nc.dram_tensor(name, shape, dt, kind="Internal").ap()
    with Stage(nc, "whole") as w:
        g.gate = w.sem("gate")
        sb = w.sb
        g.x, g.h = sb("x", [P, NT, FD]), sb("h", [P, NT, FD])
        g.ident, g.strict, g.count_f = sb("ident", [P, P]), sb("strict", [P, P]), sb("countf", [P, P])
        g.node_f, g.deg, g.has = sb("nodef", [P, NT]), sb("deg", [P, NT]), sb("has", [P, NT])
        g.last_row, g.start_row = sb("lastrow", [P, NT], I32), sb("startrow", [P, NT], I32)
        g.first_row, g.dst_first, g.lane_i = (sb(n, [P, 1], I32) for n in ("firstrow", "dstfirst", "lanei"))
        g.mend_from, g.mend_to = sb("mendfrom", [P, 1], I32), sb("mendto", [P, 1], I32)
        g.first_f, g.lane_f, g.joined = sb("firstf", [P, 1]), sb("lanef", [P, 1]), sb("joined", [1, P])
        g.keep_t, g.dst_t, g.src_t, g.type8_t, g.norm_t = (
            dram(n, [EROWS, 1]) for n in ("keep_d", "dst_d", "srcf_d", "type8_d", "norm_d"))
        flat = lambda t: t.rearrange("(p j) o -> p (j o)", p=P)
        g.keep_d, g.dst_d, g.src_fd, g.type8_d = (flat(t) for t in (g.keep_t, g.dst_t, g.src_t, g.type8_t))
        g.idx8_d, g.idx90_d = dram("idx8_d", [P, EP], I32), dram("idx90_d", [P, EP], I32)
        g.src_id = a.src
        g.total_d = dram("total_d", [NP + 1, 1])
        g.carry_d = dram("carry_d", [P, 102])
        expand = {n: dram(f"expand{n}", [XROWS, k]) for n, k in
                  (("att1", 3), ("att2", 1), ("rel", R8), ("sheaf", FD + 1), ("relatt", 1))}
        g.by_src = [[dram(f"bysrc{k}{r}", [NP + P, FD]) for r in range(NSUM)] for k in range(2)]
        g.sums = {n: dram(f"sums{n}", [EROWS + P, k]) for n, k in
                  (("att1", 102), ("att2", 34), ("count", R8), ("rel", FD), ("sheaf", FD), ("relatt", FD))}
        g.to_zero = [t[EROWS:EROWS + P] for t in g.sums.values()] + list(expand.values()) + [t for ts in g.by_src for t in ts]

        with Stage(nc, "sources") as hs:
            g.src_lo, g.src_hi = hs.sb("srclo", [P, EP], I32), hs.sb("srchi", [P, EP], I32)
            set_up(nc, a, g)
            source_degrees(nc, g)
        node_ranges(nc, g)

        with Stage(nc, "gat") as s:
            h1, c1, h2, c2 = 3, 32, 1, 32
            w1, w2, wf = s.sb("w1", [FD, h1 * c1 + 2 * h1]), s.sb("w2", [h1 * c1, c2 + 2]), s.sb("wf", [c2, FD])
            b1, b2, bf = s.sb("b1", [P, h1 * c1]), s.sb("b2", [P, c2]), s.sb("bf", [P, FD])
            table1, table2 = dram("att1_t", [NP, 102]), dram("att2_t", [NP, 34])
            sums1, sums2 = g.sums["att1"], g.sums["att2"]
            load_constants(nc, "gat_in", [(b1[:, :], a.L0_gnn_b1.partition_broadcast(P)),
                                          (b2[:, :], a.L0_gnn_b2.partition_broadcast(P)),
                                          (bf[:, :], a.L0_gnn_bf.partition_broadcast(P)), (wf[:, :], a.L0_gnn_Wf)])
            attention_weights(nc, g, "gat_w1", a.L0_gnn_W1, a.L0_gnn_a_src1, a.L0_gnn_a_dst1, w1, FD, h1, c1)
            attention_weights(nc, g, "gat_w2", a.L0_gnn_W2, a.L0_gnn_a_src2, a.L0_gnn_a_dst2, w2, h1 * c1, h2, c2)
            layer_norm(nc, g, "ln1")
            with Stage(nc, "gat1") as t:
                parts = t.sb("parts", [P, NT, h1])
                project(nc, g, "gat1_p", g.h, FD, w1, 102, table1, (parts, 99))
                spread(nc, g, "gat1_s", parts, table1, expand["att1"], h1)
            attention_pass(nc, g, "gat1_e", h1, c1, table1, expand["att1"], sums1)
            carry_over(nc, g, "gat1_c", sums1, 102, h1)
            with Stage(nc, "gat1n") as t:
                big, parts = t.sb("big", [P, NT, 102]), t.sb("parts", [P, NT, 1])
                gather_to(nc, g, "gat1_g", sums1, g.last_row, 102, big)
                finish_attention(nc, g, "gat1_f", big, table1, b1[:, :], h1, c1)
                project(nc, g, "gat2_p", big, 96, w2, 34, table2, (parts, 33))
                spread(nc, g, "gat2_s", parts, table2, expand["att2"], h2)
            attention_pass(nc, g, "gat2_e", h2, c2, table2, expand["att2"], sums2)
            carry_over(nc, g, "gat2_c", sums2, 34, h2)
            with Stage(nc, "gat2n") as t:
                big = t.sb("big", [P, NT, 34])
                gather_to(nc, g, "gat2_g", sums2, g.last_row, 34, big)
                finish_attention(nc, g, "gat2_f", big, table2, b2[:, :], h2, c2)
                project(nc, g, "gatf_p", big, c2, wf, FD, None, (g.h, 0))
                add_rows(nc, g, "gatf_a", g.h, bf[:, :])

        with Stage(nc, "rgcn") as s:
            wide = R8 * FD + FD
            w = [s.sb(f"w{n}", [FD, wide]) for n in range(2)]
            bias = [s.sb(f"b{n}", [P, FD]) for n in range(2)]
            counts_d = dram("counts_t", [NP, R8])
            tables = [dram(f"rel_t{n}", [NP, R8 * FD]) for n in range(2)]
            load_constants(nc, "rgcn_in", [
                x for n, (wr, root, b) in enumerate(((a.L1_gnn_W1, a.L1_gnn_root1, a.L1_gnn_b1),
                                                     (a.L1_gnn_W2, a.L1_gnn_root2, a.L1_gnn_b2)))
                for x in ((w[n][:, 0:R8 * FD].rearrange("i (r o) -> i r o", r=R8), wr.rearrange("r i o -> i r o")),
                          (w[n][:, R8 * FD:], root), (bias[n][:, :], b.partition_broadcast(P)))])
            count_pass(nc, g, "count_e", g.sums["count"])
            carry_over(nc, g, "count_c", g.sums["count"], R8)
            with Stage(nc, "counts") as t:
                counts = t.sb("counts", [P, NT, R8])
                gather_to(nc, g, "count_g", g.sums["count"], g.last_row, R8, counts)
                reciprocal_counts(nc, g, "count_r", counts, counts_d)
                spread(nc, g, "count_s", counts, counts_d, expand["rel"], R8)
            layer_norm(nc, g, "ln2")
            for n in range(2):
                with Stage(nc, f"rgcn{n}") as t:
                    root_part, agg = t.sb("root", [P, NT, FD]), t.sb("agg", [P, NT, FD])
                    project(nc, g, f"rgcn{n}_p", g.h, FD, w[n], wide, tables[n], (root_part, R8 * FD))
                    relation_pass(nc, g, f"rgcn{n}_e", tables[n].rearrange("n (r o) -> (n r) o", r=R8), g.idx8_d,
                                  g.sums["rel"], expand["rel"] if n == 0 else None)
                    carry_over(nc, g, f"rgcn{n}_c", g.sums["rel"], FD)
                    gather_to(nc, g, f"rgcn{n}_g", g.sums["rel"], g.last_row, FD, agg)
                    finish_relation(nc, g, f"rgcn{n}_f", agg, root_part, bias[n][:, :], g.h, n == 1)

        with Stage(nc, "sheaf") as s:
            w1, w2, b1, b2 = s.sb("w1", [2 * FD, P]), s.sb("w2", [P, 2 * FD]), s.sb("b1", [P, 1]), s.sb("b2", [P, 2 * FD])
            table = dram("sheaf_t", [NP, FD + 1])
            values = s.sb("values", [P, NT, FD + 1])
            sheaf_weights(nc, g, "sheaf_w", a, w1, w2, b1, b2)
            layer_norm(nc, g, "ln3")
            sheaf_table(nc, g, "sheaf_n", table, values)
            spread(nc, g, "sheaf_s", values, table, expand["sheaf"], FD + 1)
            sheaf_pass(nc, g, "sheaf_e", w1[:, :], w2[:, :], b1[:, :], b2[:, :], table, expand["sheaf"],
                       g.sums["sheaf"])
            carry_over(nc, g, "sheaf_c", g.sums["sheaf"], FD)
            with Stage(nc, "sheafn") as t:
                agg = t.sb("agg", [P, NT, FD])
                gather_to(nc, g, "sheaf_g", g.sums["sheaf"], g.last_row, FD, agg)
                finish_sheaf(nc, g, "sheaf_f", agg, values)

        with Stage(nc, "typed") as s:
            M = R90 * (FD + 1)
            w, attr_w = s.sb("w", [FD, M + 1]), s.sb("attrw", [P, FD])
            g.mixed_d = dram("mixed_d", [FD * R90, FD])
            table, part_d = dram("typed_t", [NP, M]), dram("typed_dst", [NP, 1])
            relation_weights(nc, g, "typed_w", a, w, attr_w[:, :])
            layer_norm(nc, g, "ln4")
            with Stage(nc, "typedp") as t:
                parts = t.sb("parts", [P, NT, 1])
                project(nc, g, "typed_p", g.h, FD, w, M + 1, table, (parts, M))
                store_nodes(nc, "typed_d", part_d, parts)
                spread(nc, g, "typed_s", parts, part_d, expand["relatt"], 1)
            typed_attention_pass(nc, g, "typed_e", table.rearrange("n (r c) -> (n r) c", c=FD + 1),
                                 expand["relatt"], a.attr, attr_w[:, :], g.sums["relatt"])
            carry_over(nc, g, "typed_c", g.sums["relatt"], FD)
            with Stage(nc, "typedn") as t:
                agg = t.sb("agg", [P, NT, FD])
                gather_to(nc, g, "typed_g", g.sums["relatt"], g.last_row, FD, agg)
                finish_all(nc, g, "typed_f", agg, out)


def add_rows(nc, g, name, rows_, bias):
    with Stage(nc, name) as s:
        dve_o = s.sem("dve")
        with nc.Block() as block:
            @block.vector
            def _(dve):
                o = Order(dve, dve_o)
                x = g.x[:, :, :]
                o.link(dve.tensor_tensor(x, x, rows_[:, :, :], ALU.add))
                dve.tensor_tensor(x, x, bias.unsqueeze(1).to_broadcast([P, NT, FD]), ALU.add)



_WEIGHTS = [f"L0_gnn_{n}" for n in ("W1", "a_src1", "a_dst1", "b1", "W2", "a_src2", "a_dst2", "b2", "Wf", "bf")] + \
           [f"L1_gnn_{n}" for n in ("W1", "root1", "b1", "W2", "root2", "b2")] + \
           [f"L2_gnn_{n}" for n in ("W1", "b1", "W2", "b2")] + \
           [f"L3_gnn_{n}" for n in ("Ws", "Wa", "weight", "w_comp")]


def kernel(**inputs):
    import types

    import concourse.bacc as bacc
    from concourse.bass_utils import run_bass_kernel_spmd

    extra = P * EP - E

    def by_partition(v, fill):
        return np.pad(v, (0, extra), constant_values=fill).reshape(P, EP)

    given = {n: np.asarray(inputs[n]) for n in ("x", "src", "dst", "edge_attr_16", "edge_type_8", "edge_type_90",
                                                *_WEIGHTS)}
    arrays = {
        "x": np.pad(given["x"], ((0, NP - N), (0, 0))),
        "src": by_partition(given["src"], N),
        "dst": by_partition(given["dst"], N),
        "type8": by_partition(given["edge_type_8"], 0),
        "type90": by_partition(given["edge_type_90"], 0),
        "attr": np.pad(given["edge_attr_16"], ((0, extra), (0, 0))).reshape(P, EP, FD),
        **{n: given[n] for n in _WEIGHTS},
    }
    nc = bacc.Bacc("TRN2", target_bir_lowering=False, num_devices=1)
    a = types.SimpleNamespace(**{
        n: nc.dram_tensor(f"in_{n}", list(v.shape), mybir.dt.from_np(v.dtype), kind="ExternalInput").ap()
        for n, v in arrays.items()})
    out = nc.dram_tensor("out", [NP, FD], F32, kind="ExternalOutput").ap()
    build(nc, a, out)
    r = run_bass_kernel_spmd(nc, [{f"in_{n}": np.ascontiguousarray(v) for n, v in arrays.items()}], core_ids=[0])
    return r.results[0]["out"][:N]
```

```python
from contextlib import ExitStack

import numpy as np

import concourse.bass as bass
from concourse import mybir

F32 = mybir.dt.float32
BF16 = mybir.dt.bfloat16
I32 = mybir.dt.int32
ALU = mybir.AluOpType
ACT = mybir.ActivationFunctionType
AX = mybir.AxisListType

P = 128
N, FD = 12500, 16
E = 412500
NT = -(-N // P)
NP = NT * P
J = 52
EP = 2 * J * -(-E // (P * 2 * J))
NCH = EP // J
EROWS = P * EP
XROWS = EROWS + NP
NSUM = 4
GT = 7
NG = NT // GT
R8, R90, NB = 8, 90, 30
BIG = 1.0e38
SLOPE = 0.2
SELU_SCALE, SELU_ALPHA = 1.0507009873554805, 1.6732632423543772
CSPLIT = 8
CROW = EP // CSPLIT


class Stage:

    def __init__(self, nc, name):
        self.nc, self.name, self.stack, self.sems = nc, name, ExitStack(), []
        self.credits = []

    def __enter__(self):
        return self

    def sb(self, name, shape, dt=F32):
        return self.stack.enter_context(self.nc.sbuf_tensor(f"{self.name}_{name}", shape, dt))

    def ps(self, name, shape):
        return self.stack.enter_context(self.nc.psum_tensor(f"{self.name}_{name}", shape, F32))

    def sem(self, name, credit=0):
        s = self.nc.alloc_semaphore(f"{self.name}_{name}")
        self.sems.append(s)
        if credit:
            self.credits.append((s, credit))
        return s

    def grant(self, eng):
        for s, credit in self.credits:
            eng.sem_inc(s, credit)

    def __exit__(self, *a):
        self.stack.close()
        if a[0] is None:
            self.nc.clear_and_free_semaphores(self.sems)
            self.nc.all_engine_barrier()


class Order:

    def __init__(self, eng, sem, base=0):
        self.eng, self.sem, self.base, self.n = eng, sem, base, 0

    def step(self, ins):
        self.n += 1
        ins.then_inc(self.sem, 1)

    def link(self, ins):
        self.step(ins)
        self.eng.wait_ge(self.sem, self.base + self.n)


def by_edge(table):
    return table[0:EROWS].rearrange("(p j) w -> p j w", p=P)


def by_node(table):
    return table.rearrange("(t p) w -> p t w", p=P)


def chunk(view, i, k):
    return view[:, bass.ds((i * 2 + k) * J, J)]


def rows(ap):
    return bass.IndirectOffsetOnAxis(ap=ap, axis=0)



def set_up(nc, a, g):
    with Stage(nc, "setup") as s:
        src_i, dst_i, t8_i, t90_i = (s.sb(n, [P, EP], I32) for n in ("src", "dst", "t8", "t90"))
        idx8, idx90 = s.sb("idx8", [P, EP], I32), s.sb("idx90", [P, EP], I32)
        src_f, dst_f, t8_f, keep = (s.sb(n, [P, EP]) for n in ("srcf", "dstf", "t8f", "keep"))
        lane, tile = s.sb("lane", [P, EP]), s.sb("tile", [P, EP])
        zero = s.sb("zero", [P, XROWS // P])
        iota_n, iota_j, iota_p = s.sb("ion", [P, NT], I32), s.sb("ioj", [P, P], I32), s.sb("iop", [P, 1], I32)
        loaded = [s.sem(f"loaded{n}") for n in range(5)]
        stored, iotas, zeroed, zero_ready, ready, dve_o, pool_o = (
            s.sem(n) for n in ("stored", "iotas", "zeroed", "zero_ready", "ready", "dve", "pool"))
        n_zero = len(g.to_zero)
        with nc.Block() as block:
            @block.sync
            def _(sp):
                for n, (dst, src) in enumerate(((dst_i, a.dst), (src_i, a.src), (t8_i, a.type8), (t90_i, a.type90))):
                    sp.dma_start(dst[:, :], src).then_inc(loaded[n], 16)
                sp.dma_start(g.x[:, :, :], by_node(a.x)).then_inc(loaded[4], 16)
                sp.wait_ge(zero_ready, 1)
                for table in g.to_zero:
                    n_rows, w = table.shape
                    flat = table.rearrange("(p m) w -> p (m w)", p=P)
                    m = n_rows // P
                    sp.dma_start(flat.rearrange("p (w m) -> p w m", w=w),
                                 zero[:, 0:m].unsqueeze(1).to_broadcast([P, w, m])).then_inc(zeroed, 16)
                sp.wait_ge(zeroed, 16 * n_zero)
                sp.wait_ge(loaded[4], 16)

            @block.gpsimd
            def _(pool):
                pool.iota(iota_n[:, :], pattern=[[P, NT]], base=0, channel_multiplier=1).then_inc(iotas, 1)
                pool.iota(iota_j[:, :], pattern=[[1, P]], base=0, channel_multiplier=0).then_inc(iotas, 1)
                pool.iota(iota_p[:, :], pattern=[[0, 1]], base=0, channel_multiplier=EP).then_inc(iotas, 1)
                pool.iota(g.first_row[:, :], pattern=[[0, 1]], base=0, channel_multiplier=EP).then_inc(iotas, 1)
                pool.iota(g.lane_i[:, :], pattern=[[0, 1]], base=0, channel_multiplier=1).then_inc(iotas, 1)
                pool.memset(g.ident[:, :], 0.0).then_inc(pool_o, 1)
                pool.wait_ge(pool_o, 1)
                pool.affine_select(out=g.ident[:, :], in_=g.ident[:, :], compare_op=ALU.not_equal, fill=1.0, base=0,
                                   pattern=[[-1, P]], channel_multiplier=1).then_inc(pool_o, 1)
                pool.memset(g.strict[:, :], 1.0).then_inc(pool_o, 1)
                pool.wait_ge(pool_o, 3)
                pool.affine_select(out=g.strict[:, :], in_=g.strict[:, :], compare_op=ALU.is_gt, fill=0.0, base=0,
                                   pattern=[[-1, P]], channel_multiplier=1).then_inc(pool_o, 1)

            @block.vector
            def _(dve):
                o = Order(dve, dve_o)
                dve.memset(zero[:, :], 0.0).then_inc(zero_ready, 1)
                dve.memset(keep[:, 0:1], 0.0)
                dve.wait_ge(iotas, 5)
                dve.tensor_copy(g.node_f[:, :], iota_n[:, :])
                dve.tensor_copy(g.count_f[:, :], iota_j[:, :])
                dve.tensor_copy(g.lane_f[:, :], g.lane_i[:, :])
                o.step(dve.tensor_copy(g.first_f[:, :], iota_p[:, :]))
                dve.wait_ge(loaded[0], 16)
                o.link(dve.tensor_copy(dst_f[:, :], dst_i[:, :]))
                dve.tensor_tensor(keep[:, 1:EP], dst_f[:, 1:EP], dst_f[:, 0:EP - 1], ALU.is_equal)
                dve.wait_ge(loaded[1], 16)
                o.step(dve.tensor_copy(src_f[:, :], src_i[:, :]))
                dve.tensor_scalar(idx8[:, :], src_i[:, :], P - 1, None, ALU.bitwise_and)
                o.link(dve.tensor_scalar(idx90[:, :], src_i[:, :], 7, None, ALU.logical_shift_right))
                dve.tensor_copy(lane[:, :], idx8[:, :])
                o.link(dve.tensor_copy(tile[:, :], idx90[:, :]))
                dve.wait_ge(loaded[2], 16)
                dve.tensor_copy(t8_f[:, :], t8_i[:, :])
                dve.scalar_tensor_tensor(idx8[:, :], src_i[:, :], float(R8), t8_i[:, :], ALU.mult, ALU.add)
                dve.wait_ge(loaded[3], 16)
                dve.scalar_tensor_tensor(idx90[:, :], src_i[:, :], float(R90), t90_i[:, :], ALU.mult,
                                         ALU.add).then_inc(ready, 1)

            @block.scalar
            def _(act):
                act.wait_ge(ready, 1)
                pairs = ((g.keep_d, keep), (g.dst_d, dst_f), (g.src_fd, src_f), (g.type8_d, t8_f), (g.lane_d, lane),
                         (g.tile_d, tile), (g.idx8_d, idx8),
                         (g.idx90_d, idx90))
                for dram, values in pairs:
                    act.dma_start(dram, values[:, :]).then_inc(stored, 16)
                act.wait_ge(stored, 16 * len(pairs))


def gather_by_node(nc, g, name, table, index, width, consume, per_turn):
    with Stage(nc, name) as s:
        got_rows = [s.sb(f"rows{k}", [P, GT, width]) for k in range(2)]
        row_g = [s.sb(f"index{k}", [P, GT], I32) for k in range(2)]
        dve_o = s.sem("dve")
        staged = [s.sem(f"staged{k}") for k in range(2)]
        got = [s.sem(f"got{k}") for k in range(2)]
        with nc.Block() as block:
            @block.gpsimd
            def _(pool):
                with pool.Fori(0, NG // 2) as i:
                    for k in range(2):
                        pool.wait_ge(staged[k], i + 1)
                        pool.sem_inc(g.gate, 1)
                        for c in range(GT):
                            pool.indirect_dma_start(got_rows[k][:, c, :], None, table, rows(row_g[k][:, c:c + 1]))\
                                .then_inc(got[k], 16)

            @block.vector
            def _(dve):
                with dve.Fori(0, NG // 2) as i:
                    o = Order(dve, dve_o, i * per_turn)
                    for k in range(2):
                        dve.tensor_copy(row_g[k][:, :], index[:, bass.ds((i * 2 + k) * GT, GT)])\
                            .then_inc(staged[k], 1)
                    for k in range(2):
                        dve.wait_ge(got[k], i * (16 * GT) + 16 * GT)
                        consume(dve, o, i * 2 + k, got_rows[k])
                    assert o.n == per_turn, (name, o.n)


def gather_to(nc, g, name, table, index, width, into):
    def copy(dve, o, group, rows_):
        o.link(dve.tensor_copy(into[:, bass.ds(group * GT, GT), 0:width], rows_[:, :, :]))
    gather_by_node(nc, g, name, table, index, width, copy, 2)


def node_ranges(nc, g):
    n_rows = P * CSPLIT
    dst_rows = g.dst_d.rearrange("p (k c) -> (p k) c", k=CSPLIT)
    with Stage(nc, "ranges") as r:
        cnt, row_f, row_i = r.sb("cnt", [P, NT]), r.sb("rowf", [P, NT]), r.sb("rowi", [P, NT], I32)
        node_g, cnt_g, seen = r.sb("node", [P, GT]), r.sb("cntg", [P, GT]), r.sb("seen", [P, n_rows])

        with Stage(nc, "heads") as s:
            heads = s.sb("heads", [P, n_rows])
            in_, dve_o = s.sem("in"), s.sem("dve")
            with nc.Block() as block:
                @block.sync
                def _(sp):
                    with nc.allow_non_contiguous_dma(reason="one word of each row, once"):
                        sp.dma_start(heads[:, :], dst_rows[:, 0:1].rearrange("r c -> c r").to_broadcast([P, n_rows]))\
                          .then_inc(in_, 16)

                @block.vector
                def _(dve):
                    dve.wait_ge(in_, 16)
                    with dve.Fori(0, NG) as i:
                        o = Order(dve, dve_o, i * (GT + 2))
                        o.link(dve.tensor_copy(node_g[:, :], g.node_f[:, bass.ds(i * GT, GT)]))
                        for c in range(GT):
                            o.link(dve.tensor_scalar(seen[:, :], heads[:, :], node_g[:, c:c + 1], None, ALU.is_le,
                                                     ALU.add, accum_out=cnt_g[:, c:c + 1]))
                        o.link(dve.tensor_copy(cnt[:, bass.ds(i * GT, GT)], cnt_g[:, :]))
                    o = Order(dve, dve_o, NG * (GT + 2))
                    o.link(dve.tensor_scalar(row_f[:, :], cnt[:, :], -1.0, 0.0, ALU.add, ALU.max))
                    dve.tensor_copy(row_i[:, :], row_f[:, :])

        def count(dve, o, group, rows_):
            o.link(dve.tensor_copy(node_g[:, :], g.node_f[:, bass.ds(group * GT, GT)]))
            for c in range(GT):
                o.link(dve.tensor_scalar(seen[:, 0:CROW], rows_[:, c, :], node_g[:, c:c + 1], None, ALU.is_le,
                                         ALU.add, accum_out=cnt_g[:, c:c + 1]))
            o.link(dve.tensor_copy(cnt[:, bass.ds(group * GT, GT)], cnt_g[:, :]))
        gather_by_node(nc, g, "count", dst_rows, row_i, CROW, count, 2 * (GT + 2))

        with Stage(nc, "limits") as s:
            total, before, t = s.sb("total", [P, NT]), s.sb("before", [P, NT]), s.sb("t", [P, NT])
            zero = s.sb("zero", [1, 1])
            d_first, d_prev, d_row = s.sb("dfirst", [P, 1]), s.sb("dprev", [P, 1]), s.sb("drow", [1, P + 1])
            after_first, t_first, fix, ins_ = (s.sb("af", [P, 1], I32), s.sb("tf", [P, 1]), s.sb("fix", [P, 1]),
                                               s.sb("ins", [P, 1]))
            dump_f, dump_n, t1 = s.sb("dump", [P, 1]), s.sb("dumpn", [P, NT]), s.sb("t1", [P, 1])
            dve_o, cleared, ends_in, totalled, stored, before_in, asked, first_total = (
                s.sem(n) for n in ("dve", "cleared", "ends_in", "totalled", "stored", "before_in", "asked",
                                   "first_total"))
            with nc.Block() as block:
                @block.sync
                def _(sp):
                    with nc.allow_non_contiguous_dma(reason="one word per partition or node, once"):
                        sp.wait_ge(cleared, 1)
                        sp.dma_start(d_first[:, :], g.dst_d[:, 0:1]).then_inc(ends_in, 16)
                        sp.dma_start(d_prev[1:P, :], g.dst_d[0:P - 1, EP - 1:EP]).then_inc(ends_in, 16)
                        sp.dma_start(d_row[:, 1:P + 1], g.dst_d[:, EP - 1:EP].rearrange("p o -> o p"))\
                          .then_inc(ends_in, 16)
                        sp.wait_ge(totalled, 1)
                        sp.dma_start(g.total_d[1:NP + 1].rearrange("(t p) o -> p (t o)", p=P), total[:, :])\
                          .then_inc(stored, 16)
                        sp.dma_start(g.total_d[0:1], zero[:, :]).then_inc(stored, 16)
                        sp.wait_ge(stored, 32)
                        sp.dma_start(before[:, :], g.total_d[0:NP].rearrange("(t p) o -> p (t o)", p=P))\
                          .then_inc(before_in, 16)

                @block.gpsimd
                def _(pool):
                    pool.wait_ge(asked, 1)
                    pool.wait_ge(stored, 32)
                    pool.sem_inc(g.gate, 1)
                    pool.indirect_dma_start(t_first[:, :], None, g.total_d, rows(after_first[:, :]))\
                        .then_inc(first_total, 16)

                @block.vector
                def _(dve):
                    o = Order(dve, dve_o)
                    dve.memset(zero[:, :], 0.0)
                    dve.memset(d_row[:, 0:1], -1.0)
                    dve.memset(d_prev[:, :], -1.0).then_inc(cleared, 1)
                    o.link(dve.scalar_tensor_tensor(total[:, :], row_f[:, :], float(CROW), cnt[:, :], ALU.mult,
                                                    ALU.add))
                    dve.tensor_copy(t[:, :], total[:, :]).then_inc(totalled, 1)
                    dve.wait_ge(ends_in, 48)
                    o.link(dve.tensor_scalar(t1[:, :], d_first[:, :], 1.0, None, ALU.add))
                    dve.tensor_copy(after_first[:, :], t1[:, :]).then_inc(asked, 1)
                    dve.tensor_copy(g.dst_first[:, :], d_first[:, :])
                    dve.tensor_tensor(g.joined[:, :], d_row[:, 1:P + 1], d_row[:, 0:P], ALU.is_equal)
                    o.link(dve.tensor_scalar(t[:, :], total[:, :], -1.0, 0.0, ALU.add, ALU.max))
                    dve.tensor_copy(g.last_row[:, :], t[:, :])
                    dve.wait_ge(before_in, 16)
                    o.link(dve.tensor_tensor(g.has[:, :], total[:, :], before[:, :], ALU.is_gt))
                    o.link(dve.tensor_tensor(g.deg[:, :], total[:, :], before[:, :], ALU.subtract))
                    o.link(dve.tensor_scalar(dump_f[:, :], g.lane_f[:, :], float(EROWS), None, ALU.add))
                    o.link(dve.tensor_scalar(dump_n[:, :], g.node_f[:, :], float(EROWS), None, ALU.add))
                    o.link(dve.tensor_tensor(before[:, :], before[:, :], dump_n[:, :], ALU.subtract))
                    o.link(dve.tensor_tensor(before[:, :], before[:, :], g.has[:, :], ALU.mult))
                    o.link(dve.tensor_tensor(before[:, :], before[:, :], dump_n[:, :], ALU.add))
                    dve.tensor_copy(g.start_row[:, :], before[:, :])
                    dve.wait_ge(first_total, 16)
                    o.link(dve.tensor_tensor(fix[:, :], d_first[:, :], d_prev[:, :], ALU.is_equal))
                    o.link(dve.tensor_scalar(t1[:, :], g.first_f[:, :], float(EP), None, ALU.add))
                    o.link(dve.tensor_tensor(ins_[:, :], t_first[:, :], t1[:, :], ALU.is_le))
                    o.link(dve.tensor_tensor(fix[:, :], fix[:, :], ins_[:, :], ALU.mult))
                    for base, row in ((g.first_f, g.mend_from), (dump_f, g.mend_to)):
                        o.link(dve.scalar_tensor_tensor(t1[:, :], t_first[:, :], -1.0, base[:, :], ALU.add,
                                                        ALU.subtract))
                        o.link(dve.tensor_tensor(t1[:, :], t1[:, :], fix[:, :], ALU.mult))
                        o.link(dve.tensor_tensor(t1[:, :], t1[:, :], base[:, :], ALU.add))
                        o.link(dve.tensor_copy(row[:, :], t1[:, :]))



def project(nc, g, name, x, width, weights, cols, table=None, keep=None):
    most = -(-cols // -(-cols // 512))
    parts = [(c, min(most, cols - c)) for c in range(0, cols, most)]
    width_t = table.shape[1] if table is not None else 0
    with Stage(nc, name) as s:
        rows_in = [s.sb(f"x{k}", [P, width]) for k in range(2)]
        turned = [s.sb(f"xt{k}", [width, P]) for k in range(2)]
        rows_out = [s.sb(f"y{k}", [P, cols]) for k in range(2)]
        xt_ps = [s.ps(f"xtp{k}", [P, 512]) for k in range(2)]
        y_ps = [[s.ps(f"yp{k}{n}", [P, 512]) for n in range(len(parts))] for k in range(2)]
        staged, turned_ps, turned_sb, product, copied, stored = (
            [s.sem(f"{n}{k}", c) for k in range(2)] for n, c in
            (("staged", 0), ("tps", 1), ("tsb", 1), ("product", 1), ("copied", 1), ("stored", 16)))
        view = by_node(table) if table is not None else None
        with nc.Block() as block:
            @block.vector
            def _(dve):
                with dve.Fori(0, NT // 2) as i:
                    for k in range(2):
                        t = i * 2 + k
                        dve.wait_ge(turned_ps[k], i + 1)
                        dve.tensor_copy(rows_in[k][:, :], x[:, bass.ds(t, 1), 0:width].rearrange("p o w -> p (o w)"))\
                            .then_inc(staged[k], 1)
                    for k in range(2):
                        t = i * 2 + k
                        dve.wait_ge(product[k], i + 2)
                        dve.wait_ge(stored[k], i * 16 + 16)
                        for n, (c, w) in enumerate(parts):
                            last = dve.tensor_copy(rows_out[k][:, c:c + w], y_ps[k][n][:, 0:w])
                        if keep is not None:
                            into, c0 = keep
                            kw = into.shape[2]
                            c = max(n for n, (c, _) in enumerate(parts) if c <= c0)
                            off = c0 - parts[c][0]
                            last = dve.tensor_copy(into[:, bass.ds(t, 1), :].rearrange("p o w -> p (o w)"),
                                                   y_ps[k][c][:, off:off + kw])
                        last.then_inc(copied[k], 1)

            @block.tensor
            def _(pe):
                with pe.Fori(0, NT // 2) as i:
                    for k in range(2):
                        pe.wait_ge(staged[k], i + 1)
                        pe.wait_ge(turned_sb[k], i + 1)
                        pe.transpose(xt_ps[k][0:width, 0:P], rows_in[k][:, :], g.ident[:, :]).then_inc(turned_ps[k], 1)
                        pe.wait_ge(turned_sb[k], i + 2)
                        pe.wait_ge(copied[k], i + 1)
                        for n, (c, w) in enumerate(parts):
                            last = pe.matmul(y_ps[k][n][:, 0:w], turned[k][:, :], weights[0:width, c:c + w],
                                             start=True, stop=True)
                        last.then_inc(product[k], 1)

            @block.scalar
            def _(act):
                with act.Fori(0, NT // 2) as i:
                    for k in range(2):
                        act.wait_ge(turned_ps[k], i + 2)
                        act.wait_ge(product[k], i + 1)
                        act.copy(turned[k][:, :], xt_ps[k][0:width, 0:P]).then_inc(turned_sb[k], 1)

            @block.sync
            def _(sp):
                s.grant(sp)
                with sp.Fori(0, NT // 2) as i:
                    for k in range(2):
                        sp.wait_ge(copied[k], i + 2)
                        if view is None:
                            sp.sem_inc(stored[k], 16)
                        else:
                            sp.dma_start(view[:, bass.ds(i * 2 + k, 1), :].rearrange("p o w -> p (o w)"),
                                         rows_out[k][:, 0:width_t]).then_inc(stored[k], 16)
                for k in range(2):
                    sp.wait_ge(stored[k], 16 * (NT // 2) + 16)


def spread(nc, g, name, values, node_table, expand, width):
    w_t = node_table.shape[1]
    with Stage(nc, name) as s:
        vals = [s.sb(f"v{k}", [P, GT, width]) for k in range(2)]
        row_g = [s.sb(f"row{k}", [P, GT], I32) for k in range(2)]
        first = s.sb("first", [P, w_t])
        first_v = s.sb("firstv", [P, width])
        got, ready, put = s.sem("got"), s.sem("ready"), s.sem("put")
        staged = [s.sem(f"staged{k}") for k in range(2)]
        out = [s.sem(f"out{k}") for k in range(2)]
        with nc.Block() as block:
            @block.vector
            def _(dve):
                def turn(i, first):
                    for k in range(2):
                        if not first:
                            dve.wait_ge(out[k], i * (16 * GT))
                        grp = bass.ds((i * 2 + k) * GT, GT)
                        dve.tensor_copy(row_g[k][:, :], g.start_row[:, grp])
                        dve.tensor_copy(vals[k][:, :, :], values[:, grp, :]).then_inc(staged[k], 1)
                turn(0, True)
                with dve.Fori(1, NG // 2) as i:
                    turn(i, False)
                dve.wait_ge(got, 16)
                dve.tensor_copy(first_v[:, :], first[:, w_t - width:w_t]).then_inc(ready, 1)

            @block.gpsimd
            def _(pool):
                pool.indirect_dma_start(first[:, :], None, node_table, rows(g.dst_first[:, :])).then_inc(got, 16)
                with pool.Fori(0, NG // 2) as i:
                    for k in range(2):
                        pool.wait_ge(staged[k], i + 1)
                        pool.sem_inc(g.gate, 1)
                        for c in range(GT):
                            pool.indirect_dma_start(expand, rows(row_g[k][:, c:c + 1]), vals[k][:, c, :], None)\
                                .then_inc(out[k], 16)
                for k in range(2):
                    pool.wait_ge(out[k], 16 * GT * (NG // 2))
                pool.wait_ge(ready, 1)
                pool.indirect_dma_start(expand, rows(g.first_row[:, :]), first_v[:, :], None).then_inc(put, 16)
                pool.wait_ge(put, 16)




def scan_sum(dve, out, keep, values, before):
    return dve.tensor_tensor_scan(out, keep, values, before, ALU.mult, ALU.add)


def scan_max(dve, out, penalty, values, before):
    return dve.tensor_tensor_scan(out, penalty, values, before, ALU.add, ALU.max)


class EdgeBuffers:

    def __init__(self, s, g, table_w, index_d, extras, sums_w):
        self.index_d, self.extras = index_d, extras
        self.rows = [s.sb(f"rows{k}", [P, J, table_w]) for k in range(2)]
        self.index = [s.sb(f"index{k}", [P, J], I32) for k in range(2)]
        self.extra = [[s.sb(f"extra{n}{k}", [P, J, e.shape[2]]) for n, e in enumerate(extras)] for k in range(2)]
        self.keep = [e[0][:, :, :].rearrange("p j o -> p (j o)") for e in self.extra]
        self.sums = [s.sb(f"sums{k}", [P, J, sums_w]) for k in range(2)]
        self.index_in, self.extra_in, self.gathered, self.used, self.done, self.stored = (
            [s.sem(f"{n}{k}", c) for k in range(2)] for n, c in
            (("index_in", 0), ("extra_in", 0), ("gathered", 0), ("used", 0), ("done", 1), ("stored", 16)))
        self.stage = s

    def load(self, sp):
        self.stage.grant(sp)

        def turn(i, first):
            for k in range(2):
                if not first:
                    sp.wait_ge(self.gathered[k], i * (16 * J))
                sp.dma_start(self.index[k][:, :], chunk(self.index_d, i, k)).then_inc(self.index_in[k], 16)
                sp.wait_ge(self.done[k], i + 1)
                for n, e in enumerate(self.extras):
                    sp.dma_start(self.extra[k][n][:, :, :], chunk(e, i, k)).then_inc(self.extra_in[k], 16)
        turn(0, True)
        with sp.Fori(1, NCH // 2) as i:
            turn(i, False)

    def wait_to_gather(self, pool, turn, k):
        pool.wait_ge(self.done[k], turn + 1)
        pool.wait_ge(self.index_in[k], turn * 16 + 16)

    def gather_column(self, pool, table, k, j):
        pool.indirect_dma_start(self.rows[k][:, j, :], None, table, rows(self.index[k][:, j:j + 1]))\
            .then_inc(self.gathered[k], 16)

    def gather_chunk(self, pool, g, table, turn, k):
        self.wait_to_gather(pool, turn, k)
        pool.sem_inc(g.gate, 1)
        for j in range(J):
            self.gather_column(pool, table, k, j)

    def gather(self, pool, g, table):
        with pool.Fori(0, NCH // 2) as i:
            for k in range(2):
                self.gather_chunk(pool, g, table, i, k)

    def store_chunk(self, act, acc, i, k):
        act.wait_ge(self.done[k], i + 2)
        act.dma_start(chunk(acc, i, k), self.sums[k][:, :, :]).then_inc(self.stored[k], 16)

    def all_stored(self, act):
        for k in range(2):
            act.wait_ge(self.stored[k], 16 * (NCH // 2) + 16)

    def wait_rows(self, dve, i, k):
        dve.wait_ge(self.gathered[k], i * (16 * J) + 16 * J)

    def wait_extra(self, dve, i, k):
        dve.wait_ge(self.extra_in[k], (i + 1) * (16 * len(self.extras)))


def attention_pass(nc, g, name, heads, width, table, expand, sums_d, kinds=False):
    hw = heads * width
    sw = hw + 2 * heads
    with Stage(nc, name) as s:
        b = EdgeBuffers(s, g, sw, g.src_id, [by_edge(t) for t in (g.keep_t, expand, g.type8_t)[:3 if kinds else 2]],
                        sums_d.shape[1])
        hot = s.sb("hot", [P, J, R8]) if kinds else None
        dst_part = [s.sb(f"dst{k}", [P, J, heads]) for k in range(2)]
        top = [s.sb(f"top{k}", [P, J + 1, heads]) for k in range(2)]
        e_, penalty = s.sb("e", [P, J, heads]), s.sb("penalty", [P, J])
        drop, factor = s.sb("drop", [P, 2, J, heads]), s.sb("factor", [P, 2, J, heads])
        dve_o = s.sem("dve")
        dropped, raised = [s.sem(f"dropped{k}") for k in range(2)], [s.sem(f"raised{k}") for k in range(2)]
        acc = by_edge(sums_d)
        with nc.Block() as block:
            @block.sync
            def _(sp):
                b.load(sp)

            @block.gpsimd
            def _(pool):
                b.gather(pool, g, table)

            @block.vector
            def _(dve):
                o = Order(dve, dve_o)
                dve.memset(dst_part[1][:, J - 1, :], 0.0)
                dve.memset(top[1][:, J, :], 0.0)
                o.link(dve.memset(b.sums[1][:, J - 1, :], 0.0))
                with dve.Fori(0, NCH // 2) as i:
                    per = 16 if kinds else 14
                    o = Order(dve, dve_o, i * per + 1)
                    for k in range(2):
                        keep, rows_, sums = b.keep[k], b.rows[k], b.sums[k]
                        before = b.sums[1 - k]
                        b.wait_extra(dve, i, k)
                        for h in range(heads):
                            scan_sum(dve, dst_part[k][:, :, h], keep, b.extra[k][1][:, :, h],
                                     dst_part[1 - k][:, J - 1, h:h + 1])
                        dve.tensor_scalar(penalty[:, :], keep, -1.0, BIG, ALU.add, ALU.mult)
                        if kinds:
                            kind = b.extra[k][2][:, :, :].rearrange("p j o -> p (j o)")
                            o.step(dve.tensor_tensor(hot[:, :, :],
                                                     g.count_f[:, 0:R8].unsqueeze(1).to_broadcast([P, J, R8]),
                                                     kind.unsqueeze(2).to_broadcast([P, J, R8]), ALU.is_equal))
                        o.link(dve.tensor_copy(top[k][:, 0, :], top[1 - k][:, J, :]))
                        b.wait_rows(dve, i, k)
                        o.link(dve.tensor_tensor(e_[:, :, :], rows_[:, :, hw:hw + heads], dst_part[k][:, :, :],
                                                 ALU.add))
                        o.link(dve.scalar_tensor_tensor(e_[:, :, :], e_[:, :, :], SLOPE, e_[:, :, :], ALU.mult,
                                                        ALU.max))
                        for h in range(heads):
                            last = scan_max(dve, top[k][:, 1:J + 1, h], penalty[:, :], e_[:, :, h],
                                            top[k][:, 0, h:h + 1])
                        o.link(last)
                        dve.tensor_tensor(drop[:, 1, :, :], e_[:, :, :], top[k][:, 1:J + 1, :], ALU.subtract)
                        o.link(dve.tensor_tensor(drop[:, 0, :, :], top[k][:, 0:J, :], top[k][:, 1:J + 1, :],
                                                 ALU.subtract))
                        dve.tensor_scalar(drop[:, 0, :, :], drop[:, 0, :, :], 0.0, None, ALU.min)\
                            .then_inc(dropped[k], 1)
                        dve.wait_ge(raised[k], i + 1)
                        o.link(dve.tensor_tensor(factor[:, 0, :, :], factor[:, 0, :, :],
                                                 keep.unsqueeze(2).to_broadcast([P, J, heads]), ALU.mult))
                        shaped = rows_[:, :, 0:hw].rearrange("p j (h c) -> p j h c", h=heads)
                        o.link(dve.tensor_tensor(shaped, shaped, factor[:, 1, :, :].unsqueeze(3)
                                                 .to_broadcast([P, J, heads, width]), ALU.mult))
                        dve.wait_ge(b.stored[k], i * 16 + 16)
                        dve.tensor_copy(sums[:, :, hw + heads:sw], top[k][:, 1:J + 1, :])
                        for r in range(R8 if kinds else 0):
                            scan_sum(dve, sums[:, :, sw + r], keep, hot[:, :, r], before[:, J - 1, sw + r:sw + r + 1])
                        for h in range(heads):
                            decay = factor[:, 0, :, h]
                            c = hw + h
                            scan_sum(dve, sums[:, :, c], decay, factor[:, 1, :, h], before[:, J - 1, c:c + 1])
                            for c in range(h * width, (h + 1) * width):
                                last = scan_sum(dve, sums[:, :, c], decay, rows_[:, :, c], before[:, J - 1, c:c + 1])
                        last.then_inc(b.done[k], 1)
                        dve.wait_ge(b.done[k], i + 2)
                    assert o.n == per, o.n

            @block.scalar
            def _(act):
                with act.Fori(0, NCH // 2) as i:
                    for k in range(2):
                        act.wait_ge(dropped[k], i + 1)
                        act.activation(factor[:, :, :, :], drop[:, :, :, :], ACT.Exp).then_inc(raised[k], 1)
                        b.store_chunk(act, acc, i, k)
                b.all_stored(act)


def carry_over(nc, g, name, sums_d, heads=0, per=0):
    acc = by_edge(sums_d)
    width = sums_d.shape[1]
    hw = heads * per
    sw = hw + 2 * heads
    with Stage(nc, name) as s:
        line = s.sb("line", [1, P, width])
        own, from_before = s.sb("own", [P, width]), s.sb("before", [P, width])
        top = s.sb("top", [1, P + 1, max(heads, 1)])
        penalty, drop, factor = (s.sb("penalty", [1, P]), s.sb("drop", [1, 2, P, max(heads, 1)]),
                                 s.sb("factor", [1, 2, P, max(heads, 1)]))
        top2, drop2, factor2 = (s.sb("top2", [P, max(heads, 1)]), s.sb("drop2", [P, 2, max(heads, 1)]),
                                s.sb("factor2", [P, 2, max(heads, 1)]))
        line_in, dve_o, scanned, line_out, before_in, cleared, own_in, mended, put, dropped, raised = (
            s.sem(n) for n in ("line_in", "dve", "scanned", "line_out", "before_in", "cleared", "own_in", "mended",
                               "put", "dropped", "raised"))
        carry = g.carry_d[:, 0:width]
        joined = g.joined[:, :]
        with nc.Block() as block:
            @block.sync
            def _(sp):
                sp.dma_start(line[:, :, :], acc[:, EP - 1:EP, :].rearrange("p o w -> o p w")).then_inc(line_in, 16)
                sp.wait_ge(scanned, 1)
                sp.dma_start(carry[1:P, :].unsqueeze(0), line[:, 0:P - 1, :]).then_inc(line_out, 16)
                sp.wait_ge(line_out, 16)
                sp.wait_ge(cleared, 1)
                sp.dma_start(from_before[1:P, :], carry[1:P, :]).then_inc(before_in, 16)

            @block.gpsimd
            def _(pool):
                pool.indirect_dma_start(own[:, :], None, sums_d, rows(g.mend_from[:, :])).then_inc(own_in, 16)
                pool.wait_ge(mended, 1)
                pool.indirect_dma_start(sums_d, rows(g.mend_to[:, :]), own[:, :], None).then_inc(put, 16)
                pool.wait_ge(put, 16)

            @block.vector
            def _(dve):
                o = Order(dve, dve_o)
                dve.memset(from_before[:, :], 0.0).then_inc(cleared, 1)
                dve.wait_ge(line_in, 16)
                for c in range(sw, width):
                    last = scan_sum(dve, line[:, :, c], joined, line[:, :, c], 0.0)
                if not heads:
                    last.then_inc(scanned, 1)
                    dve.wait_ge(own_in, 16)
                    dve.wait_ge(before_in, 16)
                    dve.tensor_tensor(own[:, :], own[:, :], from_before[:, :], ALU.add).then_inc(mended, 1)
                    return
                dve.tensor_scalar(penalty[:, :], joined, -1.0, BIG, ALU.add, ALU.mult)
                o.link(dve.memset(top[:, 0, :], 0.0))
                for h in range(heads):
                    last = scan_max(dve, top[:, 1:P + 1, h], penalty[:, :], line[:, :, hw + heads + h], 0.0)
                o.link(last)
                dve.tensor_tensor(drop[:, 1, :, :], line[:, :, hw + heads:sw], top[:, 1:P + 1, :], ALU.subtract)
                o.link(dve.tensor_tensor(drop[:, 0, :, :], top[:, 0:P, :], top[:, 1:P + 1, :], ALU.subtract))
                dve.tensor_scalar(drop[:, 0, :, :], drop[:, 0, :, :], 0.0, None, ALU.min).then_inc(dropped, 1)
                dve.wait_ge(raised, 1)
                dve.tensor_tensor(factor[:, 0, :, :], factor[:, 0, :, :],
                                  joined.unsqueeze(2).to_broadcast([1, P, heads]), ALU.mult)
                shaped = line[:, :, 0:hw].rearrange("o p (h c) -> o p h c", h=heads)
                dve.tensor_tensor(shaped, shaped, factor[:, 1, :, :].unsqueeze(3).to_broadcast([1, P, heads, per]),
                                  ALU.mult)
                dve.tensor_copy(line[:, :, hw + heads:sw], top[:, 1:P + 1, :])
                o.link(dve.tensor_tensor(line[:, :, hw:hw + heads], line[:, :, hw:hw + heads], factor[:, 1, :, :],
                                         ALU.mult))
                for h in range(heads):
                    for c in [hw + h, *range(h * per, (h + 1) * per)]:
                        last = scan_sum(dve, line[:, :, c], factor[:, 0, :, h], line[:, :, c], 0.0)
                last.then_inc(scanned, 1)
                dve.wait_ge(own_in, 16)
                dve.wait_ge(before_in, 16)
                o.link(dve.tensor_tensor(top2[:, :], own[:, hw + heads:sw], from_before[:, hw + heads:sw], ALU.max))
                dve.tensor_tensor(drop2[:, 0, :], own[:, hw + heads:sw], top2[:, :], ALU.subtract)
                dve.tensor_tensor(drop2[:, 1, :], from_before[:, hw + heads:sw], top2[:, :], ALU.subtract)\
                    .then_inc(dropped, 1)
                dve.wait_ge(raised, 2)
                for n, t in enumerate((own, from_before)):
                    shaped = t[:, 0:hw].rearrange("p (h c) -> p h c", h=heads)
                    dve.tensor_tensor(shaped, shaped, factor2[:, n, :].unsqueeze(2).to_broadcast([P, heads, per]),
                                      ALU.mult)
                    last = dve.tensor_tensor(t[:, hw:hw + heads], t[:, hw:hw + heads], factor2[:, n, :], ALU.mult)
                o.link(last)
                dve.tensor_copy(own[:, hw + heads:sw], top2[:, :])
                if width > sw:
                    dve.tensor_tensor(own[:, sw:], own[:, sw:], from_before[:, sw:], ALU.add)
                dve.tensor_tensor(own[:, 0:hw + heads], own[:, 0:hw + heads], from_before[:, 0:hw + heads], ALU.add)\
                    .then_inc(mended, 1)

            @block.scalar
            def _(act):
                if heads:
                    act.wait_ge(dropped, 1)
                    act.activation(factor[:, :, :, :], drop[:, :, :, :], ACT.Exp).then_inc(raised, 1)
                    act.wait_ge(dropped, 2)
                    act.activation(factor2[:, :, :], drop2[:, :, :], ACT.Exp).then_inc(raised, 1)



def load_constants(nc, name, pairs):
    with Stage(nc, name) as s:
        in_ = s.sem("in")
        with nc.Block() as block:
            @block.sync
            def _(sp):
                with nc.allow_non_contiguous_dma(reason="small weights, once"):
                    for dst, src in pairs:
                        sp.dma_start(dst, src).then_inc(in_, 16)
                    sp.wait_ge(in_, 16 * len(pairs))


def layer_norm(nc, g, name):
    with Stage(nc, name) as s:
        sq, total, mean, var, std = s.sb("sq", [P, NT, FD]), *(s.sb(n, [P, NT]) for n in ("tot", "mean", "var", "std"))
        dve_o, var_ready, root = s.sem("dve"), s.sem("var_ready"), s.sem("root")
        x, h = g.x[:, :, :], g.h[:, :, :]
        wide = [P, NT, FD]
        with nc.Block() as block:
            @block.vector
            def _(dve):
                o = Order(dve, dve_o)
                o.link(dve.tensor_reduce(total[:, :], x, AX.X, ALU.add))
                o.link(dve.tensor_scalar(mean[:, :], total[:, :], 1.0 / FD, None, ALU.mult))
                o.link(dve.tensor_tensor(h, x, mean[:, :].unsqueeze(2).to_broadcast(wide), ALU.subtract))
                o.link(dve.tensor_tensor(sq[:, :, :], h, h, ALU.mult))
                o.link(dve.tensor_reduce(total[:, :], sq[:, :, :], AX.X, ALU.add))
                dve.tensor_scalar(var[:, :], total[:, :], 1.0 / FD, 1e-5, ALU.mult, ALU.add).then_inc(var_ready, 1)
                dve.wait_ge(root, 1)
                o.link(dve.reciprocal(mean[:, :], std[:, :]))
                o.link(dve.tensor_tensor(h, h, mean[:, :].unsqueeze(2).to_broadcast(wide), ALU.mult))
                dve.tensor_scalar(h, h, 0.0, None, ALU.max)

            @block.scalar
            def _(act):
                act.wait_ge(var_ready, 1)
                act.activation(std[:, :], var[:, :], ACT.Sqrt).then_inc(root, 1)


def attention_weights(nc, g, name, w, a_src, a_dst, into, rows_w, heads, width):
    hw = heads * width
    with Stage(nc, name) as s:
        both, prod = s.sb("both", [rows_w, 2, hw]), s.sb("prod", [rows_w, 2, hw])
        in_, dve_o = s.sem("in"), s.sem("dve")
        with nc.Block() as block:
            @block.sync
            def _(sp):
                sp.dma_start(into[0:rows_w, 0:hw], w).then_inc(in_, 16)
                for n, v in enumerate((a_src, a_dst)):
                    sp.dma_start(both[:, n, :], v.rearrange("h c -> (h c)").partition_broadcast(rows_w))\
                        .then_inc(in_, 16)

            @block.vector
            def _(dve):
                o = Order(dve, dve_o)
                dve.wait_ge(in_, 48)
                o.link(dve.tensor_tensor(prod[:, :, :], both[:, :, :],
                                         into[0:rows_w, 0:hw].unsqueeze(1).to_broadcast([rows_w, 2, hw]), ALU.mult))
                dve.tensor_reduce(into[0:rows_w, hw:hw + 2 * heads],
                                  prod[:, :, :].rearrange("p n (h c) -> p (n h) c", h=heads), AX.X, ALU.add)


def finish_attention(nc, g, name, sums, table, bias, heads, width):
    hw = heads * width
    part_w = [P, NT, heads]
    with Stage(nc, name) as s:
        own, e_, top, drop, factor, inv = (s.sb("own", [P, NT, hw + 2 * heads]), s.sb("e", part_w), s.sb("top", part_w),
                                           s.sb("drop", [P, 2, NT, heads]), s.sb("factor", [P, 2, NT, heads]),
                                           s.sb("inv", part_w))
        own_in, dve_o, dropped, weighed, cut, raised = (
            s.sem(n) for n in ("own_in", "dve", "dropped", "weighed", "cut", "raised"))
        v, low = sums[:, :, 0:hw], own[:, :, 0:hw]

        def per_head(dve, t, scale):
            for h in range(heads):
                part = t[:, :, h * width:(h + 1) * width]
                last = dve.tensor_tensor(part, part, scale[:, :, h].unsqueeze(2).to_broadcast([P, NT, width]),
                                         ALU.mult)
            return last

        with nc.Block() as block:
            @block.sync
            def _(sp):
                sp.dma_start(own[:, :, :], by_node(table)).then_inc(own_in, 16)

            @block.vector
            def _(dve):
                o = Order(dve, dve_o)
                o.link(dve.tensor_scalar(inv[:, :, 0], g.has[:, :], -1.0, BIG, ALU.add, ALU.mult))
                m = sums[:, :, hw + heads:hw + 2 * heads]
                o.link(dve.tensor_tensor(m, m, inv[:, :, 0].unsqueeze(2).to_broadcast(part_w), ALU.add))
                dve.wait_ge(own_in, 16)
                o.link(dve.tensor_tensor(e_[:, :, :], own[:, :, hw:hw + heads], own[:, :, hw + heads:], ALU.add))
                o.link(dve.scalar_tensor_tensor(e_[:, :, :], e_[:, :, :], SLOPE, e_[:, :, :], ALU.mult, ALU.max))
                o.link(dve.tensor_tensor(top[:, :, :], e_[:, :, :], m, ALU.max))
                dve.tensor_tensor(drop[:, 0, :, :], m, top[:, :, :], ALU.subtract)
                dve.tensor_tensor(drop[:, 1, :, :], e_[:, :, :], top[:, :, :], ALU.subtract).then_inc(dropped, 1)
                dve.wait_ge(weighed, 1)
                z = sums[:, :, hw:hw + heads]
                per_head(dve, v, factor[:, 0, :, :])
                per_head(dve, low, factor[:, 1, :, :])
                o.link(dve.tensor_tensor(z, z, factor[:, 0, :, :], ALU.mult))
                o.link(dve.tensor_tensor(z, z, factor[:, 1, :, :], ALU.add))
                o.link(dve.tensor_scalar(inv[:, :, :], z, 1e-16, None, ALU.add))
                o.step(dve.reciprocal(inv[:, :, :], inv[:, :, :]))
                o.link(dve.tensor_tensor(v, v, low, ALU.add))
                o.link(per_head(dve, v, inv))
                o.link(dve.tensor_tensor(v, v, bias.unsqueeze(1).to_broadcast([P, NT, hw]), ALU.add))
                dve.tensor_scalar(low, v, 0.0, None, ALU.min).then_inc(cut, 1)
                dve.wait_ge(raised, 1)
                sa = SELU_SCALE * SELU_ALPHA
                dve.tensor_scalar(v, v, 0.0, SELU_SCALE, ALU.max, ALU.mult)
                o.link(dve.tensor_scalar(low, low, sa, -sa, ALU.mult, ALU.add))
                dve.tensor_tensor(v, v, low, ALU.add)

            @block.scalar
            def _(act):
                act.wait_ge(dropped, 1)
                act.activation(factor[:, :, :, :], drop[:, :, :, :], ACT.Exp).then_inc(weighed, 1)
                act.wait_ge(cut, 1)
                act.activation(low, low, ACT.Exp).then_inc(raised, 1)


def relation_pass(nc, g, name, table, index_d, sums_d, expand=None):
    first = expand is not None
    extras = [by_edge(g.keep_t)] + ([by_edge(g.type8_t), by_edge(expand)] if first else
                                    [by_edge(t) for t in (g.norm_t, g.lane_t, g.tile_t)])
    with Stage(nc, name) as s:
        b = EdgeBuffers(s, g, FD, index_d, extras, FD)
        inv = [s.sb(f"inv{k}", [P, J, R8]) for k in range(2)]
        hot = s.sb("hot", [P, J, R8])
        norm = [s.sb(f"norm{k}", [P, J]) for k in range(2)]
        dve_o = s.sem("dve")
        norm_ready, norm_stored = [s.sem(f"norm_ready{k}") for k in range(2)], [s.sem(f"norm_out{k}", 16) for k in range(2)]
        if not first:
            lo_hot = [s.sb(f"lo{k}", [P, J, P], BF16) for k in range(2)]
            hi_hot = [s.sb(f"hi{k}", [P, J, NT], BF16) for k in range(2)]
            none = s.sb("none", [P, P], BF16)
            hist = s.ps("hist", [P, 512])
            none_ready, counted = s.sem("none_ready"), s.sem("counted")
            hot_ready = [s.sem(f"hot{k}") for k in range(2)]
            hot_used = [s.sem(f"hot_used{k}", 1) for k in range(2)]
        acc = by_edge(sums_d)
        norm_d = g.norm_t.rearrange("(p j) o -> p (j o)", p=P)
        with nc.Block() as block:
            @block.sync
            def _(sp):
                b.load(sp)

            @block.gpsimd
            def _(pool):
                b.gather(pool, g, table)

            @block.vector
            def _(dve):
                o = Order(dve, dve_o)
                dve.memset(inv[1][:, J - 1, :], 0.0)
                if not first:
                    dve.memset(none[:, :], 0.0).then_inc(none_ready, 1)
                o.link(dve.memset(b.sums[1][:, J - 1, :], 0.0))
                per = 8 if first else 2
                with dve.Fori(0, NCH // 2) as i:
                    o = Order(dve, dve_o, i * per + 1)
                    for k in range(2):
                        rows_, sums = b.rows[k], b.sums[k]
                        b.wait_extra(dve, i, k)
                        if first:
                            kind = b.extra[k][1][:, :, :].rearrange("p j o -> p (j o)")
                            for r in range(R8):
                                last = scan_sum(dve, inv[k][:, :, r], b.keep[k], b.extra[k][2][:, :, r],
                                                inv[1 - k][:, J - 1, r:r + 1])
                            o.step(last)
                            o.link(dve.tensor_tensor(hot[:, :, :],
                                                     g.count_f[:, 0:R8].unsqueeze(1).to_broadcast([P, J, R8]),
                                                     kind.unsqueeze(2).to_broadcast([P, J, R8]), ALU.is_equal))
                            o.link(dve.tensor_tensor(hot[:, :, :], hot[:, :, :], inv[k][:, :, :], ALU.mult))
                            dve.wait_ge(norm_stored[k], i * 16 + 16)
                            dve.tensor_reduce(norm[k][:, :], hot[:, :, :], AX.X, ALU.add).then_inc(norm_ready[k], 1)
                            dve.wait_ge(norm_ready[k], i + 1)
                            scale = norm[k][:, :]
                        else:
                            scale, lo, hi = (e[:, :, :].rearrange("p j o -> p (j o)") for e in b.extra[k][1:])
                            dve.wait_ge(hot_used[k], i + 1)
                            dve.tensor_tensor(lo_hot[k][:, :, :],
                                              g.count_f[:, :].unsqueeze(1).to_broadcast([P, J, P]),
                                              lo.unsqueeze(2).to_broadcast([P, J, P]), ALU.is_equal)
                            dve.tensor_tensor(hi_hot[k][:, :, :],
                                              g.count_f[:, 0:NT].unsqueeze(1).to_broadcast([P, J, NT]),
                                              hi.unsqueeze(2).to_broadcast([P, J, NT]),
                                              ALU.is_equal).then_inc(hot_ready[k], 1)
                        b.wait_rows(dve, i, k)
                        o.link(dve.tensor_tensor(rows_[:, :, :], rows_[:, :, :],
                                                 scale.unsqueeze(2).to_broadcast([P, J, FD]), ALU.mult))
                        dve.wait_ge(b.stored[k], i * 16 + 16)
                        for c in range(FD):
                            last = scan_sum(dve, sums[:, :, c], b.keep[k], rows_[:, :, c],
                                            b.sums[1 - k][:, J - 1, c:c + 1])
                        last.then_inc(b.done[k], 1)
                        dve.wait_ge(b.done[k], i + 2)
                    assert o.n == per, o.n
                if not first:
                    dve.wait_ge(counted, 1)
                    dve.tensor_tensor(g.deg[:, :], g.deg[:, :], hist[:, 0:NT], ALU.add)

            @block.tensor
            def _(pe):
                if first:
                    return
                pe.wait_ge(none_ready, 1)
                pe.matmul(hist[:, 0:NT], none[:, :], none[:, 0:NT], start=True, stop=False)
                with pe.Fori(0, NCH // 2) as i:
                    for k in range(2):
                        pe.wait_ge(hot_ready[k], i + 1)
                        for j in range(J):
                            last = pe.matmul(hist[:, 0:NT], lo_hot[k][:, j, :], hi_hot[k][:, j, :], start=False,
                                             stop=False)
                        last.then_inc(hot_used[k], 1)
                pe.matmul(hist[:, 0:NT], none[:, :], none[:, 0:NT], start=False, stop=True).then_inc(counted, 1)

            @block.scalar
            def _(act):
                with act.Fori(0, NCH // 2) as i:
                    for k in range(2):
                        if first:
                            act.wait_ge(norm_ready[k], i + 1)
                            act.dma_start(chunk(norm_d, i, k), norm[k][:, :]).then_inc(norm_stored[k], 16)
                        b.store_chunk(act, acc, i, k)
                b.all_stored(act)
                if first:
                    for k in range(2):
                        act.wait_ge(norm_stored[k], 16 * (NCH // 2) + 16)


def reciprocal_counts(nc, g, name, counts, node_table):
    with Stage(nc, name) as s:
        dve_o, ready, out_ = s.sem("dve"), s.sem("ready"), s.sem("out")
        with nc.Block() as block:
            @block.vector
            def _(dve):
                o = Order(dve, dve_o)
                c = counts
                o.link(dve.tensor_tensor(c, c, g.has[:, :].unsqueeze(2).to_broadcast([P, NT, R8]), ALU.mult))
                o.link(dve.tensor_scalar(c, c, 1.0, None, ALU.max))
                dve.reciprocal(c, c).then_inc(ready, 1)

            @block.sync
            def _(sp):
                sp.wait_ge(ready, 1)
                sp.dma_start(by_node(node_table), counts).then_inc(out_, 16)
                sp.wait_ge(out_, 16)


def finish_relation(nc, g, name, agg, root_part, bias, into, last):
    wide = [P, NT, FD]
    with Stage(nc, name) as s:
        exps, top, total, log = s.sb("exps", wide), *(s.sb(n, [P, NT]) for n in ("top", "total", "log"))
        dve_o, shifted, raised, summed, logged = (s.sem(n) for n in ("dve", "shifted", "raised", "summed", "logged"))
        with nc.Block() as block:
            @block.vector
            def _(dve):
                o = Order(dve, dve_o)
                v = agg[:, :, :]
                o.link(dve.tensor_tensor(v, v, g.has[:, :].unsqueeze(2).to_broadcast(wide), ALU.mult))
                o.link(dve.tensor_tensor(v, v, root_part[:, :, :], ALU.add))
                o.link(dve.tensor_tensor(v, v, bias.unsqueeze(1).to_broadcast(wide), ALU.add))
                if not last:
                    dve.tensor_scalar(into[:, :, :], v, 0.0, None, ALU.max)
                    return
                o.link(dve.tensor_reduce(top[:, :], v, AX.X, ALU.max))
                dve.tensor_tensor(v, v, top[:, :].unsqueeze(2).to_broadcast(wide), ALU.subtract).then_inc(shifted, 1)
                dve.wait_ge(raised, 1)
                dve.tensor_reduce(total[:, :], exps[:, :, :], AX.X, ALU.add).then_inc(summed, 1)
                dve.wait_ge(logged, 1)
                o.link(dve.tensor_tensor(v, v, log[:, :].unsqueeze(2).to_broadcast(wide), ALU.subtract))
                dve.tensor_tensor(g.x[:, :, :], g.x[:, :, :], v, ALU.add)

            @block.scalar
            def _(act):
                if last:
                    act.wait_ge(shifted, 1)
                    act.activation(exps[:, :, :], agg[:, :, :], ACT.Exp).then_inc(raised, 1)
                    act.wait_ge(summed, 1)
                    act.activation(log[:, :], total[:, :], ACT.Ln).then_inc(logged, 1)


def sheaf_pass(nc, g, name, w1, w2, b1, b2, table, expand, sums_d):
    QC = 4
    NQ = J // QC
    HALF = J // 2
    F2 = 2 * FD
    HID = P // 2
    with Stage(nc, name) as s:
        b = EdgeBuffers(s, g, FD + 1, g.src_id, [by_edge(g.keep_t), by_edge(expand), by_edge(g.src_t)], FD)
        src_of = [e[2][:, :, :].rearrange("p j o -> p (j o)") for e in b.extra]
        filled = [s.sb(f"filled{k}", [P, J, FD + 1]) for k in range(2)]
        ends = s.sb("ends", [P, J, F2])
        v = s.sb("v", [P, J, F2])
        prod, once, twice = s.sb("prod", [P, J, F2]), s.sb("once", [P, J, F2]), s.sb("twice", [P, J, F2])
        dots, inv2 = s.sb("dots", [P, J, 2]), s.sb("inv2", [P, J, 2])
        same = s.sb("same", [P, J, P])
        earlier = s.sb("earlier", [P, QC, P])
        rank, place = s.sb("rank", [P, J]), s.sb("place", [P, J])
        spare_f = s.sb("spare", [P, 1])
        to_row = [s.sb(f"torow{k}", [P, J], I32) for k in range(2)]
        to_add = [s.sb(f"toadd{k}", [P, J, FD]) for k in range(2)]
        ends_t = [s.sb(f"endst{k}", [F2, QC * P]) for k in range(2)]
        hidden = [s.sb(f"hidden{k}", [P, QC * P]) for k in range(2)]
        across = [s.ps(f"across{k}", [P, QC * P]) for k in range(2)]
        ends_ps = [s.ps(f"endsp{k}", [F2, QC * P]) for k in range(2)]
        hidden_ps, v_ps = s.ps("hiddenp", [P, QC * P]), s.ps("vp", [P, QC * F2])
        added_ps = [s.ps(f"added{n}", [P, HALF * FD]) for n in range(2)]
        (dve_o, ends_ready, across_ready, across_used, ends_turned, ends_copied, hid_ready, hid_done, v_ready, v_used,
         same_ready, msg_ready, added) = (
            s.sem(n, c) for n, c in (("dve", 0), ("ends_ready", 0), ("across_ready", 0), ("across_used", 0),
                                     ("ends_turned", 0), ("ends_copied", 2), ("hid_ready", 2), ("hid_done", 1),
                                     ("v_ready", 1), ("v_used", 1), ("same_ready", 0), ("msg_ready", 0), ("added", 0)))
        added_taken = s.sem("added_taken", 1)
        to_add_free = [s.sem(f"to_add_free{k}", 1) for k in range(2)]
        to_add_ready = [s.sem(f"to_add_ready{k}") for k in range(2)]
        summed = [[s.sem(f"summed{k}{r}") for r in range(NSUM)] for k in range(2)]
        acc = by_edge(sums_d)
        per_table = J // NSUM
        with nc.Block() as block:
            @block.sync
            def _(sp):
                b.load(sp)

            @block.gpsimd
            def _(pool):
                def scatters(i, k, first=False, gathers=True):
                    pool.wait_ge(to_add_ready[k], i + 1)
                    if gathers:
                        b.wait_to_gather(pool, i + 1, k)
                    pool.sem_inc(g.gate, 1)
                    for j in range(J):
                        r = j % NSUM
                        if not (first and j < NSUM):
                            pool.wait_ge(summed[k][r], i * (16 * per_table) + 16 * (j // NSUM))
                            pool.sem_inc(g.gate, 1)
                        pool.indirect_dma_start(g.by_src[k][r], rows(to_row[k][:, j:j + 1]), to_add[k][:, j, :], None,
                                                compute_op=ALU.add).then_inc(summed[k][r], 16)
                        if gathers:
                            b.gather_column(pool, table, k, j)
                        if j == HALF and not (first and k == 0):
                            for r in range(NSUM):
                                pool.wait_ge(summed[1 - k][r], (i + k) * (16 * per_table))
                            pool.sem_inc(to_add_free[1 - k], 1)

                def turn(i, first=False, gathers=True):
                    for k in range(2):
                        scatters(i, k, first, gathers)
                for k in range(2):
                    b.gather_chunk(pool, g, table, 0, k)
                turn(0, first=True)
                with pool.Fori(1, NCH // 2 - 1) as i:
                    turn(i)
                turn(NCH // 2 - 1, gathers=False)
                for k in range(2):
                    for r in range(NSUM):
                        pool.wait_ge(summed[k][r], 16 * per_table * (NCH // 2))

            @block.vector
            def _(dve):
                o = Order(dve, dve_o)
                dve.memset(filled[1][:, J - 1, :], 0.0)
                dve.tensor_scalar(spare_f[:, :], g.lane_f[:, :], float(NP), None, ALU.add)
                o.link(dve.memset(b.sums[1][:, J - 1, :], 0.0))
                per = 2 * (NQ + 16)
                with dve.Fori(0, NCH // 2) as i:
                    o = Order(dve, dve_o, i * per + 1)
                    for k in range(2):
                        q0 = i * (2 * NQ) + k * NQ
                        c0 = i * 2 + k
                        rows_, sums = b.rows[k], b.sums[k]
                        b.wait_extra(dve, i, k)
                        for c in range(FD + 1):
                            last = scan_sum(dve, filled[k][:, :, c], b.keep[k], b.extra[k][1][:, :, c],
                                            filled[1 - k][:, J - 1, c:c + 1])
                        o.link(last)
                        b.wait_rows(dve, i, k)
                        dve.tensor_copy(ends[:, :, 0:FD], rows_[:, :, 0:FD])
                        dve.tensor_copy(ends[:, :, FD:F2], filled[k][:, :, 0:FD]).then_inc(ends_ready, 1)

                        def take_v(q):
                            dve.wait_ge(v_ready, q0 + q + 2)
                            dve.tensor_tensor(v[:, q * QC:(q + 1) * QC, :],
                                              v_ps[:, :].rearrange("p (c w) -> p c w", c=QC),
                                              b2.unsqueeze(1).to_broadcast([P, QC, F2]), ALU.add).then_inc(v_used, 1)
                        for q in range(NQ):
                            js = slice(q * QC, (q + 1) * QC)
                            dve.wait_ge(across_ready, q0 + q + 1)
                            o.link(dve.tensor_tensor(same[:, js, :],
                                                     across[q % 2][:, :].rearrange("p (c w) -> p c w", c=QC),
                                                     src_of[k][:, js].unsqueeze(2).to_broadcast([P, QC, P]),
                                                     ALU.is_equal))
                            dve.tensor_tensor(earlier[:, :, :], same[:, js, :],
                                              g.strict[:, :].unsqueeze(1).to_broadcast([P, QC, P]), ALU.mult)\
                                .then_inc(across_used, 1)
                            dve.wait_ge(across_used, q0 + q + 1)
                            dve.tensor_reduce(rank[:, js], earlier[:, :, :], AX.X, ALU.add).then_inc(same_ready, 1)
                            if q >= 1:
                                take_v(q - 1)
                            dve.wait_ge(same_ready, q0 + q + 1)
                        take_v(NQ - 1)
                        dve.wait_ge(v_used, q0 + NQ + 1)
                        o.link(dve.tensor_scalar(rank[:, :], rank[:, :], 0.0, None, ALU.is_equal))
                        o.link(dve.tensor_scalar(place[:, :], src_of[k], spare_f[:, :], None, ALU.subtract))
                        o.link(dve.tensor_tensor(place[:, :], place[:, :], rank[:, :], ALU.mult))
                        dve.wait_ge(to_add_free[k], i + 1)
                        dve.tensor_scalar(to_row[k][:, :], place[:, :], spare_f[:, :], None, ALU.add)
                        pairs = [P, J, 2]

                        def halves(t):
                            return t[:, :, :].rearrange("p j (n c) -> p j n c", n=2)

                        def wide(t):
                            return t[:, :, :].unsqueeze(3).to_broadcast([P, J, 2, FD])
                        o.link(dve.tensor_tensor(prod[:, :, :], v[:, :, :], v[:, :, :], ALU.mult))
                        o.link(dve.tensor_reduce(inv2[:, :, :], halves(prod), AX.X, ALU.add))
                        o.link(dve.tensor_scalar(inv2[:, :, :], inv2[:, :, :], 0.5, 0.5e-24, ALU.mult, ALU.max))
                        dve.reciprocal(inv2[:, :, :], inv2[:, :, :])
                        o.link(dve.tensor_tensor(prod[:, :, :], v[:, :, :], ends[:, :, :], ALU.mult))
                        o.link(dve.tensor_reduce(dots[:, :, :], halves(prod), AX.X, ALU.add))
                        o.link(dve.tensor_tensor(dots[:, :, :], dots[:, :, :], inv2[:, :, :], ALU.mult))
                        o.link(dve.tensor_tensor(halves(prod), halves(v), wide(dots), ALU.mult))
                        o.link(dve.tensor_tensor(once[:, :, :], ends[:, :, :], prod[:, :, :], ALU.subtract))
                        dve.tensor_tensor(prod[:, :, 0:FD], v[:, :, 0:FD], once[:, :, FD:F2], ALU.mult)
                        o.link(dve.tensor_tensor(prod[:, :, FD:F2], v[:, :, FD:F2], once[:, :, 0:FD], ALU.mult))
                        o.link(dve.tensor_reduce(dots[:, :, :], halves(prod), AX.X, ALU.add))
                        o.link(dve.tensor_tensor(dots[:, :, :], dots[:, :, :], inv2[:, :, :], ALU.mult))
                        o.link(dve.tensor_tensor(halves(prod), halves(v), wide(dots), ALU.mult))
                        dve.tensor_tensor(twice[:, :, 0:FD], once[:, :, FD:F2], prod[:, :, 0:FD], ALU.subtract)\
                            .then_inc(msg_ready, 1)
                        dve.tensor_tensor(twice[:, :, FD:F2], once[:, :, 0:FD], prod[:, :, FD:F2], ALU.subtract)\
                            .then_inc(msg_ready, 1)
                        dve.wait_ge(msg_ready, c0 * 4 + 2)
                        dve.tensor_tensor(twice[:, :, FD:F2], twice[:, :, FD:F2],
                                          rows_[:, :, FD:].to_broadcast([P, J, FD]), ALU.mult).then_inc(msg_ready, 1)
                        dve.tensor_tensor(twice[:, :, 0:FD], twice[:, :, 0:FD],
                                          filled[k][:, :, FD:].to_broadcast([P, J, FD]), ALU.mult)\
                            .then_inc(msg_ready, 1)
                        dve.wait_ge(msg_ready, c0 * 4 + 4)
                        dve.wait_ge(b.stored[k], i * 16 + 16)
                        for c in range(FD):
                            last = scan_sum(dve, sums[:, :, c], b.keep[k], twice[:, :, FD + c],
                                            b.sums[1 - k][:, J - 1, c:c + 1])
                        last.then_inc(b.done[k], 1)
                        dve.wait_ge(b.done[k], i + 2)
                    assert o.n == per, o.n

            @block.tensor
            def _(pe):
                with pe.Fori(0, NCH // 2) as i:
                    for k in range(2):
                        q0 = i * (2 * NQ) + k * NQ
                        c0 = i * 2 + k
                        pe.wait_ge(ends_ready, c0 + 1)

                        def spin(q):
                            if q >= 2:
                                pe.wait_ge(across_used, q0 + q - 1)
                            for c in range(QC):
                                j = q * QC + c
                                last = pe.matmul(across[q % 2][:, c * P:(c + 1) * P],
                                                 src_of[k][:, j:j + 1].to_broadcast([P, P]), g.ident[:, :],
                                                 start=True, stop=True)
                            last.then_inc(across_ready, 1)
                            pe.wait_ge(ends_copied, q0 + q + 1)
                            for c in range(QC):
                                last = pe.transpose(ends_ps[(q + k * NQ) % 2][:, c * P:(c + 1) * P],
                                                    ends[:, q * QC + c, :], g.ident[:, :])
                            last.then_inc(ends_turned, 1)

                        def hide(q):
                            pe.wait_ge(ends_copied, q0 + q + 3)
                            pe.wait_ge(hid_done, q0 + q + 1)
                            pe.matmul(hidden_ps[:, :], w1, ends_t[(q + k * NQ) % 2][:, :], start=True, stop=True)\
                                .then_inc(hid_ready, 1)

                        def unhide(q):
                            pe.wait_ge(hid_done, q0 + q + 2)
                            pe.wait_ge(v_used, q0 + q + 1)
                            for c in range(QC):
                                last = pe.matmul(v_ps[:, c * F2:(c + 1) * F2],
                                                 hidden[(q + k * NQ) % 2][:, c * P:(c + 1) * P], w2,
                                                 start=True, stop=True)
                            last.then_inc(v_ready, 1)
                        spin(0)
                        for q in range(NQ):
                            if q + 1 < NQ:
                                spin(q + 1)
                            hide(q)
                            if q >= 1:
                                unhide(q - 1)
                        unhide(NQ - 1)
                        pe.wait_ge(msg_ready, c0 * 4 + 4)
                        pe.wait_ge(same_ready, q0 + NQ)
                        pe.wait_ge(added_taken, c0 + 1)
                        for j in range(J):
                            last = pe.matmul(added_ps[j // HALF][:, (j % HALF) * FD:(j % HALF + 1) * FD],
                                             same[:, j, :], twice[:, j, 0:FD], start=True, stop=True)
                        last.then_inc(added, 1)

            @block.scalar
            def _(act):
                with act.Fori(0, NCH // 2) as i:
                    for k in range(2):
                        q0 = i * (2 * NQ) + k * NQ

                        def take_ends(q):
                            act.wait_ge(ends_turned, q0 + q + 1)
                            act.wait_ge(hid_ready, q0 + q + 1)
                            act.copy(ends_t[(q + k * NQ) % 2][:, :], ends_ps[(q + k * NQ) % 2][:, :])\
                                .then_inc(ends_copied, 1)
                        take_ends(0)
                        for q in range(NQ):
                            if q + 1 < NQ:
                                take_ends(q + 1)
                            act.wait_ge(hid_ready, q0 + q + 3)
                            if q > 0 or k > 0:
                                act.wait_ge(v_ready, q0 + q)
                            act.activation(hidden[(q + k * NQ) % 2][:, :], hidden_ps[:, :], ACT.Relu, bias=b1)\
                                .then_inc(hid_done, 1)
                        b.store_chunk(act, acc, i, k)
                        act.wait_ge(added, i * 2 + k + 1)
                        act.wait_ge(to_add_free[k], i + 1)
                        act.copy(to_add[k][:, 0:HALF, :], added_ps[0][:, :].rearrange("p (c w) -> p c w", w=FD))
                        act.copy(to_add[k][:, HALF:J, :], added_ps[1][:, :].rearrange("p (c w) -> p c w", w=FD))\
                            .then_inc(to_add_ready[k], 1)
                        act.wait_ge(to_add_ready[k], i + 1)
                        act.sem_inc(added_taken, 1)
                b.all_stored(act)


def sheaf_table(nc, g, name, table, values):
    with Stage(nc, name) as s:
        t1 = s.sb("t1", [P, NT])
        dve_o, capped, root, ready, out_ = (s.sem(n) for n in ("dve", "capped", "root", "ready", "out"))
        with nc.Block() as block:
            @block.vector
            def _(dve):
                dve.tensor_scalar(t1[:, :], g.deg[:, :], 1e-5, None, ALU.max).then_inc(capped, 1)
                dve.tensor_copy(values[:, :, 0:FD], g.h[:, :, :])
                dve.wait_ge(root, 1)
                dve.reciprocal(values[:, :, FD], t1[:, :]).then_inc(ready, 1)

            @block.scalar
            def _(act):
                act.wait_ge(capped, 1)
                act.activation(t1[:, :], t1[:, :], ACT.Sqrt).then_inc(root, 1)

            @block.sync
            def _(sp):
                sp.wait_ge(ready, 1)
                sp.dma_start(by_node(table), values[:, :, :]).then_inc(out_, 16)
                sp.wait_ge(out_, 16)


def finish_sheaf(nc, g, name, agg, values):
    wide = [P, NT, FD]
    tables = [t for ts in g.by_src for t in ts]
    with Stage(nc, name) as s:
        parts = [s.sb(f"part{n}", wide) for n in range(len(tables))]
        in_ = [s.sem(f"in{n}") for n in range(len(tables))]
        dve_o = s.sem("dve")
        with nc.Block() as block:
            @block.sync
            def _(sp):
                for n, t in enumerate(tables):
                    sp.dma_start(parts[n][:, :, :], by_node(t[0:NP])).then_inc(in_[n], 16)

            @block.vector
            def _(dve):
                o = Order(dve, dve_o)
                v = agg[:, :, :]
                o.link(dve.tensor_tensor(v, v, g.has[:, :].unsqueeze(2).to_broadcast(wide), ALU.mult))
                for n in range(len(tables)):
                    dve.wait_ge(in_[n], 16)
                    o.link(dve.tensor_tensor(v, v, parts[n][:, :, :], ALU.add))
                o.link(dve.tensor_tensor(v, v, values[:, :, FD:].to_broadcast(wide), ALU.mult))
                o.link(dve.tensor_tensor(v, v, g.h[:, :, :], ALU.add))
                o.link(dve.tensor_scalar(v, v, 0.0, None, ALU.max))
                dve.tensor_tensor(g.x[:, :, :], g.x[:, :, :], v, ALU.add)


def sheaf_weights(nc, g, name, a, w1, w2, b1, b2):
    hid = P // 2
    with Stage(nc, name) as s:
        in_, cleared = s.sem("in"), s.sem("cleared")
        with nc.Block() as block:
            @block.vector
            def _(dve):
                dve.memset(w2[:, :], 0.0).then_inc(cleared, 1)

            @block.sync
            def _(sp):
                w1t, w2t = a.L2_gnn_W1.rearrange("h i -> i h"), a.L2_gnn_W2.rearrange("o h -> h o")
                b1c = a.L2_gnn_b1.unsqueeze(1)
                sp.wait_ge(cleared, 1)
                with nc.allow_non_contiguous_dma(reason="small weights, once"):
                    pairs = [(w1[:, 0:hid], w1t), (w1[0:FD, hid:], w1t[FD:, :]), (w1[FD:, hid:], w1t[0:FD, :]),
                             (w2[0:hid, 0:FD], w2t), (w2[hid:, FD:], w2t), (b1[0:hid, :], b1c), (b1[hid:, :], b1c),
                             (b2[:, 0:FD], a.L2_gnn_b2.partition_broadcast(P)),
                             (b2[:, FD:], a.L2_gnn_b2.partition_broadcast(P))]
                    for dst, src in pairs:
                        sp.dma_start(dst, src).then_inc(in_, 16)
                    sp.wait_ge(in_, 16 * len(pairs))


def relation_weights(nc, g, name, a, w, attr_w):
    M = R90 * (FD + 1)
    with Stage(nc, name) as s:
        comp_t, bases = s.sb("compt", [NB, R90]), s.sb("bases", [NB, FD, FD])
        mixed, ws, wa = s.sb("mixed", [R90, FD, FD]), s.sb("ws", [FD, FD]), s.sb("wa", [FD, 3])
        wa_wide, parts = s.sb("wawide", [FD, P]), s.sb("parts", [FD, 2])
        mixed_ps, parts_ps, attr_ps = s.ps("mixedp", [R90, FD * FD]), s.ps("partsp", [FD, 2]), s.ps("attrp", [P, FD])
        in_, mixed_ready, mixed_sb, out_, back, wide_ready, small, cp = (
            s.sem(n) for n in ("in", "mixed_ready", "mixed_sb", "out", "back", "wide_ready", "small", "cp"))
        w_view = w[:, 0:M].rearrange("i (r c) -> i r c", r=R90)
        flat = g.mixed_d
        with nc.Block() as block:
            @block.sync
            def _(sp):
                with nc.allow_non_contiguous_dma(reason="small weights, once"):
                    v = a.L3_gnn_weight.rearrange("b i o -> (b i) o").rearrange("(i b) o -> b i o", b=NB)
                    pairs = [(comp_t[:, :], a.L3_gnn_w_comp.rearrange("r b -> b r")), (bases[:, :, :], v),
                             (ws[:, :], a.L3_gnn_Ws), (wa[:, :], a.L3_gnn_Wa.rearrange("u (n o) -> o (u n)", n=3))]
                    for dst, src in pairs:
                        sp.dma_start(dst, src).then_inc(in_, 16)
                sp.wait_ge(mixed_sb, 1)
                sp.dma_start(flat.rearrange("(i r) o -> r i o", r=R90), mixed[:, :, :]).then_inc(out_, 16)
                sp.wait_ge(out_, 16)
                sp.dma_start(w_view[:, :, 0:FD], flat.rearrange("(r i) o -> i r o", i=FD)).then_inc(back, 16)
                sp.wait_ge(back, 16)

            @block.tensor
            def _(pe):
                pe.wait_ge(in_, 64)
                pe.matmul(mixed_ps[:, :], comp_t[:, :], bases[:, :, :].rearrange("b i o -> b (i o)"), start=True,
                          stop=True).then_inc(mixed_ready, 1)
                pe.matmul(parts_ps[:, 0:1], ws[:, :], wa[:, 0:1], start=True, stop=True)
                pe.matmul(parts_ps[:, 1:2], ws[:, :], wa[:, 2:3], start=True, stop=True)
                pe.wait_ge(wide_ready, 1)
                pe.matmul(attr_ps[:, :], wa_wide[:, :], ws[:, :], start=True, stop=True).then_inc(small, 1)

            @block.vector
            def _(dve):
                dve.wait_ge(in_, 64)
                dve.tensor_copy(wa_wide[:, :], wa[:, 1:2].to_broadcast([FD, P])).then_inc(wide_ready, 1)
                dve.wait_ge(mixed_ready, 1)
                dve.tensor_copy(mixed[:, :, :].rearrange("r i o -> r (i o)"), mixed_ps[:, :]).then_inc(mixed_sb, 1)
                dve.wait_ge(small, 1)
                dve.tensor_copy(attr_w, attr_ps[:, :])
                dve.tensor_copy(parts[:, :], parts_ps[:, :]).then_inc(cp, 1)
                dve.wait_ge(cp, 1)
                dve.tensor_copy(w[:, M:M + 1], parts[:, 1:2])
                dve.tensor_copy(w_view[:, :, FD], parts[:, 0:1].to_broadcast([FD, R90]))


def store_nodes(nc, name, table, values):
    with Stage(nc, name) as s:
        out_ = s.sem("out")
        with nc.Block() as block:
            @block.sync
            def _(sp):
                with nc.allow_non_contiguous_dma(reason="one word per node, once"):
                    sp.dma_start(by_node(table), values[:, :, :]).then_inc(out_, 16)
                    sp.wait_ge(out_, 16)


def typed_attention_pass(nc, g, name, table, expand, attr, attr_w, sums_d):
    with Stage(nc, name) as s:
        b = EdgeBuffers(s, g, FD + 1, g.idx90_d, [by_edge(g.keep_t), by_edge(expand), attr], FD)
        dst_part = [s.sb(f"dst{k}", [P, J]) for k in range(2)]
        weight = s.sb("weight", [P, J])
        dve_o = s.sem("dve")
        acc = by_edge(sums_d)
        with nc.Block() as block:
            @block.sync
            def _(sp):
                b.load(sp)

            @block.gpsimd
            def _(pool):
                b.gather(pool, g, table)

            @block.vector
            def _(dve):
                o = Order(dve, dve_o)
                dve.memset(dst_part[1][:, :], 0.0)
                o.link(dve.memset(b.sums[1][:, J - 1, :], 0.0))
                per = 10
                with dve.Fori(0, NCH // 2) as i:
                    o = Order(dve, dve_o, i * per + 1)
                    for k in range(2):
                        rows_, at = b.rows[k], b.extra[k][2]
                        b.wait_extra(dve, i, k)
                        o.step(scan_sum(dve, dst_part[k][:, :], b.keep[k], b.extra[k][1][:, :, 0],
                                        dst_part[1 - k][:, J - 1:J]))
                        o.link(dve.tensor_tensor(at[:, :, :], at[:, :, :],
                                                 attr_w.unsqueeze(1).to_broadcast([P, J, FD]), ALU.mult))
                        o.link(dve.tensor_reduce(weight[:, :], at[:, :, :], AX.X, ALU.add))
                        o.link(dve.tensor_tensor(weight[:, :], weight[:, :], dst_part[k][:, :], ALU.add))
                        b.wait_rows(dve, i, k)
                        part = rows_[:, :, FD:].rearrange("p j o -> p (j o)")
                        o.link(dve.tensor_tensor(weight[:, :], weight[:, :], part, ALU.add))
                        dve.tensor_tensor(rows_[:, :, 0:FD], rows_[:, :, 0:FD],
                                          weight[:, :].unsqueeze(2).to_broadcast([P, J, FD]), ALU.mult)\
                            .then_inc(b.used[k], 1)
                        dve.wait_ge(b.used[k], i + 1)
                        dve.wait_ge(b.stored[k], i * 16 + 16)
                        for c in range(FD):
                            last = scan_sum(dve, b.sums[k][:, :, c], b.keep[k], rows_[:, :, c],
                                            b.sums[1 - k][:, J - 1, c:c + 1])
                        last.then_inc(b.done[k], 1)
                        dve.wait_ge(b.done[k], i + 2)
                    assert o.n == per, o.n

            @block.scalar
            def _(act):
                with act.Fori(0, NCH // 2) as i:
                    for k in range(2):
                        b.store_chunk(act, acc, i, k)
                b.all_stored(act)


def finish_all(nc, g, name, agg, out):
    with Stage(nc, name) as s:
        dve_o, ready, out_ = s.sem("dve"), s.sem("ready"), s.sem("out")
        with nc.Block() as block:
            @block.vector
            def _(dve):
                v = agg[:, :, :]
                Order(dve, dve_o).link(dve.tensor_tensor(v, v, g.has[:, :].unsqueeze(2).to_broadcast([P, NT, FD]),
                                                         ALU.mult))
                dve.tensor_tensor(v, v, g.x[:, :, :], ALU.add).then_inc(ready, 1)

            @block.sync
            def _(sp):
                sp.wait_ge(ready, 1)
                sp.dma_start(by_node(out), agg[:, :, :]).then_inc(out_, 16)
                sp.wait_ge(out_, 16)


def add_rows(nc, g, name, rows_, bias):
    with Stage(nc, name) as s:
        dve_o = s.sem("dve")
        with nc.Block() as block:
            @block.vector
            def _(dve):
                o = Order(dve, dve_o)
                x = g.x[:, :, :]
                o.link(dve.tensor_tensor(x, x, rows_[:, :, :], ALU.add))
                dve.tensor_tensor(x, x, bias.unsqueeze(1).to_broadcast([P, NT, FD]), ALU.add)



def attention_layers(nc, a, g):
    with Stage(nc, "gat") as s:
        h1, c1, h2, c2 = 3, 32, 1, 32
        w1, w2, wf = s.sb("w1", [FD, h1 * c1 + 2 * h1]), s.sb("w2", [h1 * c1, c2 + 2]), s.sb("wf", [c2, FD])
        b1, b2, bf = s.sb("b1", [P, h1 * c1]), s.sb("b2", [P, c2]), s.sb("bf", [P, FD])
        table1, table2 = g.dram("att1_t", [NP, 102]), g.dram("att2_t", [NP, 34])
        sums1, sums2 = g.sums["att1"], g.sums["att2"]
        load_constants(nc, "gat_in", [(b1[:, :], a.L0_gnn_b1.partition_broadcast(P)),
                                      (b2[:, :], a.L0_gnn_b2.partition_broadcast(P)),
                                      (bf[:, :], a.L0_gnn_bf.partition_broadcast(P)), (wf[:, :], a.L0_gnn_Wf)])
        attention_weights(nc, g, "gat_w1", a.L0_gnn_W1, a.L0_gnn_a_src1, a.L0_gnn_a_dst1, w1, FD, h1, c1)
        attention_weights(nc, g, "gat_w2", a.L0_gnn_W2, a.L0_gnn_a_src2, a.L0_gnn_a_dst2, w2, h1 * c1, h2, c2)
        layer_norm(nc, g, "ln1")
        with Stage(nc, "gat1") as t:
            parts = t.sb("parts", [P, NT, h1])
            project(nc, g, "gat1_p", g.h, FD, w1, 102, table1, (parts, 99))
            spread(nc, g, "gat1_s", parts, table1, g.expand["att1"], h1)
        attention_pass(nc, g, "gat1_e", h1, c1, table1, g.expand["att1"], sums1)
        carry_over(nc, g, "gat1_c", sums1, h1, c1)
        with Stage(nc, "gat1n") as t:
            big, parts = t.sb("big", [P, NT, 102]), t.sb("parts", [P, NT, 1])
            gather_to(nc, g, "gat1_g", sums1, g.last_row, 102, big)
            finish_attention(nc, g, "gat1_f", big, table1, b1[:, :], h1, c1)
            project(nc, g, "gat2_p", big, 96, w2, 34, table2, (parts, 33))
            spread(nc, g, "gat2_s", parts, table2, g.expand["att2"], h2)
        attention_pass(nc, g, "gat2_e", h2, c2, table2, g.expand["att2"], sums2, kinds=True)
        carry_over(nc, g, "gat2_c", sums2, h2, c2)
        with Stage(nc, "gat2n") as t:
            sw = c2 + 2
            big = t.sb("big", [P, NT, sw + R8])
            gather_to(nc, g, "gat2_g", sums2, g.last_row, sw + R8, big)
            counts = big[:, :, sw:]
            reciprocal_counts(nc, g, "count_r", counts, g.counts_d)
            spread(nc, g, "count_s", counts, g.counts_d, g.expand["rel"], R8)
            finish_attention(nc, g, "gat2_f", big, table2, b2[:, :], h2, c2)
            project(nc, g, "gatf_p", big, c2, wf, FD, None, (g.h, 0))
            add_rows(nc, g, "gatf_a", g.h, bf[:, :])


def relation_layers(nc, a, g):
    with Stage(nc, "rgcn") as s:
        wide = R8 * FD + FD
        w = [s.sb(f"w{n}", [FD, wide]) for n in range(2)]
        bias = [s.sb(f"b{n}", [P, FD]) for n in range(2)]
        tables = [g.dram(f"rel_t{n}", [NP, R8 * FD]) for n in range(2)]
        load_constants(nc, "rgcn_in", [
            x for n, (wr, root, b) in enumerate(((a.L1_gnn_W1, a.L1_gnn_root1, a.L1_gnn_b1),
                                                 (a.L1_gnn_W2, a.L1_gnn_root2, a.L1_gnn_b2)))
            for x in ((w[n][:, 0:R8 * FD].rearrange("i (r o) -> i r o", r=R8), wr.rearrange("r i o -> i r o")),
                      (w[n][:, R8 * FD:], root), (bias[n][:, :], b.partition_broadcast(P)))])
        layer_norm(nc, g, "ln2")
        for n in range(2):
            with Stage(nc, f"rgcn{n}") as t:
                root_part, agg = t.sb("root", [P, NT, FD]), t.sb("agg", [P, NT, FD])
                project(nc, g, f"rgcn{n}_p", g.h, FD, w[n], wide, tables[n], (root_part, R8 * FD))
                relation_pass(nc, g, f"rgcn{n}_e", tables[n].rearrange("n (r o) -> (n r) o", r=R8), g.idx8_d,
                              g.sums["rel"], g.expand["rel"] if n == 0 else None)
                carry_over(nc, g, f"rgcn{n}_c", g.sums["rel"])
                gather_to(nc, g, f"rgcn{n}_g", g.sums["rel"], g.last_row, FD, agg)
                finish_relation(nc, g, f"rgcn{n}_f", agg, root_part, bias[n][:, :], g.h, n == 1)


def sheaf_layer(nc, a, g):
    with Stage(nc, "sheaf") as s:
        w1, w2, b1, b2 = s.sb("w1", [2 * FD, P]), s.sb("w2", [P, 2 * FD]), s.sb("b1", [P, 1]), s.sb("b2", [P, 2 * FD])
        table = g.dram("sheaf_t", [NP, FD + 1])
        values = s.sb("values", [P, NT, FD + 1])
        sheaf_weights(nc, g, "sheaf_w", a, w1, w2, b1, b2)
        layer_norm(nc, g, "ln3")
        sheaf_table(nc, g, "sheaf_n", table, values)
        spread(nc, g, "sheaf_s", values, table, g.expand["sheaf"], FD + 1)
        sheaf_pass(nc, g, "sheaf_e", w1[:, :], w2[:, :], b1[:, :], b2[:, :], table, g.expand["sheaf"],
                   g.sums["sheaf"])
        carry_over(nc, g, "sheaf_c", g.sums["sheaf"])
        with Stage(nc, "sheafn") as t:
            agg = t.sb("agg", [P, NT, FD])
            gather_to(nc, g, "sheaf_g", g.sums["sheaf"], g.last_row, FD, agg)
            finish_sheaf(nc, g, "sheaf_f", agg, values)


def typed_layer(nc, a, g, out):
    with Stage(nc, "typed") as s:
        M = R90 * (FD + 1)
        w, attr_w = s.sb("w", [FD, M + 1]), s.sb("attrw", [P, FD])
        g.mixed_d = g.dram("mixed_d", [FD * R90, FD])
        table, part_d = g.dram("typed_t", [NP, M]), g.dram("typed_dst", [NP, 1])
        relation_weights(nc, g, "typed_w", a, w, attr_w[:, :])
        layer_norm(nc, g, "ln4")
        with Stage(nc, "typedp") as t:
            parts = t.sb("parts", [P, NT, 1])
            project(nc, g, "typed_p", g.h, FD, w, M + 1, table, (parts, M))
            store_nodes(nc, "typed_d", part_d, parts)
            spread(nc, g, "typed_s", parts, part_d, g.expand["typed"], 1)
        typed_attention_pass(nc, g, "typed_e", table.rearrange("n (r c) -> (n r) c", c=FD + 1),
                             g.expand["typed"], a.attr, attr_w[:, :], g.sums["typed"])
        carry_over(nc, g, "typed_c", g.sums["typed"])
        with Stage(nc, "typedn") as t:
            agg = t.sb("agg", [P, NT, FD])
            gather_to(nc, g, "typed_g", g.sums["typed"], g.last_row, FD, agg)
            finish_all(nc, g, "typed_f", agg, out)


class Arrays:
    pass


def declare(nc, a, g, w):
    sb = w.sb

    def dram(name, shape, dt=F32):
        return nc.dram_tensor(name, shape, dt, kind="Internal").ap()

    def flat(t):
        return t.rearrange("(p j) o -> p (j o)", p=P)
    g.dram = dram
    g.gate = w.sem("gate")
    g.x, g.h = sb("x", [P, NT, FD]), sb("h", [P, NT, FD])
    g.ident, g.strict, g.count_f = sb("ident", [P, P]), sb("strict", [P, P]), sb("countf", [P, P])
    g.node_f, g.deg, g.has = sb("nodef", [P, NT]), sb("deg", [P, NT]), sb("has", [P, NT])
    g.last_row, g.start_row = sb("lastrow", [P, NT], I32), sb("startrow", [P, NT], I32)
    g.first_row, g.dst_first, g.lane_i = (sb(n, [P, 1], I32) for n in ("firstrow", "dstfirst", "lanei"))
    g.mend_from, g.mend_to = sb("mendfrom", [P, 1], I32), sb("mendto", [P, 1], I32)
    g.first_f, g.lane_f, g.joined = sb("firstf", [P, 1]), sb("lanef", [P, 1]), sb("joined", [1, P])
    g.keep_t, g.dst_t, g.src_t, g.lane_t, g.tile_t, g.type8_t, g.norm_t = (
        dram(n, [EROWS, 1]) for n in ("keep_d", "dst_d", "srcf_d", "lane_d", "tile_d", "type8_d", "norm_d"))
    g.keep_d, g.dst_d, g.src_fd, g.lane_d, g.tile_d, g.type8_d = (
        flat(t) for t in (g.keep_t, g.dst_t, g.src_t, g.lane_t, g.tile_t, g.type8_t))
    g.idx8_d, g.idx90_d = dram("idx8_d", [P, EP], I32), dram("idx90_d", [P, EP], I32)
    g.src_id = a.src
    g.total_d = dram("total_d", [NP + 1, 1])
    g.carry_d = dram("carry_d", [P, 102])
    g.counts_d = dram("counts_t", [NP, R8])
    g.expand = {n: dram(f"expand{n}", [XROWS, k]) for n, k in
                (("att1", 3), ("att2", 1), ("rel", R8), ("sheaf", FD + 1), ("typed", 1))}
    g.by_src = [[dram(f"bysrc{k}{r}", [NP + P, FD]) for r in range(NSUM)] for k in range(2)]
    g.sums = {n: dram(f"sums{n}", [EROWS + P, k]) for n, k in
              (("att1", 102), ("att2", 34 + R8), ("rel", FD), ("sheaf", FD), ("typed", FD))}
    g.to_zero = [t[EROWS:EROWS + P] for t in g.sums.values()] + list(g.expand.values()) + \
                [t for ts in g.by_src for t in ts]


def build(nc, a, out):
    g = Arrays()
    with Stage(nc, "whole") as w:
        declare(nc, a, g, w)
        set_up(nc, a, g)
        node_ranges(nc, g)
        attention_layers(nc, a, g)
        relation_layers(nc, a, g)
        sheaf_layer(nc, a, g)
        typed_layer(nc, a, g, out)



_WEIGHTS = [f"L0_gnn_{n}" for n in ("W1", "a_src1", "a_dst1", "b1", "W2", "a_src2", "a_dst2", "b2", "Wf", "bf")] + \
           [f"L1_gnn_{n}" for n in ("W1", "root1", "b1", "W2", "root2", "b2")] + \
           [f"L2_gnn_{n}" for n in ("W1", "b1", "W2", "b2")] + \
           [f"L3_gnn_{n}" for n in ("Ws", "Wa", "weight", "w_comp")]


def kernel(**inputs):
    import types

    import concourse.bacc as bacc
    from concourse.bass_utils import run_bass_kernel_spmd

    extra = P * EP - E

    def by_partition(v, fill):
        return np.pad(v, (0, extra), constant_values=fill).reshape(P, EP)

    given = {n: np.asarray(inputs[n]) for n in ("x", "src", "dst", "edge_attr_16", "edge_type_8", "edge_type_90",
                                                *_WEIGHTS)}
    arrays = {
        "x": np.pad(given["x"], ((0, NP - N), (0, 0))),
        "src": by_partition(given["src"], N),
        "dst": by_partition(given["dst"], N),
        "type8": by_partition(given["edge_type_8"], 0),
        "type90": by_partition(given["edge_type_90"], 0),
        "attr": np.pad(given["edge_attr_16"], ((0, extra), (0, 0))).reshape(P, EP, FD),
        **{n: given[n] for n in _WEIGHTS},
    }
    nc = bacc.Bacc("TRN2", target_bir_lowering=False, num_devices=1)
    a = types.SimpleNamespace(**{
        n: nc.dram_tensor(f"in_{n}", list(v.shape), mybir.dt.from_np(v.dtype), kind="ExternalInput").ap()
        for n, v in arrays.items()})
    out = nc.dram_tensor("out", [NP, FD], F32, kind="ExternalOutput").ap()
    build(nc, a, out)
    r = run_bass_kernel_spmd(nc, [{f"in_{n}": np.ascontiguousarray(v) for n, v in arrays.items()}], core_ids=[0])
    return r.results[0]["out"][:N]
```

```python
from contextlib import ExitStack

import numpy as np

import concourse.bass as bass
from concourse import mybir

F32 = mybir.dt.float32
BF16 = mybir.dt.bfloat16
I32 = mybir.dt.int32
ALU = mybir.AluOpType
ACT = mybir.ActivationFunctionType
AX = mybir.AxisListType

P = 128
N, FD = 12500, 16
E = 412500
NT = -(-N // P)
NP = NT * P
J = 52
EP = 2 * J * -(-E // (P * 2 * J))
NCH = EP // J
EROWS = P * EP
XROWS = EROWS + NP
NSUM = 4
GT = 7
NG = NT // GT
R8, R90, NB = 8, 90, 30
BIG = 1.0e38
SLOPE = 0.2
SELU_SCALE, SELU_ALPHA = 1.0507009873554805, 1.6732632423543772
CSPLIT = 8
CROW = EP // CSPLIT


class Stage:

    def __init__(self, nc, name):
        self.nc, self.name, self.stack, self.sems = nc, name, ExitStack(), []
        self.credits = []

    def __enter__(self):
        return self

    def sb(self, name, shape, dt=F32):
        return self.stack.enter_context(self.nc.sbuf_tensor(f"{self.name}_{name}", shape, dt))

    def ps(self, name, shape):
        return self.stack.enter_context(self.nc.psum_tensor(f"{self.name}_{name}", shape, F32))

    def sem(self, name, credit=0):
        s = self.nc.alloc_semaphore(f"{self.name}_{name}")
        self.sems.append(s)
        if credit:
            self.credits.append((s, credit))
        return s

    def grant(self, eng):
        for s, credit in self.credits:
            eng.sem_inc(s, credit)

    def __exit__(self, *a):
        self.stack.close()
        if a[0] is None:
            self.nc.clear_and_free_semaphores(self.sems)
            self.nc.all_engine_barrier()


class Order:

    def __init__(self, eng, sem, base=0):
        self.eng, self.sem, self.base, self.n = eng, sem, base, 0

    def step(self, ins):
        self.n += 1
        ins.then_inc(self.sem, 1)

    def link(self, ins):
        self.step(ins)
        self.eng.wait_ge(self.sem, self.base + self.n)


def by_edge(table):
    return table[0:EROWS].rearrange("(p j) w -> p j w", p=P)


def by_node(table):
    return table.rearrange("(t p) w -> p t w", p=P)


def chunk(view, i, k):
    return view[:, bass.ds((i * 2 + k) * J, J)]


def rows(ap):
    return bass.IndirectOffsetOnAxis(ap=ap, axis=0)



def set_up(nc, a, g):
    with Stage(nc, "setup") as s:
        src_i, dst_i, t8_i, t90_i = (s.sb(n, [P, EP], I32) for n in ("src", "dst", "t8", "t90"))
        idx8, idx90 = s.sb("idx8", [P, EP], I32), s.sb("idx90", [P, EP], I32)
        src_f, dst_f, t8_f, keep = (s.sb(n, [P, EP]) for n in ("srcf", "dstf", "t8f", "keep"))
        lane, tile = s.sb("lane", [P, EP]), s.sb("tile", [P, EP])
        zero = s.sb("zero", [P, XROWS // P])
        iota_n, iota_j, iota_p = s.sb("ion", [P, NT], I32), s.sb("ioj", [P, P], I32), s.sb("iop", [P, 1], I32)
        loaded = [s.sem(f"loaded{n}") for n in range(5)]
        stored, iotas, zeroed, zero_ready, ready, dve_o, pool_o = (
            s.sem(n) for n in ("stored", "iotas", "zeroed", "zero_ready", "ready", "dve", "pool"))
        n_zero = len(g.to_zero)
        with nc.Block() as block:
            @block.sync
            def _(sp):
                for n, (dst, src) in enumerate(((dst_i, a.dst), (src_i, a.src), (t8_i, a.type8), (t90_i, a.type90))):
                    sp.dma_start(dst[:, :], src).then_inc(loaded[n], 16)
                sp.dma_start(g.x[:, :, :], by_node(a.x)).then_inc(loaded[4], 16)
                sp.wait_ge(zero_ready, 1)
                for table in g.to_zero:
                    n_rows, w = table.shape
                    flat = table.rearrange("(p m) w -> p (m w)", p=P)
                    m = n_rows // P
                    sp.dma_start(flat.rearrange("p (w m) -> p w m", w=w),
                                 zero[:, 0:m].unsqueeze(1).to_broadcast([P, w, m])).then_inc(zeroed, 16)
                sp.wait_ge(zeroed, 16 * n_zero)
                sp.wait_ge(loaded[4], 16)

            @block.gpsimd
            def _(pool):
                pool.iota(iota_n[:, :], pattern=[[P, NT]], base=0, channel_multiplier=1).then_inc(iotas, 1)
                pool.iota(iota_j[:, :], pattern=[[1, P]], base=0, channel_multiplier=0).then_inc(iotas, 1)
                pool.iota(iota_p[:, :], pattern=[[0, 1]], base=0, channel_multiplier=EP).then_inc(iotas, 1)
                pool.iota(g.first_row[:, :], pattern=[[0, 1]], base=0, channel_multiplier=EP).then_inc(iotas, 1)
                pool.iota(g.lane_i[:, :], pattern=[[0, 1]], base=0, channel_multiplier=1).then_inc(iotas, 1)
                pool.memset(g.ident[:, :], 0.0).then_inc(pool_o, 1)
                pool.wait_ge(pool_o, 1)
                pool.affine_select(out=g.ident[:, :], in_=g.ident[:, :], compare_op=ALU.not_equal, fill=1.0, base=0,
                                   pattern=[[-1, P]], channel_multiplier=1).then_inc(pool_o, 1)
                pool.memset(g.strict[:, :], 1.0).then_inc(pool_o, 1)
                pool.wait_ge(pool_o, 3)
                pool.affine_select(out=g.strict[:, :], in_=g.strict[:, :], compare_op=ALU.is_gt, fill=0.0, base=0,
                                   pattern=[[-1, P]], channel_multiplier=1).then_inc(pool_o, 1)

            @block.vector
            def _(dve):
                o = Order(dve, dve_o)
                dve.memset(zero[:, :], 0.0).then_inc(zero_ready, 1)
                dve.memset(keep[:, 0:1], 0.0)
                dve.wait_ge(iotas, 5)
                dve.tensor_copy(g.node_f[:, :], iota_n[:, :])
                dve.tensor_copy(g.count_f[:, :], iota_j[:, :])
                dve.tensor_copy(g.lane_f[:, :], g.lane_i[:, :])
                o.step(dve.tensor_copy(g.first_f[:, :], iota_p[:, :]))
                dve.wait_ge(loaded[0], 16)
                o.link(dve.tensor_copy(dst_f[:, :], dst_i[:, :]))
                dve.tensor_tensor(keep[:, 1:EP], dst_f[:, 1:EP], dst_f[:, 0:EP - 1], ALU.is_equal)
                dve.wait_ge(loaded[1], 16)
                o.step(dve.tensor_copy(src_f[:, :], src_i[:, :]))
                dve.tensor_scalar(idx8[:, :], src_i[:, :], P - 1, None, ALU.bitwise_and)
                o.link(dve.tensor_scalar(idx90[:, :], src_i[:, :], 7, None, ALU.logical_shift_right))
                dve.tensor_copy(lane[:, :], idx8[:, :])
                o.link(dve.tensor_copy(tile[:, :], idx90[:, :]))
                dve.wait_ge(loaded[2], 16)
                dve.tensor_copy(t8_f[:, :], t8_i[:, :])
                dve.scalar_tensor_tensor(idx8[:, :], src_i[:, :], float(R8), t8_i[:, :], ALU.mult, ALU.add)
                dve.wait_ge(loaded[3], 16)
                dve.scalar_tensor_tensor(idx90[:, :], src_i[:, :], float(R90), t90_i[:, :], ALU.mult,
                                         ALU.add).then_inc(ready, 1)

            @block.scalar
            def _(act):
                act.wait_ge(ready, 1)
                pairs = ((g.keep_d, keep), (g.dst_d, dst_f), (g.src_fd, src_f), (g.type8_d, t8_f), (g.lane_d, lane),
                         (g.tile_d, tile), (g.idx8_d, idx8),
                         (g.idx90_d, idx90))
                for dram, values in pairs:
                    act.dma_start(dram, values[:, :]).then_inc(stored, 16)
                act.wait_ge(stored, 16 * len(pairs))


def gather_by_node(nc, g, name, table, index, width, consume, per_turn):
    with Stage(nc, name) as s:
        got_rows = [s.sb(f"rows{k}", [P, GT, width]) for k in range(2)]
        row_g = [s.sb(f"index{k}", [P, GT], I32) for k in range(2)]
        dve_o = s.sem("dve")
        staged = [s.sem(f"staged{k}") for k in range(2)]
        got = [s.sem(f"got{k}") for k in range(2)]
        with nc.Block() as block:
            @block.gpsimd
            def _(pool):
                with pool.Fori(0, NG // 2) as i:
                    for k in range(2):
                        pool.wait_ge(staged[k], i + 1)
                        pool.sem_inc(g.gate, 1)
                        for c in range(GT):
                            pool.indirect_dma_start(got_rows[k][:, c, :], None, table, rows(row_g[k][:, c:c + 1]))\
                                .then_inc(got[k], 16)

            @block.vector
            def _(dve):
                with dve.Fori(0, NG // 2) as i:
                    o = Order(dve, dve_o, i * per_turn)
                    for k in range(2):
                        dve.tensor_copy(row_g[k][:, :], index[:, bass.ds((i * 2 + k) * GT, GT)])\
                            .then_inc(staged[k], 1)
                    for k in range(2):
                        dve.wait_ge(got[k], i * (16 * GT) + 16 * GT)
                        consume(dve, o, i * 2 + k, got_rows[k])
                    assert o.n == per_turn, (name, o.n)


def gather_to(nc, g, name, table, index, width, into):
    def copy(dve, o, group, rows_):
        o.link(dve.tensor_copy(into[:, bass.ds(group * GT, GT), 0:width], rows_[:, :, :]))
    gather_by_node(nc, g, name, table, index, width, copy, 2)


def node_ranges(nc, g):
    n_rows = P * CSPLIT
    dst_rows = g.dst_d.rearrange("p (k c) -> (p k) c", k=CSPLIT)
    with Stage(nc, "ranges") as r:
        cnt, row_f, row_i = r.sb("cnt", [P, NT]), r.sb("rowf", [P, NT]), r.sb("rowi", [P, NT], I32)
        node_g, cnt_g, seen = r.sb("node", [P, GT]), r.sb("cntg", [P, GT]), r.sb("seen", [P, n_rows])

        with Stage(nc, "heads") as s:
            line, ones = s.sb("line", [1, n_rows]), s.sb("ones", [1, P])
            heads, heads_ps = s.sb("heads", [P, n_rows]), s.ps("headsp", [P, n_rows])
            in_, ones_ready, spread_, dve_o = s.sem("in"), s.sem("ones_ready"), s.sem("spread"), s.sem("dve")
            with nc.Block() as block:
                @block.sync
                def _(sp):
                    with nc.allow_non_contiguous_dma(reason="one word of each row, once"):
                        sp.dma_start(line[:, :], dst_rows[:, 0:1].rearrange("r c -> c r")).then_inc(in_, 16)

                @block.tensor
                def _(pe):
                    pe.wait_ge(ones_ready, 1)
                    pe.wait_ge(in_, 16)
                    for c in range(0, n_rows, 512):
                        last = pe.matmul(heads_ps[:, c:c + 512], ones[:, :], line[:, c:c + 512], start=True, stop=True)
                    last.then_inc(spread_, 1)

                @block.vector
                def _(dve):
                    dve.memset(ones[:, :], 1.0).then_inc(ones_ready, 1)
                    dve.wait_ge(spread_, 1)
                    Order(dve, dve_o).link(dve.tensor_copy(heads[:, :], heads_ps[:, :]))
                    with dve.Fori(0, NG) as i:
                        o = Order(dve, dve_o, i * (GT + 2) + 1)
                        o.link(dve.tensor_copy(node_g[:, :], g.node_f[:, bass.ds(i * GT, GT)]))
                        for c in range(GT):
                            o.link(dve.tensor_scalar(seen[:, :], heads[:, :], node_g[:, c:c + 1], None, ALU.is_le,
                                                     ALU.add, accum_out=cnt_g[:, c:c + 1]))
                        o.link(dve.tensor_copy(cnt[:, bass.ds(i * GT, GT)], cnt_g[:, :]))
                    o = Order(dve, dve_o, NG * (GT + 2) + 1)
                    o.link(dve.tensor_scalar(row_f[:, :], cnt[:, :], -1.0, 0.0, ALU.add, ALU.max))
                    dve.tensor_copy(row_i[:, :], row_f[:, :])

        def count(dve, o, group, rows_):
            o.link(dve.tensor_copy(node_g[:, :], g.node_f[:, bass.ds(group * GT, GT)]))
            for c in range(GT):
                o.link(dve.tensor_scalar(seen[:, 0:CROW], rows_[:, c, :], node_g[:, c:c + 1], None, ALU.is_le,
                                         ALU.add, accum_out=cnt_g[:, c:c + 1]))
            o.link(dve.tensor_copy(cnt[:, bass.ds(group * GT, GT)], cnt_g[:, :]))
        gather_by_node(nc, g, "count", dst_rows, row_i, CROW, count, 2 * (GT + 2))

        with Stage(nc, "limits") as s:
            total, before, t = s.sb("total", [P, NT]), s.sb("before", [P, NT]), s.sb("t", [P, NT])
            zero = s.sb("zero", [1, 1])
            d_first, d_prev, d_row = s.sb("dfirst", [P, 1]), s.sb("dprev", [P, 1]), s.sb("drow", [1, P + 1])
            after_first, t_first, fix, ins_ = (s.sb("af", [P, 1], I32), s.sb("tf", [P, 1]), s.sb("fix", [P, 1]),
                                               s.sb("ins", [P, 1]))
            dump_f, dump_n, t1 = s.sb("dump", [P, 1]), s.sb("dumpn", [P, NT]), s.sb("t1", [P, 1])
            dve_o, cleared, ends_in, totalled, stored, before_in, asked, first_total = (
                s.sem(n) for n in ("dve", "cleared", "ends_in", "totalled", "stored", "before_in", "asked",
                                   "first_total"))
            with nc.Block() as block:
                @block.sync
                def _(sp):
                    with nc.allow_non_contiguous_dma(reason="one word per partition or node, once"):
                        sp.wait_ge(cleared, 1)
                        sp.dma_start(d_first[:, :], g.dst_d[:, 0:1]).then_inc(ends_in, 16)
                        sp.dma_start(d_prev[1:P, :], g.dst_d[0:P - 1, EP - 1:EP]).then_inc(ends_in, 16)
                        sp.dma_start(d_row[:, 1:P + 1], g.dst_d[:, EP - 1:EP].rearrange("p o -> o p"))\
                          .then_inc(ends_in, 16)
                        sp.wait_ge(totalled, 1)
                        sp.dma_start(g.total_d[1:NP + 1].rearrange("(t p) o -> p (t o)", p=P), total[:, :])\
                          .then_inc(stored, 16)
                        sp.dma_start(g.total_d[0:1], zero[:, :]).then_inc(stored, 16)
                        sp.wait_ge(stored, 32)
                        sp.dma_start(before[:, :], g.total_d[0:NP].rearrange("(t p) o -> p (t o)", p=P))\
                          .then_inc(before_in, 16)

                @block.gpsimd
                def _(pool):
                    pool.wait_ge(asked, 1)
                    pool.wait_ge(stored, 32)
                    pool.sem_inc(g.gate, 1)
                    pool.indirect_dma_start(t_first[:, :], None, g.total_d, rows(after_first[:, :]))\
                        .then_inc(first_total, 16)

                @block.vector
                def _(dve):
                    o = Order(dve, dve_o)
                    dve.memset(zero[:, :], 0.0)
                    dve.memset(d_row[:, 0:1], -1.0)
                    dve.memset(d_prev[:, :], -1.0).then_inc(cleared, 1)
                    o.link(dve.scalar_tensor_tensor(total[:, :], row_f[:, :], float(CROW), cnt[:, :], ALU.mult,
                                                    ALU.add))
                    dve.tensor_copy(t[:, :], total[:, :]).then_inc(totalled, 1)
                    dve.wait_ge(ends_in, 48)
                    o.link(dve.tensor_scalar(t1[:, :], d_first[:, :], 1.0, None, ALU.add))
                    dve.tensor_copy(after_first[:, :], t1[:, :]).then_inc(asked, 1)
                    dve.tensor_copy(g.dst_first[:, :], d_first[:, :])
                    dve.tensor_tensor(g.joined[:, :], d_row[:, 1:P + 1], d_row[:, 0:P], ALU.is_equal)
                    o.link(dve.tensor_scalar(t[:, :], total[:, :], -1.0, 0.0, ALU.add, ALU.max))
                    dve.tensor_copy(g.last_row[:, :], t[:, :])
                    dve.wait_ge(before_in, 16)
                    o.link(dve.tensor_tensor(g.has[:, :], total[:, :], before[:, :], ALU.is_gt))
                    o.link(dve.tensor_tensor(g.deg[:, :], total[:, :], before[:, :], ALU.subtract))
                    o.link(dve.tensor_scalar(dump_f[:, :], g.lane_f[:, :], float(EROWS), None, ALU.add))
                    o.link(dve.tensor_scalar(dump_n[:, :], g.node_f[:, :], float(EROWS), None, ALU.add))
                    o.link(dve.tensor_tensor(before[:, :], before[:, :], dump_n[:, :], ALU.subtract))
                    o.link(dve.tensor_tensor(before[:, :], before[:, :], g.has[:, :], ALU.mult))
                    o.link(dve.tensor_tensor(before[:, :], before[:, :], dump_n[:, :], ALU.add))
                    dve.tensor_copy(g.start_row[:, :], before[:, :])
                    dve.wait_ge(first_total, 16)
                    o.link(dve.tensor_tensor(fix[:, :], d_first[:, :], d_prev[:, :], ALU.is_equal))
                    o.link(dve.tensor_scalar(t1[:, :], g.first_f[:, :], float(EP), None, ALU.add))
                    o.link(dve.tensor_tensor(ins_[:, :], t_first[:, :], t1[:, :], ALU.is_le))
                    o.link(dve.tensor_tensor(fix[:, :], fix[:, :], ins_[:, :], ALU.mult))
                    for base, row in ((g.first_f, g.mend_from), (dump_f, g.mend_to)):
                        o.link(dve.scalar_tensor_tensor(t1[:, :], t_first[:, :], -1.0, base[:, :], ALU.add,
                                                        ALU.subtract))
                        o.link(dve.tensor_tensor(t1[:, :], t1[:, :], fix[:, :], ALU.mult))
                        o.link(dve.tensor_tensor(t1[:, :], t1[:, :], base[:, :], ALU.add))
                        o.link(dve.tensor_copy(row[:, :], t1[:, :]))



def project(nc, g, name, x, width, weights, cols, table=None, keep=None, put=None, dt=F32):
    if cols <= 512:
        T, per_bank = GT, 512 // cols
        pieces = [(c, c // per_bank, c % per_bank * cols, 0, cols) for c in range(T)]
    else:
        T, most = 1, -(-cols // -(-cols // 512))
        pieces = [(0, n, 0, c, min(most, cols - c)) for n, c in enumerate(range(0, cols, most))]
    banks = pieces[-1][1] + 1
    turns = NT // T // 2
    kw = keep[0].shape[2] if keep is not None else 0
    values, expand, node_table = put or (None, None, None)
    put_kept = put is not None and values is keep[0]
    with Stage(nc, name) as s:
        rows_in = [s.sb(f"x{k}", [P, T, width]) for k in range(2)]
        turned = [s.sb(f"xt{k}", [width, T * P], dt) for k in range(2)]
        rows_out = [s.sb(f"y{k}", [P, T, cols]) for k in range(2)]
        xt_ps = [s.ps(f"xtp{n}", [P, 512]) for n in range(-(-T // 4))]
        y_ps = [[s.ps(f"yp{k}{n}", [P, 512]) for n in range(banks)] for k in range(2)]
        staged, turned_ps, turned_sb, product, copied, stored = (
            [s.sem(f"{n}{k}", c) for k in range(2)] for n, c in
            (("staged", 0), ("tps", 0), ("tsb", 1), ("product", 1), ("copied", 1), ("stored", 16)))
        dve_o, by_node_out = s.sem("dve"), s.sem("by_node_out")
        if expand is not None:
            vw = values.shape[2]
            to_put = [s.sb(f"v{k}", [P, T, vw]) for k in range(2)]
            row_g = [s.sb(f"row{k}", [P, T], I32) for k in range(2)]
            first = s.sb("first", [P, node_table.shape[1]])
            first_v = s.sb("firstv", [P, vw])
            got, ready, put_first = s.sem("got"), s.sem("ready"), s.sem("put_first")
            to_put_ready = [s.sem(f"to_put{k}") for k in range(2)]
            out = [s.sem(f"out{k}") for k in range(2)]
        with nc.Block() as block:
            @block.vector
            def _(dve):
                def stage(i, k):
                    dve.tensor_copy(rows_in[k][:, :, :], x[:, bass.ds((i * 2 + k) * T, T), 0:width])\
                        .then_inc(staged[k], 1)

                def turn(i, first=False, last=False):
                    o = Order(dve, dve_o, i * 2)
                    for k in range(2):
                        grp = bass.ds((i * 2 + k) * T, T)
                        dve.wait_ge(product[k], i + 2)
                        if not last:
                            stage(i + 1, k)
                        dve.wait_ge(stored[k], i * 16 + 16)
                        if expand is not None and not first:
                            dve.wait_ge(out[k], i * (16 * T))
                        for n in range(banks):
                            part = [p for p in pieces if p[1] == n]
                            if T == 1:
                                _, _, _, c, w = part[0]
                                ins = dve.tensor_copy(rows_out[k][:, 0, c:c + w], y_ps[k][n][:, 0:w])
                            else:
                                t0, m = part[0][0], len(part)
                                ins = dve.tensor_copy(
                                    rows_out[k][:, t0:t0 + m, :],
                                    y_ps[k][n][:, 0:m * cols].rearrange("p (t c) -> p t c", t=m))
                        if keep is None:
                            ins.then_inc(copied[k], 1)
                            continue
                        o.link(ins)
                        into, c0 = keep
                        kept = rows_out[k][:, :, c0:c0 + kw]
                        dve.tensor_copy(into[:, grp, :], kept).then_inc(copied[k], 1)
                        if expand is not None:
                            dve.tensor_copy(row_g[k][:, :], g.start_row[:, grp])
                            dve.tensor_copy(to_put[k][:, :, :], kept if put_kept else values[:, grp, :])\
                                .then_inc(to_put_ready[k], 1)
                for k in range(2):
                    stage(0, k)
                turn(0, first=True)
                with dve.Fori(1, turns - 1) as i:
                    turn(i)
                turn(turns - 1, last=True)
                if expand is not None:
                    dve.wait_ge(got, 16)
                    dve.tensor_copy(first_v[:, :], first[:, node_table.shape[1] - vw:]).then_inc(ready, 1)

            @block.tensor
            def _(pe):
                def turn_group(i, k):
                    pe.wait_ge(staged[k], i + 1)
                    for t in range(T):
                        last = pe.transpose(xt_ps[t // 4][0:width, t % 4 * P:(t % 4 + 1) * P],
                                            rows_in[k][:, t, :], g.ident[:, :])
                    last.then_inc(turned_ps[k], 1)

                def turn(i, last=False):
                    for k in range(2):
                        pe.wait_ge(turned_sb[k], i + 2)
                        if k == 0 or not last:
                            turn_group(i + k, 1 - k)
                        pe.wait_ge(copied[k], i + 1)
                        for t, n, at, c, w in pieces:
                            ins = pe.matmul(y_ps[k][n][:, at:at + w], turned[k][:, t * P:(t + 1) * P],
                                            weights[0:width, c:c + w], start=True, stop=True)
                        ins.then_inc(product[k], 1)
                turn_group(0, 0)
                with pe.Fori(0, turns - 1) as i:
                    turn(i)
                turn(turns - 1, last=True)

            @block.scalar
            def _(act):
                with act.Fori(0, turns) as i:
                    for k in range(2):
                        act.wait_ge(turned_ps[k], i + 1)
                        act.wait_ge(product[k], i + 1)
                        for n in range(len(xt_ps)):
                            w = min(4, T - 4 * n) * P
                            last = act.copy(turned[k][:, n * 4 * P:n * 4 * P + w], xt_ps[n][0:width, 0:w])
                        last.then_inc(turned_sb[k], 1)

            @block.sync
            def _(sp):
                s.grant(sp)
                with sp.Fori(0, turns) as i:
                    for k in range(2):
                        sp.wait_ge(copied[k], i + 2)
                        if table is None:
                            sp.sem_inc(stored[k], 16)
                        else:
                            sp.dma_start(by_node(table)[:, bass.ds((i * 2 + k) * T, T), :],
                                         rows_out[k][:, :, 0:table.shape[1]]).then_inc(stored[k], 16)
                for k in range(2):
                    sp.wait_ge(stored[k], 16 * turns + 16)
                if put_kept and node_table is not table:
                    with nc.allow_non_contiguous_dma(reason="one word per node, once"):
                        sp.dma_start(by_node(node_table), keep[0][:, :, :]).then_inc(by_node_out, 16)
                        sp.wait_ge(by_node_out, 16)

            @block.gpsimd
            def _(pool):
                if expand is None:
                    return
                with pool.Fori(0, turns) as i:
                    for k in range(2):
                        pool.wait_ge(to_put_ready[k], i + 1)
                        pool.sem_inc(g.gate, 1)
                        for t in range(T):
                            pool.indirect_dma_start(expand, rows(row_g[k][:, t:t + 1]), to_put[k][:, t, :], None)\
                                .then_inc(out[k], 16)
                for k in range(2):
                    pool.wait_ge(stored[k], 16 * turns + 16)
                    pool.wait_ge(out[k], 16 * T * turns)
                if put_kept and node_table is not table:
                    pool.wait_ge(by_node_out, 16)
                pool.sem_inc(g.gate, 1)
                pool.indirect_dma_start(first[:, :], None, node_table, rows(g.dst_first[:, :])).then_inc(got, 16)
                pool.wait_ge(ready, 1)
                pool.indirect_dma_start(expand, rows(g.first_row[:, :]), first_v[:, :], None).then_inc(put_first, 16)
                pool.wait_ge(put_first, 16)


def spread(nc, g, name, values, node_table, expand, width):
    w_t = node_table.shape[1]
    with Stage(nc, name) as s:
        vals = [s.sb(f"v{k}", [P, GT, width]) for k in range(2)]
        row_g = [s.sb(f"row{k}", [P, GT], I32) for k in range(2)]
        first = s.sb("first", [P, w_t])
        first_v = s.sb("firstv", [P, width])
        got, ready, put = s.sem("got"), s.sem("ready"), s.sem("put")
        staged = [s.sem(f"staged{k}") for k in range(2)]
        out = [s.sem(f"out{k}") for k in range(2)]
        with nc.Block() as block:
            @block.vector
            def _(dve):
                def turn(i, first):
                    for k in range(2):
                        if not first:
                            dve.wait_ge(out[k], i * (16 * GT))
                        grp = bass.ds((i * 2 + k) * GT, GT)
                        dve.tensor_copy(row_g[k][:, :], g.start_row[:, grp])
                        dve.tensor_copy(vals[k][:, :, :], values[:, grp, :]).then_inc(staged[k], 1)
                turn(0, True)
                with dve.Fori(1, NG // 2) as i:
                    turn(i, False)
                dve.wait_ge(got, 16)
                dve.tensor_copy(first_v[:, :], first[:, w_t - width:w_t]).then_inc(ready, 1)

            @block.gpsimd
            def _(pool):
                pool.indirect_dma_start(first[:, :], None, node_table, rows(g.dst_first[:, :])).then_inc(got, 16)
                with pool.Fori(0, NG // 2) as i:
                    for k in range(2):
                        pool.wait_ge(staged[k], i + 1)
                        pool.sem_inc(g.gate, 1)
                        for c in range(GT):
                            pool.indirect_dma_start(expand, rows(row_g[k][:, c:c + 1]), vals[k][:, c, :], None)\
                                .then_inc(out[k], 16)
                for k in range(2):
                    pool.wait_ge(out[k], 16 * GT * (NG // 2))
                pool.wait_ge(ready, 1)
                pool.indirect_dma_start(expand, rows(g.first_row[:, :]), first_v[:, :], None).then_inc(put, 16)
                pool.wait_ge(put, 16)




def scan_sum(dve, out, keep, values, before):
    return dve.tensor_tensor_scan(out, keep, values, before, ALU.mult, ALU.add)


def scan_max(dve, out, penalty, values, before):
    return dve.tensor_tensor_scan(out, penalty, values, before, ALU.add, ALU.max)


class EdgeBuffers:

    def __init__(self, s, g, table_w, index_d, extras, sums_w):
        self.index_d, self.extras = index_d, extras
        self.rows = [s.sb(f"rows{k}", [P, J, table_w]) for k in range(2)]
        self.index = [s.sb(f"index{k}", [P, J], I32) for k in range(2)]
        self.extra = [[s.sb(f"extra{n}{k}", [P, J, e.shape[2]]) for n, e in enumerate(extras)] for k in range(2)]
        self.keep = [e[0][:, :, :].rearrange("p j o -> p (j o)") for e in self.extra]
        self.sums = [s.sb(f"sums{k}", [P, J, sums_w]) for k in range(2)]
        self.index_in, self.extra_in, self.gathered, self.used, self.done, self.stored = (
            [s.sem(f"{n}{k}", c) for k in range(2)] for n, c in
            (("index_in", 0), ("extra_in", 0), ("gathered", 0), ("used", 0), ("done", 1), ("stored", 16)))
        self.stage = s

    def load(self, sp):
        self.stage.grant(sp)

        def turn(i, first):
            for k in range(2):
                if not first:
                    sp.wait_ge(self.gathered[k], i * (16 * J))
                sp.dma_start(self.index[k][:, :], chunk(self.index_d, i, k)).then_inc(self.index_in[k], 16)
                sp.wait_ge(self.done[k], i + 1)
                for n, e in enumerate(self.extras):
                    sp.dma_start(self.extra[k][n][:, :, :], chunk(e, i, k)).then_inc(self.extra_in[k], 16)
        turn(0, True)
        with sp.Fori(1, NCH // 2) as i:
            turn(i, False)

    def wait_to_gather(self, pool, turn, k):
        pool.wait_ge(self.done[k], turn + 1)
        pool.wait_ge(self.index_in[k], turn * 16 + 16)

    def gather_column(self, pool, table, k, j):
        pool.indirect_dma_start(self.rows[k][:, j, :], None, table, rows(self.index[k][:, j:j + 1]))\
            .then_inc(self.gathered[k], 16)

    def gather_chunk(self, pool, g, table, turn, k):
        self.wait_to_gather(pool, turn, k)
        pool.sem_inc(g.gate, 1)
        for j in range(J):
            self.gather_column(pool, table, k, j)

    def gather(self, pool, g, table):
        with pool.Fori(0, NCH // 2) as i:
            for k in range(2):
                self.gather_chunk(pool, g, table, i, k)

    def store_chunk(self, act, acc, i, k):
        act.wait_ge(self.done[k], i + 2)
        act.dma_start(chunk(acc, i, k), self.sums[k][:, :, :]).then_inc(self.stored[k], 16)

    def all_stored(self, act):
        for k in range(2):
            act.wait_ge(self.stored[k], 16 * (NCH // 2) + 16)

    def wait_rows(self, dve, i, k):
        dve.wait_ge(self.gathered[k], i * (16 * J) + 16 * J)

    def wait_extra(self, dve, i, k):
        dve.wait_ge(self.extra_in[k], (i + 1) * (16 * len(self.extras)))


def attention_pass(nc, g, name, heads, width, table, expand, sums_d, kinds=False, to_zero=()):
    by_edge_z, by_source_z = to_zero or ((), ())
    hw = heads * width
    sw = hw + 2 * heads
    with Stage(nc, name) as s:
        b = EdgeBuffers(s, g, sw, g.src_id, [by_edge(t) for t in (g.keep_t, expand, g.type8_t)[:3 if kinds else 2]],
                        sums_d.shape[1])
        hot = s.sb("hot", [P, J, R8]) if kinds else None
        dst_part = [s.sb(f"dst{k}", [P, J, heads]) for k in range(2)]
        top = [s.sb(f"top{k}", [P, J + 1, heads]) for k in range(2)]
        e_, penalty = s.sb("e", [P, J, heads]), s.sb("penalty", [P, J])
        drop, factor = s.sb("drop", [P, 2, J, heads]), s.sb("factor", [P, 2, J, heads])
        dve_o = s.sem("dve")
        dropped, raised = [s.sem(f"dropped{k}") for k in range(2)], [s.sem(f"raised{k}") for k in range(2)]
        acc = by_edge(sums_d)
        if to_zero:
            zero = s.sb("zero", [P, max([NT * t.shape[1] for t in by_edge_z] +
                                        [t.shape[0] * t.shape[1] // P for t in by_source_z])])
            zero_ready, zeroed_whole, zeroed = s.sem("zero_ready"), s.sem("zeroed_whole"), s.sem("zeroed")
        with nc.Block() as block:
            @block.sync
            def _(sp):
                b.load(sp)

            @block.gpsimd
            def _(pool):
                b.gather(pool, g, table)

            @block.vector
            def _(dve):
                o = Order(dve, dve_o)
                dve.memset(dst_part[1][:, J - 1, :], 0.0)
                dve.memset(top[1][:, J, :], 0.0)
                if to_zero:
                    dve.memset(zero[:, :], 0.0).then_inc(zero_ready, 1)
                o.link(dve.memset(b.sums[1][:, J - 1, :], 0.0))
                with dve.Fori(0, NCH // 2) as i:
                    per = 16 if kinds else 14
                    o = Order(dve, dve_o, i * per + 1)
                    for k in range(2):
                        keep, rows_, sums = b.keep[k], b.rows[k], b.sums[k]
                        before = b.sums[1 - k]
                        b.wait_extra(dve, i, k)
                        for h in range(heads):
                            scan_sum(dve, dst_part[k][:, :, h], keep, b.extra[k][1][:, :, h],
                                     dst_part[1 - k][:, J - 1, h:h + 1])
                        dve.tensor_scalar(penalty[:, :], keep, -1.0, BIG, ALU.add, ALU.mult)
                        if kinds:
                            kind = b.extra[k][2][:, :, :].rearrange("p j o -> p (j o)")
                            o.step(dve.tensor_tensor(hot[:, :, :],
                                                     g.count_f[:, 0:R8].unsqueeze(1).to_broadcast([P, J, R8]),
                                                     kind.unsqueeze(2).to_broadcast([P, J, R8]), ALU.is_equal))
                        o.link(dve.tensor_copy(top[k][:, 0, :], top[1 - k][:, J, :]))
                        b.wait_rows(dve, i, k)
                        o.link(dve.tensor_tensor(e_[:, :, :], rows_[:, :, hw:hw + heads], dst_part[k][:, :, :],
                                                 ALU.add))
                        o.link(dve.scalar_tensor_tensor(e_[:, :, :], e_[:, :, :], SLOPE, e_[:, :, :], ALU.mult,
                                                        ALU.max))
                        for h in range(heads):
                            last = scan_max(dve, top[k][:, 1:J + 1, h], penalty[:, :], e_[:, :, h],
                                            top[k][:, 0, h:h + 1])
                        o.link(last)
                        dve.tensor_tensor(drop[:, 1, :, :], e_[:, :, :], top[k][:, 1:J + 1, :], ALU.subtract)
                        o.link(dve.tensor_tensor(drop[:, 0, :, :], top[k][:, 0:J, :], top[k][:, 1:J + 1, :],
                                                 ALU.subtract))
                        dve.tensor_scalar(drop[:, 0, :, :], drop[:, 0, :, :], 0.0, None, ALU.min)\
                            .then_inc(dropped[k], 1)
                        dve.wait_ge(raised[k], i + 1)
                        o.link(dve.tensor_tensor(factor[:, 0, :, :], factor[:, 0, :, :],
                                                 keep.unsqueeze(2).to_broadcast([P, J, heads]), ALU.mult))
                        shaped = rows_[:, :, 0:hw].rearrange("p j (h c) -> p j h c", h=heads)
                        o.link(dve.tensor_tensor(shaped, shaped, factor[:, 1, :, :].unsqueeze(3)
                                                 .to_broadcast([P, J, heads, width]), ALU.mult))
                        dve.wait_ge(b.stored[k], i * 16 + 16)
                        dve.tensor_copy(sums[:, :, hw + heads:sw], top[k][:, 1:J + 1, :])
                        for r in range(R8 if kinds else 0):
                            scan_sum(dve, sums[:, :, sw + r], keep, hot[:, :, r], before[:, J - 1, sw + r:sw + r + 1])
                        for h in range(heads):
                            decay = factor[:, 0, :, h]
                            c = hw + h
                            scan_sum(dve, sums[:, :, c], decay, factor[:, 1, :, h], before[:, J - 1, c:c + 1])
                            for c in range(h * width, (h + 1) * width):
                                last = scan_sum(dve, sums[:, :, c], decay, rows_[:, :, c], before[:, J - 1, c:c + 1])
                        last.then_inc(b.done[k], 1)
                        dve.wait_ge(b.done[k], i + 2)
                    assert o.n == per, o.n

            @block.scalar
            def _(act):
                if to_zero:
                    act.wait_ge(zero_ready, 1)
                    whole = [*by_source_z, *(t[EROWS:XROWS] for t in by_edge_z)]
                    for t in whole:
                        act.dma_start(t.rearrange("(p m) w -> p (m w)", p=P), zero[:, 0:t.shape[0] * t.shape[1] // P])\
                            .then_inc(zeroed_whole, 16)
                with act.Fori(0, NCH // 2) as i:
                    for k in range(2):
                        act.wait_ge(dropped[k], i + 1)
                        act.activation(factor[:, :, :, :], drop[:, :, :, :], ACT.Exp).then_inc(raised[k], 1)
                        b.store_chunk(act, acc, i, k)
                        for t in by_edge_z:
                            w = t.shape[1]
                            act.dma_start(chunk(by_edge(t), i, k), zero[:, 0:J * w].rearrange("p (j w) -> p j w", w=w))\
                                .then_inc(zeroed, 16)
                b.all_stored(act)
                if to_zero:
                    act.wait_ge(zeroed_whole, 16 * len(whole))
                    act.wait_ge(zeroed, 16 * NCH * len(by_edge_z))


def carry_over(nc, g, name, sums_d, heads=0, per=0):
    acc = by_edge(sums_d)
    width = sums_d.shape[1]
    hw = heads * per
    sw = hw + 2 * heads
    with Stage(nc, name) as s:
        line = s.sb("line", [1, P, width])
        own, from_before = s.sb("own", [P, width]), s.sb("before", [P, width])
        top = s.sb("top", [1, P + 1, max(heads, 1)])
        penalty, drop, factor = (s.sb("penalty", [1, P]), s.sb("drop", [1, 2, P, max(heads, 1)]),
                                 s.sb("factor", [1, 2, P, max(heads, 1)]))
        top2, drop2, factor2 = (s.sb("top2", [P, max(heads, 1)]), s.sb("drop2", [P, 2, max(heads, 1)]),
                                s.sb("factor2", [P, 2, max(heads, 1)]))
        line_in, dve_o, scanned, line_out, before_in, cleared, own_in, mended, put, dropped, raised = (
            s.sem(n) for n in ("line_in", "dve", "scanned", "line_out", "before_in", "cleared", "own_in", "mended",
                               "put", "dropped", "raised"))
        carry = g.carry_d[:, 0:width]
        joined = g.joined[:, :]
        with nc.Block() as block:
            @block.sync
            def _(sp):
                sp.dma_start(line[:, :, :], acc[:, EP - 1:EP, :].rearrange("p o w -> o p w")).then_inc(line_in, 16)
                sp.wait_ge(scanned, 1)
                sp.dma_start(carry[1:P, :].unsqueeze(0), line[:, 0:P - 1, :]).then_inc(line_out, 16)
                sp.wait_ge(line_out, 16)
                sp.wait_ge(cleared, 1)
                sp.dma_start(from_before[1:P, :], carry[1:P, :]).then_inc(before_in, 16)

            @block.gpsimd
            def _(pool):
                pool.indirect_dma_start(own[:, :], None, sums_d, rows(g.mend_from[:, :])).then_inc(own_in, 16)
                pool.wait_ge(mended, 1)
                pool.indirect_dma_start(sums_d, rows(g.mend_to[:, :]), own[:, :], None).then_inc(put, 16)
                pool.wait_ge(put, 16)

            @block.vector
            def _(dve):
                o = Order(dve, dve_o)
                dve.memset(from_before[:, :], 0.0).then_inc(cleared, 1)
                dve.wait_ge(line_in, 16)
                for c in range(sw, width):
                    last = scan_sum(dve, line[:, :, c], joined, line[:, :, c], 0.0)
                if not heads:
                    last.then_inc(scanned, 1)
                    dve.wait_ge(own_in, 16)
                    dve.wait_ge(before_in, 16)
                    dve.tensor_tensor(own[:, :], own[:, :], from_before[:, :], ALU.add).then_inc(mended, 1)
                    return
                dve.tensor_scalar(penalty[:, :], joined, -1.0, BIG, ALU.add, ALU.mult)
                o.link(dve.memset(top[:, 0, :], 0.0))
                for h in range(heads):
                    last = scan_max(dve, top[:, 1:P + 1, h], penalty[:, :], line[:, :, hw + heads + h], 0.0)
                o.link(last)
                dve.tensor_tensor(drop[:, 1, :, :], line[:, :, hw + heads:sw], top[:, 1:P + 1, :], ALU.subtract)
                o.link(dve.tensor_tensor(drop[:, 0, :, :], top[:, 0:P, :], top[:, 1:P + 1, :], ALU.subtract))
                dve.tensor_scalar(drop[:, 0, :, :], drop[:, 0, :, :], 0.0, None, ALU.min).then_inc(dropped, 1)
                dve.wait_ge(raised, 1)
                dve.tensor_tensor(factor[:, 0, :, :], factor[:, 0, :, :],
                                  joined.unsqueeze(2).to_broadcast([1, P, heads]), ALU.mult)
                shaped = line[:, :, 0:hw].rearrange("o p (h c) -> o p h c", h=heads)
                dve.tensor_tensor(shaped, shaped, factor[:, 1, :, :].unsqueeze(3).to_broadcast([1, P, heads, per]),
                                  ALU.mult)
                dve.tensor_copy(line[:, :, hw + heads:sw], top[:, 1:P + 1, :])
                o.link(dve.tensor_tensor(line[:, :, hw:hw + heads], line[:, :, hw:hw + heads], factor[:, 1, :, :],
                                         ALU.mult))
                for h in range(heads):
                    for c in [hw + h, *range(h * per, (h + 1) * per)]:
                        last = scan_sum(dve, line[:, :, c], factor[:, 0, :, h], line[:, :, c], 0.0)
                last.then_inc(scanned, 1)
                dve.wait_ge(own_in, 16)
                dve.wait_ge(before_in, 16)
                o.link(dve.tensor_tensor(top2[:, :], own[:, hw + heads:sw], from_before[:, hw + heads:sw], ALU.max))
                dve.tensor_tensor(drop2[:, 0, :], own[:, hw + heads:sw], top2[:, :], ALU.subtract)
                dve.tensor_tensor(drop2[:, 1, :], from_before[:, hw + heads:sw], top2[:, :], ALU.subtract)\
                    .then_inc(dropped, 1)
                dve.wait_ge(raised, 2)
                for n, t in enumerate((own, from_before)):
                    shaped = t[:, 0:hw].rearrange("p (h c) -> p h c", h=heads)
                    dve.tensor_tensor(shaped, shaped, factor2[:, n, :].unsqueeze(2).to_broadcast([P, heads, per]),
                                      ALU.mult)
                    last = dve.tensor_tensor(t[:, hw:hw + heads], t[:, hw:hw + heads], factor2[:, n, :], ALU.mult)
                o.link(last)
                dve.tensor_copy(own[:, hw + heads:sw], top2[:, :])
                if width > sw:
                    dve.tensor_tensor(own[:, sw:], own[:, sw:], from_before[:, sw:], ALU.add)
                dve.tensor_tensor(own[:, 0:hw + heads], own[:, 0:hw + heads], from_before[:, 0:hw + heads], ALU.add)\
                    .then_inc(mended, 1)

            @block.scalar
            def _(act):
                if heads:
                    act.wait_ge(dropped, 1)
                    act.activation(factor[:, :, :, :], drop[:, :, :, :], ACT.Exp).then_inc(raised, 1)
                    act.wait_ge(dropped, 2)
                    act.activation(factor2[:, :, :], drop2[:, :, :], ACT.Exp).then_inc(raised, 1)



def load_constants(nc, name, pairs):
    with Stage(nc, name) as s:
        in_ = s.sem("in")
        with nc.Block() as block:
            @block.sync
            def _(sp):
                with nc.allow_non_contiguous_dma(reason="small weights, once"):
                    for dst, src in pairs:
                        sp.dma_start(dst, src).then_inc(in_, 16)
                    sp.wait_ge(in_, 16 * len(pairs))


def layer_norm(nc, g, name):
    with Stage(nc, name) as s:
        sq, total, mean, var, std = s.sb("sq", [P, NT, FD]), *(s.sb(n, [P, NT]) for n in ("tot", "mean", "var", "std"))
        dve_o, var_ready, root = s.sem("dve"), s.sem("var_ready"), s.sem("root")
        x, h = g.x[:, :, :], g.h[:, :, :]
        wide = [P, NT, FD]
        with nc.Block() as block:
            @block.vector
            def _(dve):
                o = Order(dve, dve_o)
                o.link(dve.tensor_reduce(total[:, :], x, AX.X, ALU.add))
                o.link(dve.tensor_scalar(mean[:, :], total[:, :], 1.0 / FD, None, ALU.mult))
                o.link(dve.tensor_tensor(h, x, mean[:, :].unsqueeze(2).to_broadcast(wide), ALU.subtract))
                o.link(dve.tensor_tensor(sq[:, :, :], h, h, ALU.mult))
                o.link(dve.tensor_reduce(total[:, :], sq[:, :, :], AX.X, ALU.add))
                dve.tensor_scalar(var[:, :], total[:, :], 1.0 / FD, 1e-5, ALU.mult, ALU.add).then_inc(var_ready, 1)
                dve.wait_ge(root, 1)
                o.link(dve.reciprocal(mean[:, :], std[:, :]))
                o.link(dve.tensor_tensor(h, h, mean[:, :].unsqueeze(2).to_broadcast(wide), ALU.mult))
                dve.tensor_scalar(h, h, 0.0, None, ALU.max)

            @block.scalar
            def _(act):
                act.wait_ge(var_ready, 1)
                act.activation(std[:, :], var[:, :], ACT.Sqrt).then_inc(root, 1)


def attention_weights(nc, g, name, w, a_src, a_dst, into, rows_w, heads, width):
    hw = heads * width
    with Stage(nc, name) as s:
        both, prod = s.sb("both", [rows_w, 2, hw]), s.sb("prod", [rows_w, 2, hw])
        in_, dve_o = s.sem("in"), s.sem("dve")
        with nc.Block() as block:
            @block.sync
            def _(sp):
                sp.dma_start(into[0:rows_w, 0:hw], w).then_inc(in_, 16)
                for n, v in enumerate((a_src, a_dst)):
                    sp.dma_start(both[:, n, :], v.rearrange("h c -> (h c)").partition_broadcast(rows_w))\
                        .then_inc(in_, 16)

            @block.vector
            def _(dve):
                o = Order(dve, dve_o)
                dve.wait_ge(in_, 48)
                o.link(dve.tensor_tensor(prod[:, :, :], both[:, :, :],
                                         into[0:rows_w, 0:hw].unsqueeze(1).to_broadcast([rows_w, 2, hw]), ALU.mult))
                dve.tensor_reduce(into[0:rows_w, hw:hw + 2 * heads],
                                  prod[:, :, :].rearrange("p n (h c) -> p (n h) c", h=heads), AX.X, ALU.add)


def finish_attention(nc, g, name, sums_d, table, bias, heads, width, into, counts=None):
    hw = heads * width
    sw = hw + 2 * heads
    with Stage(nc, name) as s:
        got_rows = [s.sb(f"rows{k}", [P, GT, sums_d.shape[1]]) for k in range(2)]
        row_g = [s.sb(f"index{k}", [P, GT], I32) for k in range(2)]
        own = [s.sb(f"own{k}", [P, GT, sw]) for k in range(2)]
        part_w = [P, GT, heads]
        has, e_, top, inv = s.sb("has", [P, GT]), s.sb("e", part_w), s.sb("top", part_w), s.sb("inv", part_w)
        drop, factor = s.sb("drop", [P, 2, GT, heads]), s.sb("factor", [P, 2, GT, heads])
        dve_o = s.sem("dve")
        staged, own_in, got, dropped, weighed, cut, raised = (
            [s.sem(f"{n}{k}") for k in range(2)]
            for n in ("staged", "own_in", "got", "dropped", "weighed", "cut", "raised"))

        def per_head(dve, t, scale):
            for h in range(heads):
                part = t[:, :, h * width:(h + 1) * width]
                last = dve.tensor_tensor(part, part, scale[:, :, h].unsqueeze(2).to_broadcast([P, GT, width]),
                                         ALU.mult)
            return last

        with nc.Block() as block:
            @block.sync
            def _(sp):
                with sp.Fori(0, NG // 2) as i:
                    for k in range(2):
                        sp.wait_ge(staged[k], i + 1)
                        sp.dma_start(own[k][:, :, :], by_node(table)[:, bass.ds((i * 2 + k) * GT, GT), :])\
                            .then_inc(own_in[k], 16)

            @block.gpsimd
            def _(pool):
                with pool.Fori(0, NG // 2) as i:
                    for k in range(2):
                        pool.wait_ge(staged[k], i + 1)
                        pool.sem_inc(g.gate, 1)
                        for c in range(GT):
                            pool.indirect_dma_start(got_rows[k][:, c, :], None, sums_d, rows(row_g[k][:, c:c + 1]))\
                                .then_inc(got[k], 16)

            @block.vector
            def _(dve):
                def stage(i, k):
                    dve.tensor_copy(row_g[k][:, :], g.last_row[:, bass.ds((i * 2 + k) * GT, GT)])\
                        .then_inc(staged[k], 1)

                def finish(o, i, k):
                    sums, grp = got_rows[k], bass.ds((i * 2 + k) * GT, GT)
                    v, low = sums[:, :, 0:hw], own[k][:, :, 0:hw]
                    z, m = sums[:, :, hw:hw + heads], sums[:, :, hw + heads:sw]
                    o.link(dve.tensor_scalar(has[:, :], g.has[:, grp], -1.0, BIG, ALU.add, ALU.mult))
                    dve.wait_ge(own_in[k], i * 16 + 16)
                    o.link(dve.tensor_tensor(e_[:, :, :], own[k][:, :, hw:hw + heads], own[k][:, :, hw + heads:],
                                             ALU.add))
                    o.link(dve.scalar_tensor_tensor(e_[:, :, :], e_[:, :, :], SLOPE, e_[:, :, :], ALU.mult, ALU.max))
                    dve.wait_ge(got[k], i * (16 * GT) + 16 * GT)
                    o.link(dve.tensor_tensor(m, m, has[:, :].unsqueeze(2).to_broadcast(part_w), ALU.add))
                    o.link(dve.tensor_tensor(top[:, :, :], e_[:, :, :], m, ALU.max))
                    dve.tensor_tensor(drop[:, 0, :, :], m, top[:, :, :], ALU.subtract)
                    dve.tensor_tensor(drop[:, 1, :, :], e_[:, :, :], top[:, :, :], ALU.subtract)\
                        .then_inc(dropped[k], 1)
                    dve.wait_ge(weighed[k], i + 1)
                    per_head(dve, v, factor[:, 0, :, :])
                    per_head(dve, low, factor[:, 1, :, :])
                    o.link(dve.tensor_tensor(z, z, factor[:, 0, :, :], ALU.mult))
                    o.link(dve.tensor_tensor(z, z, factor[:, 1, :, :], ALU.add))
                    o.link(dve.tensor_scalar(inv[:, :, :], z, 1e-16, None, ALU.add))
                    o.step(dve.reciprocal(inv[:, :, :], inv[:, :, :]))
                    o.link(dve.tensor_tensor(v, v, low, ALU.add))
                    o.link(per_head(dve, v, inv))
                    o.link(dve.tensor_tensor(v, v, bias.unsqueeze(1).to_broadcast([P, GT, hw]), ALU.add))
                    dve.tensor_scalar(low, v, 0.0, None, ALU.min).then_inc(cut[k], 1)
                    dve.tensor_scalar(v, v, 0.0, SELU_SCALE, ALU.max, ALU.mult)
                    if counts is not None:
                        dve.tensor_copy(counts[:, grp, :], sums[:, :, sw:])
                    dve.wait_ge(raised[k], i + 1)
                    sa = SELU_SCALE * SELU_ALPHA
                    o.link(dve.tensor_scalar(low, low, sa, -sa, ALU.mult, ALU.add))
                    o.link(dve.tensor_tensor(into[:, grp, :], v, low, ALU.add))

                per = 28
                for k in range(2):
                    stage(0, k)
                with dve.Fori(0, NG // 2 - 1) as i:
                    o = Order(dve, dve_o, i * per)
                    for k in range(2):
                        finish(o, i, k)
                        stage(i + 1, k)
                    assert o.n == per, (name, o.n)
                o = Order(dve, dve_o, (NG // 2 - 1) * per)
                for k in range(2):
                    finish(o, NG // 2 - 1, k)

            @block.scalar
            def _(act):
                with act.Fori(0, NG // 2) as i:
                    for k in range(2):
                        low = own[k][:, :, 0:hw]
                        act.wait_ge(dropped[k], i + 1)
                        act.activation(factor[:, :, :, :], drop[:, :, :, :], ACT.Exp).then_inc(weighed[k], 1)
                        act.wait_ge(cut[k], i + 1)
                        act.activation(low, low, ACT.Exp).then_inc(raised[k], 1)


def relation_pass(nc, g, name, table, index_d, sums_d, expand=None):
    first = expand is not None
    extras = [by_edge(g.keep_t)] + ([by_edge(g.type8_t), by_edge(expand)] if first else
                                    [by_edge(t) for t in (g.norm_t, g.lane_t, g.tile_t)])
    with Stage(nc, name) as s:
        b = EdgeBuffers(s, g, FD, index_d, extras, FD)
        inv = [s.sb(f"inv{k}", [P, J, R8]) for k in range(2)]
        hot = s.sb("hot", [P, J, R8])
        norm = [s.sb(f"norm{k}", [P, J]) for k in range(2)]
        dve_o = s.sem("dve")
        norm_ready = [s.sem(f"norm_ready{k}") for k in range(2)]
        norm_stored = [s.sem(f"norm_out{k}", 16) for k in range(2)]
        if not first:
            lo_hot = [s.sb(f"lo{k}", [P, J, P], BF16) for k in range(2)]
            hi_hot = [s.sb(f"hi{k}", [P, J, NT], BF16) for k in range(2)]
            none = s.sb("none", [P, P], BF16)
            hist = s.ps("hist", [P, 512])
            none_ready, counted = s.sem("none_ready"), s.sem("counted")
            hot_ready = [s.sem(f"hot{k}") for k in range(2)]
            hot_used = [s.sem(f"hot_used{k}", 1) for k in range(2)]
        acc = by_edge(sums_d)
        norm_d = g.norm_t.rearrange("(p j) o -> p (j o)", p=P)
        with nc.Block() as block:
            @block.sync
            def _(sp):
                b.load(sp)

            @block.gpsimd
            def _(pool):
                b.gather(pool, g, table)

            @block.vector
            def _(dve):
                o = Order(dve, dve_o)
                dve.memset(inv[1][:, J - 1, :], 0.0)
                if not first:
                    dve.memset(none[:, :], 0.0).then_inc(none_ready, 1)
                o.link(dve.memset(b.sums[1][:, J - 1, :], 0.0))
                per = 8 if first else 2
                with dve.Fori(0, NCH // 2) as i:
                    o = Order(dve, dve_o, i * per + 1)
                    for k in range(2):
                        rows_, sums = b.rows[k], b.sums[k]
                        b.wait_extra(dve, i, k)
                        if first:
                            kind = b.extra[k][1][:, :, :].rearrange("p j o -> p (j o)")
                            for r in range(R8):
                                last = scan_sum(dve, inv[k][:, :, r], b.keep[k], b.extra[k][2][:, :, r],
                                                inv[1 - k][:, J - 1, r:r + 1])
                            o.step(last)
                            o.link(dve.tensor_tensor(hot[:, :, :],
                                                     g.count_f[:, 0:R8].unsqueeze(1).to_broadcast([P, J, R8]),
                                                     kind.unsqueeze(2).to_broadcast([P, J, R8]), ALU.is_equal))
                            o.link(dve.tensor_tensor(hot[:, :, :], hot[:, :, :], inv[k][:, :, :], ALU.mult))
                            dve.wait_ge(norm_stored[k], i * 16 + 16)
                            dve.tensor_reduce(norm[k][:, :], hot[:, :, :], AX.X, ALU.add).then_inc(norm_ready[k], 1)
                            dve.wait_ge(norm_ready[k], i + 1)
                            scale = norm[k][:, :]
                        else:
                            scale, lo, hi = (e[:, :, :].rearrange("p j o -> p (j o)") for e in b.extra[k][1:])
                            dve.wait_ge(hot_used[k], i + 1)
                            dve.tensor_tensor(lo_hot[k][:, :, :],
                                              g.count_f[:, :].unsqueeze(1).to_broadcast([P, J, P]),
                                              lo.unsqueeze(2).to_broadcast([P, J, P]), ALU.is_equal)
                            dve.tensor_tensor(hi_hot[k][:, :, :],
                                              g.count_f[:, 0:NT].unsqueeze(1).to_broadcast([P, J, NT]),
                                              hi.unsqueeze(2).to_broadcast([P, J, NT]),
                                              ALU.is_equal).then_inc(hot_ready[k], 1)
                        b.wait_rows(dve, i, k)
                        o.link(dve.tensor_tensor(rows_[:, :, :], rows_[:, :, :],
                                                 scale.unsqueeze(2).to_broadcast([P, J, FD]), ALU.mult))
                        dve.wait_ge(b.stored[k], i * 16 + 16)
                        for c in range(FD):
                            last = scan_sum(dve, sums[:, :, c], b.keep[k], rows_[:, :, c],
                                            b.sums[1 - k][:, J - 1, c:c + 1])
                        last.then_inc(b.done[k], 1)
                        dve.wait_ge(b.done[k], i + 2)
                    assert o.n == per, o.n
                if not first:
                    dve.wait_ge(counted, 1)
                    dve.tensor_tensor(g.deg[:, :], g.deg[:, :], hist[:, 0:NT], ALU.add)

            @block.tensor
            def _(pe):
                if first:
                    return
                pe.wait_ge(none_ready, 1)
                pe.matmul(hist[:, 0:NT], none[:, :], none[:, 0:NT], start=True, stop=False)
                with pe.Fori(0, NCH // 2) as i:
                    for k in range(2):
                        pe.wait_ge(hot_ready[k], i + 1)
                        for j in range(J):
                            last = pe.matmul(hist[:, 0:NT], lo_hot[k][:, j, :], hi_hot[k][:, j, :], start=False,
                                             stop=False)
                        last.then_inc(hot_used[k], 1)
                pe.matmul(hist[:, 0:NT], none[:, :], none[:, 0:NT], start=False, stop=True).then_inc(counted, 1)

            @block.scalar
            def _(act):
                with act.Fori(0, NCH // 2) as i:
                    for k in range(2):
                        if first:
                            act.wait_ge(norm_ready[k], i + 1)
                            act.dma_start(chunk(norm_d, i, k), norm[k][:, :]).then_inc(norm_stored[k], 16)
                        b.store_chunk(act, acc, i, k)
                b.all_stored(act)
                if first:
                    for k in range(2):
                        act.wait_ge(norm_stored[k], 16 * (NCH // 2) + 16)


def reciprocal_counts(nc, g, name, counts, node_table):
    with Stage(nc, name) as s:
        dve_o, ready, out_ = s.sem("dve"), s.sem("ready"), s.sem("out")
        with nc.Block() as block:
            @block.vector
            def _(dve):
                o = Order(dve, dve_o)
                c = counts[:, :, :]
                o.link(dve.tensor_tensor(c, c, g.has[:, :].unsqueeze(2).to_broadcast([P, NT, R8]), ALU.mult))
                o.link(dve.tensor_scalar(c, c, 1.0, None, ALU.max))
                dve.reciprocal(c, c).then_inc(ready, 1)

            @block.sync
            def _(sp):
                sp.wait_ge(ready, 1)
                sp.dma_start(by_node(node_table), counts[:, :, :]).then_inc(out_, 16)
                sp.wait_ge(out_, 16)


def finish_relation(nc, g, name, agg, root_part, bias, into, last):
    wide = [P, NT, FD]
    with Stage(nc, name) as s:
        exps, top, total, log = s.sb("exps", wide), *(s.sb(n, [P, NT]) for n in ("top", "total", "log"))
        dve_o, shifted, raised, summed, logged = (s.sem(n) for n in ("dve", "shifted", "raised", "summed", "logged"))
        with nc.Block() as block:
            @block.vector
            def _(dve):
                o = Order(dve, dve_o)
                v = agg[:, :, :]
                o.link(dve.tensor_tensor(v, v, g.has[:, :].unsqueeze(2).to_broadcast(wide), ALU.mult))
                o.link(dve.tensor_tensor(v, v, root_part[:, :, :], ALU.add))
                o.link(dve.tensor_tensor(v, v, bias.unsqueeze(1).to_broadcast(wide), ALU.add))
                if not last:
                    dve.tensor_scalar(into[:, :, :], v, 0.0, None, ALU.max)
                    return
                o.link(dve.tensor_reduce(top[:, :], v, AX.X, ALU.max))
                dve.tensor_tensor(v, v, top[:, :].unsqueeze(2).to_broadcast(wide), ALU.subtract).then_inc(shifted, 1)
                dve.wait_ge(raised, 1)
                dve.tensor_reduce(total[:, :], exps[:, :, :], AX.X, ALU.add).then_inc(summed, 1)
                dve.wait_ge(logged, 1)
                o.link(dve.tensor_tensor(v, v, log[:, :].unsqueeze(2).to_broadcast(wide), ALU.subtract))
                dve.tensor_tensor(g.x[:, :, :], g.x[:, :, :], v, ALU.add)

            @block.scalar
            def _(act):
                if last:
                    act.wait_ge(shifted, 1)
                    act.activation(exps[:, :, :], agg[:, :, :], ACT.Exp).then_inc(raised, 1)
                    act.wait_ge(summed, 1)
                    act.activation(log[:, :], total[:, :], ACT.Ln).then_inc(logged, 1)


def sheaf_pass(nc, g, name, w1, w2, b1, b2, table, expand, sums_d):
    QC = 4
    NQ = J // QC
    HALF = J // 2
    F2 = 2 * FD
    with Stage(nc, name) as s:
        b = EdgeBuffers(s, g, FD + 1, g.src_id, [by_edge(g.keep_t), by_edge(expand), by_edge(g.src_t)], FD)
        src_of = [e[2][:, :, :].rearrange("p j o -> p (j o)") for e in b.extra]
        filled = [s.sb(f"filled{k}", [P, J, FD + 1]) for k in range(2)]
        ends = s.sb("ends", [P, J, F2])
        v = s.sb("v", [P, J, F2])
        prod, once, twice = s.sb("prod", [P, J, F2]), s.sb("once", [P, J, F2]), s.sb("twice", [P, J, F2])
        dots, inv2 = s.sb("dots", [P, J, 2]), s.sb("inv2", [P, J, 2])
        same = s.sb("same", [P, J, P])
        earlier = s.sb("earlier", [P, QC, P])
        rank, place = s.sb("rank", [P, J]), s.sb("place", [P, J])
        spare_f = s.sb("spare", [P, 1])
        to_row = [s.sb(f"torow{k}", [P, J], I32) for k in range(2)]
        to_add = [s.sb(f"toadd{k}", [P, J, FD]) for k in range(2)]
        ends_t = [s.sb(f"endst{k}", [F2, QC * P]) for k in range(2)]
        hidden = [s.sb(f"hidden{k}", [P, QC * P]) for k in range(2)]
        across = [s.ps(f"across{k}", [P, QC * P]) for k in range(2)]
        ends_ps = [s.ps(f"endsp{k}", [F2, QC * P]) for k in range(2)]
        hidden_ps, v_ps = s.ps("hiddenp", [P, QC * P]), s.ps("vp", [P, QC * F2])
        added_ps = [s.ps(f"added{n}", [P, HALF * FD]) for n in range(2)]
        (dve_o, ends_ready, across_ready, across_used, ends_turned, ends_copied, hid_ready, hid_done, v_ready, v_used,
         same_ready, msg_ready, added) = (
            s.sem(n, c) for n, c in (("dve", 0), ("ends_ready", 0), ("across_ready", 0), ("across_used", 0),
                                     ("ends_turned", 0), ("ends_copied", 2), ("hid_ready", 2), ("hid_done", 1),
                                     ("v_ready", 1), ("v_used", 1), ("same_ready", 0), ("msg_ready", 0), ("added", 0)))
        added_taken = s.sem("added_taken", 1)
        to_add_free = [s.sem(f"to_add_free{k}", 1) for k in range(2)]
        to_add_ready = [s.sem(f"to_add_ready{k}") for k in range(2)]
        summed = [[s.sem(f"summed{k}{r}") for r in range(NSUM)] for k in range(2)]
        acc = by_edge(sums_d)
        per_table = J // NSUM
        with nc.Block() as block:
            @block.sync
            def _(sp):
                b.load(sp)

            @block.gpsimd
            def _(pool):
                def scatters(i, k, first=False, gathers=True):
                    pool.wait_ge(to_add_ready[k], i + 1)
                    if gathers:
                        b.wait_to_gather(pool, i + 1, k)
                    pool.sem_inc(g.gate, 1)
                    for j in range(J):
                        r = j % NSUM
                        if not (first and j < NSUM):
                            pool.wait_ge(summed[k][r], i * (16 * per_table) + 16 * (j // NSUM))
                            pool.sem_inc(g.gate, 1)
                        pool.indirect_dma_start(g.by_src[k][r], rows(to_row[k][:, j:j + 1]), to_add[k][:, j, :], None,
                                                compute_op=ALU.add).then_inc(summed[k][r], 16)
                        if gathers:
                            b.gather_column(pool, table, k, j)
                        if j == HALF and not (first and k == 0):
                            for r in range(NSUM):
                                pool.wait_ge(summed[1 - k][r], (i + k) * (16 * per_table))
                            pool.sem_inc(to_add_free[1 - k], 1)

                def turn(i, first=False, gathers=True):
                    for k in range(2):
                        scatters(i, k, first, gathers)
                for k in range(2):
                    b.gather_chunk(pool, g, table, 0, k)
                turn(0, first=True)
                with pool.Fori(1, NCH // 2 - 1) as i:
                    turn(i)
                turn(NCH // 2 - 1, gathers=False)
                for k in range(2):
                    for r in range(NSUM):
                        pool.wait_ge(summed[k][r], 16 * per_table * (NCH // 2))

            @block.vector
            def _(dve):
                o = Order(dve, dve_o)
                dve.memset(filled[1][:, J - 1, :], 0.0)
                dve.tensor_scalar(spare_f[:, :], g.lane_f[:, :], float(NP), None, ALU.add)
                o.link(dve.memset(b.sums[1][:, J - 1, :], 0.0))
                per = 2 * (NQ + 16)
                with dve.Fori(0, NCH // 2) as i:
                    o = Order(dve, dve_o, i * per + 1)
                    for k in range(2):
                        q0 = i * (2 * NQ) + k * NQ
                        c0 = i * 2 + k
                        rows_, sums = b.rows[k], b.sums[k]
                        b.wait_extra(dve, i, k)
                        for c in range(FD + 1):
                            last = scan_sum(dve, filled[k][:, :, c], b.keep[k], b.extra[k][1][:, :, c],
                                            filled[1 - k][:, J - 1, c:c + 1])
                        o.link(last)
                        b.wait_rows(dve, i, k)
                        dve.tensor_copy(ends[:, :, 0:FD], rows_[:, :, 0:FD])
                        dve.tensor_copy(ends[:, :, FD:F2], filled[k][:, :, 0:FD]).then_inc(ends_ready, 1)

                        def take_v(q):
                            dve.wait_ge(v_ready, q0 + q + 2)
                            dve.tensor_tensor(v[:, q * QC:(q + 1) * QC, :],
                                              v_ps[:, :].rearrange("p (c w) -> p c w", c=QC),
                                              b2.unsqueeze(1).to_broadcast([P, QC, F2]), ALU.add).then_inc(v_used, 1)
                        for q in range(NQ):
                            js = slice(q * QC, (q + 1) * QC)
                            dve.wait_ge(across_ready, q0 + q + 1)
                            o.link(dve.tensor_tensor(same[:, js, :],
                                                     across[q % 2][:, :].rearrange("p (c w) -> p c w", c=QC),
                                                     src_of[k][:, js].unsqueeze(2).to_broadcast([P, QC, P]),
                                                     ALU.is_equal))
                            dve.tensor_tensor(earlier[:, :, :], same[:, js, :],
                                              g.strict[:, :].unsqueeze(1).to_broadcast([P, QC, P]), ALU.mult)\
                                .then_inc(across_used, 1)
                            dve.wait_ge(across_used, q0 + q + 1)
                            dve.tensor_reduce(rank[:, js], earlier[:, :, :], AX.X, ALU.add).then_inc(same_ready, 1)
                            if q >= 1:
                                take_v(q - 1)
                            dve.wait_ge(same_ready, q0 + q + 1)
                        take_v(NQ - 1)
                        dve.wait_ge(v_used, q0 + NQ + 1)
                        o.link(dve.tensor_scalar(rank[:, :], rank[:, :], 0.0, None, ALU.is_equal))
                        o.link(dve.tensor_scalar(place[:, :], src_of[k], spare_f[:, :], None, ALU.subtract))
                        o.link(dve.tensor_tensor(place[:, :], place[:, :], rank[:, :], ALU.mult))
                        dve.wait_ge(to_add_free[k], i + 1)
                        dve.tensor_scalar(to_row[k][:, :], place[:, :], spare_f[:, :], None, ALU.add)
                        def halves(t):
                            return t[:, :, :].rearrange("p j (n c) -> p j n c", n=2)

                        def wide(t):
                            return t[:, :, :].unsqueeze(3).to_broadcast([P, J, 2, FD])
                        o.link(dve.tensor_tensor(prod[:, :, :], v[:, :, :], v[:, :, :], ALU.mult))
                        o.link(dve.tensor_reduce(inv2[:, :, :], halves(prod), AX.X, ALU.add))
                        o.link(dve.tensor_scalar(inv2[:, :, :], inv2[:, :, :], 0.5, 0.5e-24, ALU.mult, ALU.max))
                        dve.reciprocal(inv2[:, :, :], inv2[:, :, :])
                        o.link(dve.tensor_tensor(prod[:, :, :], v[:, :, :], ends[:, :, :], ALU.mult))
                        o.link(dve.tensor_reduce(dots[:, :, :], halves(prod), AX.X, ALU.add))
                        o.link(dve.tensor_tensor(dots[:, :, :], dots[:, :, :], inv2[:, :, :], ALU.mult))
                        o.link(dve.tensor_tensor(halves(prod), halves(v), wide(dots), ALU.mult))
                        o.link(dve.tensor_tensor(once[:, :, :], ends[:, :, :], prod[:, :, :], ALU.subtract))
                        dve.tensor_tensor(prod[:, :, 0:FD], v[:, :, 0:FD], once[:, :, FD:F2], ALU.mult)
                        o.link(dve.tensor_tensor(prod[:, :, FD:F2], v[:, :, FD:F2], once[:, :, 0:FD], ALU.mult))
                        o.link(dve.tensor_reduce(dots[:, :, :], halves(prod), AX.X, ALU.add))
                        o.link(dve.tensor_tensor(dots[:, :, :], dots[:, :, :], inv2[:, :, :], ALU.mult))
                        o.link(dve.tensor_tensor(halves(prod), halves(v), wide(dots), ALU.mult))
                        dve.tensor_tensor(twice[:, :, 0:FD], once[:, :, FD:F2], prod[:, :, 0:FD], ALU.subtract)\
                            .then_inc(msg_ready, 1)
                        dve.tensor_tensor(twice[:, :, FD:F2], once[:, :, 0:FD], prod[:, :, FD:F2], ALU.subtract)\
                            .then_inc(msg_ready, 1)
                        dve.wait_ge(msg_ready, c0 * 4 + 2)
                        dve.tensor_tensor(twice[:, :, FD:F2], twice[:, :, FD:F2],
                                          rows_[:, :, FD:].to_broadcast([P, J, FD]), ALU.mult).then_inc(msg_ready, 1)
                        dve.tensor_tensor(twice[:, :, 0:FD], twice[:, :, 0:FD],
                                          filled[k][:, :, FD:].to_broadcast([P, J, FD]), ALU.mult)\
                            .then_inc(msg_ready, 1)
                        dve.wait_ge(msg_ready, c0 * 4 + 4)
                        dve.wait_ge(b.stored[k], i * 16 + 16)
                        for c in range(FD):
                            last = scan_sum(dve, sums[:, :, c], b.keep[k], twice[:, :, FD + c],
                                            b.sums[1 - k][:, J - 1, c:c + 1])
                        last.then_inc(b.done[k], 1)
                        dve.wait_ge(b.done[k], i + 2)
                    assert o.n == per, o.n

            @block.tensor
            def _(pe):
                with pe.Fori(0, NCH // 2) as i:
                    for k in range(2):
                        q0 = i * (2 * NQ) + k * NQ
                        c0 = i * 2 + k
                        pe.wait_ge(ends_ready, c0 + 1)

                        def spin(q):
                            if q >= 2:
                                pe.wait_ge(across_used, q0 + q - 1)
                            for c in range(QC):
                                j = q * QC + c
                                last = pe.matmul(across[q % 2][:, c * P:(c + 1) * P],
                                                 src_of[k][:, j:j + 1].to_broadcast([P, P]), g.ident[:, :],
                                                 start=True, stop=True)
                            last.then_inc(across_ready, 1)
                            pe.wait_ge(ends_copied, q0 + q + 1)
                            for c in range(QC):
                                last = pe.transpose(ends_ps[(q + k * NQ) % 2][:, c * P:(c + 1) * P],
                                                    ends[:, q * QC + c, :], g.ident[:, :])
                            last.then_inc(ends_turned, 1)

                        def hide(q):
                            pe.wait_ge(ends_copied, q0 + q + 3)
                            pe.wait_ge(hid_done, q0 + q + 1)
                            pe.matmul(hidden_ps[:, :], w1, ends_t[(q + k * NQ) % 2][:, :], start=True, stop=True)\
                                .then_inc(hid_ready, 1)

                        def unhide(q):
                            pe.wait_ge(hid_done, q0 + q + 2)
                            pe.wait_ge(v_used, q0 + q + 1)
                            for c in range(QC):
                                last = pe.matmul(v_ps[:, c * F2:(c + 1) * F2],
                                                 hidden[(q + k * NQ) % 2][:, c * P:(c + 1) * P], w2,
                                                 start=True, stop=True)
                            last.then_inc(v_ready, 1)
                        spin(0)
                        for q in range(NQ):
                            if q + 1 < NQ:
                                spin(q + 1)
                            hide(q)
                            if q >= 1:
                                unhide(q - 1)
                        unhide(NQ - 1)
                        pe.wait_ge(msg_ready, c0 * 4 + 4)
                        pe.wait_ge(same_ready, q0 + NQ)
                        pe.wait_ge(added_taken, c0 + 1)
                        for j in range(J):
                            last = pe.matmul(added_ps[j // HALF][:, (j % HALF) * FD:(j % HALF + 1) * FD],
                                             same[:, j, :], twice[:, j, 0:FD], start=True, stop=True)
                        last.then_inc(added, 1)

            @block.scalar
            def _(act):
                with act.Fori(0, NCH // 2) as i:
                    for k in range(2):
                        q0 = i * (2 * NQ) + k * NQ

                        def take_ends(q):
                            act.wait_ge(ends_turned, q0 + q + 1)
                            act.wait_ge(hid_ready, q0 + q + 1)
                            act.copy(ends_t[(q + k * NQ) % 2][:, :], ends_ps[(q + k * NQ) % 2][:, :])\
                                .then_inc(ends_copied, 1)
                        take_ends(0)
                        for q in range(NQ):
                            if q + 1 < NQ:
                                take_ends(q + 1)
                            act.wait_ge(hid_ready, q0 + q + 3)
                            if q > 0 or k > 0:
                                act.wait_ge(v_ready, q0 + q)
                            act.activation(hidden[(q + k * NQ) % 2][:, :], hidden_ps[:, :], ACT.Relu, bias=b1)\
                                .then_inc(hid_done, 1)
                        b.store_chunk(act, acc, i, k)
                        act.wait_ge(added, i * 2 + k + 1)
                        act.wait_ge(to_add_free[k], i + 1)
                        act.copy(to_add[k][:, 0:HALF, :], added_ps[0][:, :].rearrange("p (c w) -> p c w", w=FD))
                        act.copy(to_add[k][:, HALF:J, :], added_ps[1][:, :].rearrange("p (c w) -> p c w", w=FD))\
                            .then_inc(to_add_ready[k], 1)
                        act.wait_ge(to_add_ready[k], i + 1)
                        act.sem_inc(added_taken, 1)
                b.all_stored(act)


def sheaf_table(nc, g, name, table, values):
    with Stage(nc, name) as s:
        t1 = s.sb("t1", [P, NT])
        capped, root, ready, out_ = (s.sem(n) for n in ("capped", "root", "ready", "out"))
        with nc.Block() as block:
            @block.vector
            def _(dve):
                dve.tensor_scalar(t1[:, :], g.deg[:, :], 1e-5, None, ALU.max).then_inc(capped, 1)
                dve.tensor_copy(values[:, :, 0:FD], g.h[:, :, :])
                dve.wait_ge(root, 1)
                dve.reciprocal(values[:, :, FD], t1[:, :]).then_inc(ready, 1)

            @block.scalar
            def _(act):
                act.wait_ge(capped, 1)
                act.activation(t1[:, :], t1[:, :], ACT.Sqrt).then_inc(root, 1)

            @block.sync
            def _(sp):
                sp.wait_ge(ready, 1)
                sp.dma_start(by_node(table), values[:, :, :]).then_inc(out_, 16)
                sp.wait_ge(out_, 16)


def finish_sheaf(nc, g, name, agg, values):
    wide = [P, NT, FD]
    tables = [t for ts in g.by_src for t in ts]
    with Stage(nc, name) as s:
        parts = [s.sb(f"part{n}", wide) for n in range(len(tables))]
        in_ = [s.sem(f"in{n}") for n in range(len(tables))]
        dve_o = s.sem("dve")
        with nc.Block() as block:
            @block.sync
            def _(sp):
                for n, t in enumerate(tables):
                    sp.dma_start(parts[n][:, :, :], by_node(t[0:NP])).then_inc(in_[n], 16)

            @block.vector
            def _(dve):
                o = Order(dve, dve_o)
                v = agg[:, :, :]
                o.link(dve.tensor_tensor(v, v, g.has[:, :].unsqueeze(2).to_broadcast(wide), ALU.mult))
                for n in range(len(tables)):
                    dve.wait_ge(in_[n], 16)
                    o.link(dve.tensor_tensor(v, v, parts[n][:, :, :], ALU.add))
                o.link(dve.tensor_tensor(v, v, values[:, :, FD:].to_broadcast(wide), ALU.mult))
                o.link(dve.tensor_tensor(v, v, g.h[:, :, :], ALU.add))
                o.link(dve.tensor_scalar(v, v, 0.0, None, ALU.max))
                dve.tensor_tensor(g.x[:, :, :], g.x[:, :, :], v, ALU.add)


def sheaf_weights(nc, g, name, a, w1, w2, b1, b2):
    hid = P // 2
    with Stage(nc, name) as s:
        in_, cleared = s.sem("in"), s.sem("cleared")
        with nc.Block() as block:
            @block.vector
            def _(dve):
                dve.memset(w2[:, :], 0.0).then_inc(cleared, 1)

            @block.sync
            def _(sp):
                w1t, w2t = a.L2_gnn_W1.rearrange("h i -> i h"), a.L2_gnn_W2.rearrange("o h -> h o")
                b1c = a.L2_gnn_b1.unsqueeze(1)
                sp.wait_ge(cleared, 1)
                with nc.allow_non_contiguous_dma(reason="small weights, once"):
                    pairs = [(w1[:, 0:hid], w1t), (w1[0:FD, hid:], w1t[FD:, :]), (w1[FD:, hid:], w1t[0:FD, :]),
                             (w2[0:hid, 0:FD], w2t), (w2[hid:, FD:], w2t), (b1[0:hid, :], b1c), (b1[hid:, :], b1c),
                             (b2[:, 0:FD], a.L2_gnn_b2.partition_broadcast(P)),
                             (b2[:, FD:], a.L2_gnn_b2.partition_broadcast(P))]
                    for dst, src in pairs:
                        sp.dma_start(dst, src).then_inc(in_, 16)
                    sp.wait_ge(in_, 16 * len(pairs))


def relation_weights(nc, g, name, a, w, attr_w):
    M = R90 * (FD + 1)
    with Stage(nc, name) as s:
        comp_t, bases = s.sb("compt", [NB, R90]), s.sb("bases", [NB, FD, FD])
        mixed, ws, wa = s.sb("mixed", [R90, FD, FD]), s.sb("ws", [FD, FD]), s.sb("wa", [FD, 3])
        wa_wide, parts = s.sb("wawide", [FD, P]), s.sb("parts", [FD, 2])
        mixed_ps, parts_ps, attr_ps = s.ps("mixedp", [R90, FD * FD]), s.ps("partsp", [FD, 2]), s.ps("attrp", [P, FD])
        in_, mixed_ready, mixed_sb, out_, back, wide_ready, small, cp = (
            s.sem(n) for n in ("in", "mixed_ready", "mixed_sb", "out", "back", "wide_ready", "small", "cp"))
        w_view = w[:, 0:M].rearrange("i (r c) -> i r c", r=R90)
        flat = g.mixed_d
        with nc.Block() as block:
            @block.sync
            def _(sp):
                with nc.allow_non_contiguous_dma(reason="small weights, once"):
                    v = a.L3_gnn_weight.rearrange("b i o -> (b i) o").rearrange("(i b) o -> b i o", b=NB)
                    pairs = [(comp_t[:, :], a.L3_gnn_w_comp.rearrange("r b -> b r")), (bases[:, :, :], v),
                             (ws[:, :], a.L3_gnn_Ws), (wa[:, :], a.L3_gnn_Wa.rearrange("u (n o) -> o (u n)", n=3))]
                    for dst, src in pairs:
                        sp.dma_start(dst, src).then_inc(in_, 16)
                sp.wait_ge(mixed_sb, 1)
                sp.dma_start(flat.rearrange("(i r) o -> r i o", r=R90), mixed[:, :, :]).then_inc(out_, 16)
                sp.wait_ge(out_, 16)
                sp.dma_start(w_view[:, :, 0:FD], flat.rearrange("(r i) o -> i r o", i=FD)).then_inc(back, 16)
                sp.wait_ge(back, 16)

            @block.tensor
            def _(pe):
                pe.wait_ge(in_, 64)
                pe.matmul(mixed_ps[:, :], comp_t[:, :], bases[:, :, :].rearrange("b i o -> b (i o)"), start=True,
                          stop=True).then_inc(mixed_ready, 1)
                pe.matmul(parts_ps[:, 0:1], ws[:, :], wa[:, 0:1], start=True, stop=True)
                pe.matmul(parts_ps[:, 1:2], ws[:, :], wa[:, 2:3], start=True, stop=True)
                pe.wait_ge(wide_ready, 1)
                pe.matmul(attr_ps[:, :], wa_wide[:, :], ws[:, :], start=True, stop=True).then_inc(small, 1)

            @block.vector
            def _(dve):
                dve.wait_ge(in_, 64)
                dve.tensor_copy(wa_wide[:, :], wa[:, 1:2].to_broadcast([FD, P])).then_inc(wide_ready, 1)
                dve.wait_ge(mixed_ready, 1)
                dve.tensor_copy(mixed[:, :, :].rearrange("r i o -> r (i o)"), mixed_ps[:, :]).then_inc(mixed_sb, 1)
                dve.wait_ge(small, 1)
                dve.tensor_copy(attr_w, attr_ps[:, :])
                dve.tensor_copy(parts[:, :], parts_ps[:, :]).then_inc(cp, 1)
                dve.wait_ge(cp, 1)
                dve.tensor_copy(w[:, M:M + 1], parts[:, 1:2])
                dve.tensor_copy(w_view[:, :, FD], parts[:, 0:1].to_broadcast([FD, R90]))


PAIRS = ((0, 0), (0, 1), (1, 0), (0, 2), (1, 1), (2, 0), (1, 2), (2, 1))


def split_operands(nc, g, name, h, h_parts, w, w_parts):
    cols = w.shape[1]
    with Stage(nc, name) as s:
        short_h, rest_h = s.sb("shorth", [P, NT, FD], BF16), s.sb("resth", [P, NT, FD])
        short_w, long_w, rest_w = [s.sb(f"shortw{n}", [FD, cols], BF16) for n in range(3)], s.sb("longw", [FD, cols]), \
            s.sb("restw", [FD, cols])
        dve_o, w_split, placed = s.sem("dve"), s.sem("w_split"), s.sem("placed")
        with nc.Block() as block:
            @block.vector
            def _(dve):
                o = Order(dve, dve_o)
                for n in range(3):
                    before = w[:, :] if n == 0 else rest_w[:, :]
                    dve.tensor_copy(short_w[n][:, :], before).then_inc(w_split, 1)
                    dve.wait_ge(w_split, n + 1)
                    if n < 2:
                        o.link(dve.tensor_copy(long_w[:, :], short_w[n][:, :]))
                        o.link(dve.tensor_tensor(rest_w[:, :], before, long_w[:, :], ALU.subtract))
                for n in range(3):
                    before = h[:, :, :] if n == 0 else rest_h[:, :, :]
                    o.link(dve.tensor_copy(short_h[:, :, :], before))
                    for b, (hn, _) in enumerate(PAIRS):
                        if hn == n:
                            part = h_parts[:, :, b * FD:(b + 1) * FD]
                            last = dve.tensor_copy(part, short_h[:, :, :])
                    o.link(last)
                    if n < 2:
                        o.link(dve.tensor_tensor(rest_h[:, :, :], before, part, ALU.subtract))

            @block.sync
            def _(sp):
                for b, (_, wn) in enumerate(PAIRS):
                    sp.wait_ge(w_split, wn + 1)
                    sp.dma_start(w_parts[b * FD:(b + 1) * FD, :], short_w[wn][:, :]).then_inc(placed, 16)
                sp.wait_ge(placed, 16 * len(PAIRS))


def typed_attention_pass(nc, g, name, table, expand, attr, attr_w, sums_d):
    with Stage(nc, name) as s:
        b = EdgeBuffers(s, g, FD + 1, g.idx90_d, [by_edge(g.keep_t), by_edge(expand), attr], FD)
        dst_part = [s.sb(f"dst{k}", [P, J]) for k in range(2)]
        weight = s.sb("weight", [P, J])
        dve_o = s.sem("dve")
        acc = by_edge(sums_d)
        with nc.Block() as block:
            @block.sync
            def _(sp):
                b.load(sp)

            @block.gpsimd
            def _(pool):
                b.gather(pool, g, table)

            @block.vector
            def _(dve):
                o = Order(dve, dve_o)
                dve.memset(dst_part[1][:, :], 0.0)
                o.link(dve.memset(b.sums[1][:, J - 1, :], 0.0))
                per = 10
                with dve.Fori(0, NCH // 2) as i:
                    o = Order(dve, dve_o, i * per + 1)
                    for k in range(2):
                        rows_, at = b.rows[k], b.extra[k][2]
                        b.wait_extra(dve, i, k)
                        o.step(scan_sum(dve, dst_part[k][:, :], b.keep[k], b.extra[k][1][:, :, 0],
                                        dst_part[1 - k][:, J - 1:J]))
                        o.link(dve.tensor_tensor(at[:, :, :], at[:, :, :],
                                                 attr_w.unsqueeze(1).to_broadcast([P, J, FD]), ALU.mult))
                        o.link(dve.tensor_reduce(weight[:, :], at[:, :, :], AX.X, ALU.add))
                        o.link(dve.tensor_tensor(weight[:, :], weight[:, :], dst_part[k][:, :], ALU.add))
                        b.wait_rows(dve, i, k)
                        part = rows_[:, :, FD:].rearrange("p j o -> p (j o)")
                        o.link(dve.tensor_tensor(weight[:, :], weight[:, :], part, ALU.add))
                        dve.tensor_tensor(rows_[:, :, 0:FD], rows_[:, :, 0:FD],
                                          weight[:, :].unsqueeze(2).to_broadcast([P, J, FD]), ALU.mult)\
                            .then_inc(b.used[k], 1)
                        dve.wait_ge(b.used[k], i + 1)
                        dve.wait_ge(b.stored[k], i * 16 + 16)
                        for c in range(FD):
                            last = scan_sum(dve, b.sums[k][:, :, c], b.keep[k], rows_[:, :, c],
                                            b.sums[1 - k][:, J - 1, c:c + 1])
                        last.then_inc(b.done[k], 1)
                        dve.wait_ge(b.done[k], i + 2)
                    assert o.n == per, o.n

            @block.scalar
            def _(act):
                with act.Fori(0, NCH // 2) as i:
                    for k in range(2):
                        b.store_chunk(act, acc, i, k)
                b.all_stored(act)


def finish_all(nc, g, name, agg, out):
    with Stage(nc, name) as s:
        dve_o, ready, out_ = s.sem("dve"), s.sem("ready"), s.sem("out")
        with nc.Block() as block:
            @block.vector
            def _(dve):
                v = agg[:, :, :]
                Order(dve, dve_o).link(dve.tensor_tensor(v, v, g.has[:, :].unsqueeze(2).to_broadcast([P, NT, FD]),
                                                         ALU.mult))
                dve.tensor_tensor(v, v, g.x[:, :, :], ALU.add).then_inc(ready, 1)

            @block.sync
            def _(sp):
                sp.wait_ge(ready, 1)
                sp.dma_start(by_node(out), agg[:, :, :]).then_inc(out_, 16)
                sp.wait_ge(out_, 16)


def add_rows(nc, g, name, rows_, bias):
    with Stage(nc, name) as s:
        dve_o = s.sem("dve")
        with nc.Block() as block:
            @block.vector
            def _(dve):
                o = Order(dve, dve_o)
                x = g.x[:, :, :]
                o.link(dve.tensor_tensor(x, x, rows_[:, :, :], ALU.add))
                dve.tensor_tensor(x, x, bias.unsqueeze(1).to_broadcast([P, NT, FD]), ALU.add)



def attention_layers(nc, a, g):
    with Stage(nc, "gat") as s:
        h1, c1, h2, c2 = 3, 32, 1, 32
        w1, w2, wf = s.sb("w1", [FD, h1 * c1 + 2 * h1]), s.sb("w2", [h1 * c1, c2 + 2]), s.sb("wf", [c2, FD])
        b1, b2, bf = s.sb("b1", [P, h1 * c1]), s.sb("b2", [P, c2]), s.sb("bf", [P, FD])
        table1, table2 = g.dram("att1_t", [NP, 102]), g.dram("att2_t", [NP, 34])
        sums1, sums2 = g.sums["att1"], g.sums["att2"]
        load_constants(nc, "gat_in", [(b1[:, :], a.L0_gnn_b1.partition_broadcast(P)),
                                      (b2[:, :], a.L0_gnn_b2.partition_broadcast(P)),
                                      (bf[:, :], a.L0_gnn_bf.partition_broadcast(P)), (wf[:, :], a.L0_gnn_Wf)])
        attention_weights(nc, g, "gat_w1", a.L0_gnn_W1, a.L0_gnn_a_src1, a.L0_gnn_a_dst1, w1, FD, h1, c1)
        attention_weights(nc, g, "gat_w2", a.L0_gnn_W2, a.L0_gnn_a_src2, a.L0_gnn_a_dst2, w2, h1 * c1, h2, c2)
        layer_norm(nc, g, "ln1")
        with Stage(nc, "gat1") as t:
            parts = t.sb("parts", [P, NT, h1])
            project(nc, g, "gat1_p", g.h, FD, w1, 102, table1, (parts, 99), (parts, g.expand["att1"], table1))
        attention_pass(nc, g, "gat1_e", h1, c1, table1, g.expand["att1"], sums1,
                       to_zero=([t for n, t in g.expand.items() if n != "att1"], [t for ts in g.by_src for t in ts]))
        carry_over(nc, g, "gat1_c", sums1, h1, c1)
        with Stage(nc, "gat1n") as t:
            mid, parts = t.sb("mid", [P, NT, h1 * c1]), t.sb("parts", [P, NT, 1])
            finish_attention(nc, g, "gat1_f", sums1, table1, b1[:, :], h1, c1, mid)
            project(nc, g, "gat2_p", mid, h1 * c1, w2, 34, table2, (parts, 33), (parts, g.expand["att2"], table2))
        attention_pass(nc, g, "gat2_e", h2, c2, table2, g.expand["att2"], sums2, kinds=True)
        carry_over(nc, g, "gat2_c", sums2, h2, c2)
        with Stage(nc, "gat2n") as t:
            mid = t.sb("mid", [P, NT, c2])
            finish_attention(nc, g, "gat2_f", sums2, table2, b2[:, :], h2, c2, mid, g.counts)
            reciprocal_counts(nc, g, "count_r", g.counts, g.counts_d)
            project(nc, g, "gatf_p", mid, c2, wf, FD, None, (g.h, 0))
            add_rows(nc, g, "gatf_a", g.h, bf[:, :])


def relation_layers(nc, a, g):
    with Stage(nc, "rgcn") as s:
        wide = R8 * FD + FD
        w = [s.sb(f"w{n}", [FD, wide]) for n in range(2)]
        bias = [s.sb(f"b{n}", [P, FD]) for n in range(2)]
        tables = [g.dram(f"rel_t{n}", [NP, R8 * FD]) for n in range(2)]
        load_constants(nc, "rgcn_in", [
            x for n, (wr, root, b) in enumerate(((a.L1_gnn_W1, a.L1_gnn_root1, a.L1_gnn_b1),
                                                 (a.L1_gnn_W2, a.L1_gnn_root2, a.L1_gnn_b2)))
            for x in ((w[n][:, 0:R8 * FD].rearrange("i (r o) -> i r o", r=R8), wr.rearrange("r i o -> i r o")),
                      (w[n][:, R8 * FD:], root), (bias[n][:, :], b.partition_broadcast(P)))])
        layer_norm(nc, g, "ln2")
        for n in range(2):
            with Stage(nc, f"rgcn{n}") as t:
                root_part, agg = t.sb("root", [P, NT, FD]), t.sb("agg", [P, NT, FD])
                project(nc, g, f"rgcn{n}_p", g.h, FD, w[n], wide, tables[n], (root_part, R8 * FD),
                        (g.counts, g.expand["rel"], g.counts_d) if n == 0 else None)
                relation_pass(nc, g, f"rgcn{n}_e", tables[n].rearrange("n (r o) -> (n r) o", r=R8), g.idx8_d,
                              g.sums["rel"], g.expand["rel"] if n == 0 else None)
                carry_over(nc, g, f"rgcn{n}_c", g.sums["rel"])
                gather_to(nc, g, f"rgcn{n}_g", g.sums["rel"], g.last_row, FD, agg)
                finish_relation(nc, g, f"rgcn{n}_f", agg, root_part, bias[n][:, :], g.h, n == 1)


def sheaf_layer(nc, a, g):
    with Stage(nc, "sheaf") as s:
        w1, w2, b1, b2 = s.sb("w1", [2 * FD, P]), s.sb("w2", [P, 2 * FD]), s.sb("b1", [P, 1]), s.sb("b2", [P, 2 * FD])
        table = g.dram("sheaf_t", [NP, FD + 1])
        values = s.sb("values", [P, NT, FD + 1])
        sheaf_weights(nc, g, "sheaf_w", a, w1, w2, b1, b2)
        layer_norm(nc, g, "ln3")
        sheaf_table(nc, g, "sheaf_n", table, values)
        spread(nc, g, "sheaf_s", values, table, g.expand["sheaf"], FD + 1)
        sheaf_pass(nc, g, "sheaf_e", w1[:, :], w2[:, :], b1[:, :], b2[:, :], table, g.expand["sheaf"],
                   g.sums["sheaf"])
        carry_over(nc, g, "sheaf_c", g.sums["sheaf"])
        with Stage(nc, "sheafn") as t:
            agg = t.sb("agg", [P, NT, FD])
            gather_to(nc, g, "sheaf_g", g.sums["sheaf"], g.last_row, FD, agg)
            finish_sheaf(nc, g, "sheaf_f", agg, values)


def typed_layer(nc, a, g, out):
    with Stage(nc, "typed") as s:
        M = R90 * (FD + 1)
        w, attr_w = s.sb("w", [FD, M + 1]), s.sb("attrw", [P, FD])
        g.mixed_d = g.dram("mixed_d", [FD * R90, FD])
        table, part_d = g.dram("typed_t", [NP, M]), g.dram("typed_dst", [NP, 1])
        relation_weights(nc, g, "typed_w", a, w, attr_w[:, :])
        layer_norm(nc, g, "ln4")
        with Stage(nc, "typedp") as t:
            parts = t.sb("parts", [P, NT, 1])
            h_parts, w_parts = t.sb("hparts", [P, NT, 8 * FD]), t.sb("wparts", [8 * FD, M + 1], BF16)
            split_operands(nc, g, "typed_x", g.h, h_parts, w, w_parts)
            project(nc, g, "typed_p", h_parts, 8 * FD, w_parts, M + 1, table, (parts, M),
                    (parts, g.expand["typed"], part_d), BF16)
        typed_attention_pass(nc, g, "typed_e", table.rearrange("n (r c) -> (n r) c", c=FD + 1),
                             g.expand["typed"], a.attr, attr_w[:, :], g.sums["typed"])
        carry_over(nc, g, "typed_c", g.sums["typed"])
        with Stage(nc, "typedn") as t:
            agg = t.sb("agg", [P, NT, FD])
            gather_to(nc, g, "typed_g", g.sums["typed"], g.last_row, FD, agg)
            finish_all(nc, g, "typed_f", agg, out)


class Arrays:
    pass


def declare(nc, a, g, w):
    sb = w.sb

    def dram(name, shape, dt=F32):
        return nc.dram_tensor(name, shape, dt, kind="Internal").ap()

    def flat(t):
        return t.rearrange("(p j) o -> p (j o)", p=P)
    g.dram = dram
    g.gate = w.sem("gate")
    g.x, g.h = sb("x", [P, NT, FD]), sb("h", [P, NT, FD])
    g.counts = sb("counts", [P, NT, R8])
    g.ident, g.strict, g.count_f = sb("ident", [P, P]), sb("strict", [P, P]), sb("countf", [P, P])
    g.node_f, g.deg, g.has = sb("nodef", [P, NT]), sb("deg", [P, NT]), sb("has", [P, NT])
    g.last_row, g.start_row = sb("lastrow", [P, NT], I32), sb("startrow", [P, NT], I32)
    g.first_row, g.dst_first, g.lane_i = (sb(n, [P, 1], I32) for n in ("firstrow", "dstfirst", "lanei"))
    g.mend_from, g.mend_to = sb("mendfrom", [P, 1], I32), sb("mendto", [P, 1], I32)
    g.first_f, g.lane_f, g.joined = sb("firstf", [P, 1]), sb("lanef", [P, 1]), sb("joined", [1, P])
    g.keep_t, g.dst_t, g.src_t, g.lane_t, g.tile_t, g.type8_t, g.norm_t = (
        dram(n, [EROWS, 1]) for n in ("keep_d", "dst_d", "srcf_d", "lane_d", "tile_d", "type8_d", "norm_d"))
    g.keep_d, g.dst_d, g.src_fd, g.lane_d, g.tile_d, g.type8_d = (
        flat(t) for t in (g.keep_t, g.dst_t, g.src_t, g.lane_t, g.tile_t, g.type8_t))
    g.idx8_d, g.idx90_d = dram("idx8_d", [P, EP], I32), dram("idx90_d", [P, EP], I32)
    g.src_id = a.src
    g.total_d = dram("total_d", [NP + 1, 1])
    g.carry_d = dram("carry_d", [P, 102])
    g.counts_d = dram("counts_t", [NP, R8])
    g.expand = {n: dram(f"expand{n}", [XROWS, k]) for n, k in
                (("att1", 3), ("att2", 1), ("rel", R8), ("sheaf", FD + 1), ("typed", 1))}
    g.by_src = [[dram(f"bysrc{k}{r}", [NP + P, FD]) for r in range(NSUM)] for k in range(2)]
    g.sums = {n: dram(f"sums{n}", [EROWS + P, k]) for n, k in
              (("att1", 102), ("att2", 34 + R8), ("rel", FD), ("sheaf", FD), ("typed", FD))}
    g.to_zero = [t[EROWS:EROWS + P] for t in g.sums.values()] + [g.expand["att1"]]


def build(nc, a, out):
    g = Arrays()
    with Stage(nc, "whole") as w:
        declare(nc, a, g, w)
        set_up(nc, a, g)
        node_ranges(nc, g)
        attention_layers(nc, a, g)
        relation_layers(nc, a, g)
        sheaf_layer(nc, a, g)
        typed_layer(nc, a, g, out)



_WEIGHTS = [f"L0_gnn_{n}" for n in ("W1", "a_src1", "a_dst1", "b1", "W2", "a_src2", "a_dst2", "b2", "Wf", "bf")] + \
           [f"L1_gnn_{n}" for n in ("W1", "root1", "b1", "W2", "root2", "b2")] + \
           [f"L2_gnn_{n}" for n in ("W1", "b1", "W2", "b2")] + \
           [f"L3_gnn_{n}" for n in ("Ws", "Wa", "weight", "w_comp")]


def kernel(**inputs):
    import types

    import concourse.bacc as bacc
    from concourse.bass_utils import run_bass_kernel_spmd

    extra = P * EP - E

    def by_partition(v, fill):
        return np.pad(v, (0, extra), constant_values=fill).reshape(P, EP)

    given = {n: np.asarray(inputs[n]) for n in ("x", "src", "dst", "edge_attr_16", "edge_type_8", "edge_type_90",
                                                *_WEIGHTS)}
    arrays = {
        "x": np.pad(given["x"], ((0, NP - N), (0, 0))),
        "src": by_partition(given["src"], N),
        "dst": by_partition(given["dst"], N),
        "type8": by_partition(given["edge_type_8"], 0),
        "type90": by_partition(given["edge_type_90"], 0),
        "attr": np.pad(given["edge_attr_16"], ((0, extra), (0, 0))).reshape(P, EP, FD),
        **{n: given[n] for n in _WEIGHTS},
    }
    nc = bacc.Bacc("TRN2", target_bir_lowering=False, num_devices=1)
    a = types.SimpleNamespace(**{
        n: nc.dram_tensor(f"in_{n}", list(v.shape), mybir.dt.from_np(v.dtype), kind="ExternalInput").ap()
        for n, v in arrays.items()})
    out = nc.dram_tensor("out", [NP, FD], F32, kind="ExternalOutput").ap()
    build(nc, a, out)
    r = run_bass_kernel_spmd(nc, [{f"in_{n}": np.ascontiguousarray(v) for n, v in arrays.items()}], core_ids=[0])
    return r.results[0]["out"][:N]
```
